# Optimizing a Trainium2 kernel written in Bass

```python
import numpy as np
import jax
import jax.numpy as jnp

def _softmax(x, axis=-1):
    return jax.nn.softmax(x, axis=axis)

def _gelu(x):
    return jax.nn.gelu(x, approximate=True)

def _silu(x):
    return jax.nn.silu(x)

def _sigmoid(x):
    return jax.nn.sigmoid(x)

def _layernorm(x, axis=-1, eps=1e-05):
    m = jnp.mean(x, axis=axis, keepdims=True)
    v = jnp.var(x, axis=axis, keepdims=True)
    return (x - m) / jnp.sqrt(v + eps)

def _scatter_add(tgt, idx, src, axis=0):
    return tgt.at[idx].add(src)

def _segment_sum(src, seg, n):
    return jax.ops.segment_sum(src, seg, n)
kernel_name = 'mk_xattn_ffn_d4_seqx_r4_b9145e'

def setup_inputs(seed: int=0):
    np.random.seed(seed)
    _w = jnp.asarray

    def _rec_inputs():
        import jax
        import jax.numpy as jnp
        _rk = jax.random.key(seed)
        x = 7.22e-05 + 1 * jax.random.normal(jax.random.fold_in(_rk, 1), (2, 1024, 256), jnp.float32)
        _lenS = 1024 - jax.random.randint(jax.random.fold_in(_rk, 7), (2,), 0, max(1, 1024 // 4) + 1, jnp.int32)
        _lenS2 = 154 - jax.random.randint(jax.random.fold_in(_rk, 8), (2,), 0, max(1, 154 // 4) + 1, jnp.int32)
        _ctx_1024P = jax.random.normal(jax.random.fold_in(_rk, 11), (2, 16, 256), jnp.float32)
        _ctx_1024c = jax.random.dirichlet(jax.random.fold_in(_rk, 511), 0.3 * jnp.ones((16,), jnp.float32), (2, 154))
        _ctx_1024t = jnp.einsum('bsk,bkd->bsd', _ctx_1024c, _ctx_1024P)
        _ctx_1024t = _ctx_1024t * jax.lax.rsqrt(jnp.mean(jnp.square(_ctx_1024t)) + 1e-12) * 0.953939
        ctx_1024 = 4.13588e-05 + 0.999923 * (_ctx_1024t + 0.3 * jax.random.normal(jax.random.fold_in(_rk, 611), (2, 154, 256), jnp.float32))
        return (x, ctx_1024)
    x, ctx_1024 = _rec_inputs()

    def _L0_xattn_setup():
        import jax, jax.numpy as jnp
        import numpy as np
        D = 256
        H = 16
        DH = D // H
        key = jax.random.key(seed)
        ks = jax.random.split(key, 11)
        B, T = (4, 512)
        s = 0.02
        return {'q': jax.random.normal(ks[0], (B, T, D), jnp.float32), 'k': jax.random.normal(ks[1], (B, T, D), jnp.float32), 'v': jax.random.normal(ks[2], (B, T, D), jnp.float32), 'Wq': jax.random.normal(ks[3], (D, D), jnp.float32) * s, 'b_q': jax.random.normal(ks[4], (D,), jnp.float32) * s, 'Wk': jax.random.normal(ks[5], (D, D), jnp.float32) * s, 'b_k': jax.random.normal(ks[6], (D,), jnp.float32) * s, 'Wv': jax.random.normal(ks[7], (D, D), jnp.float32) * s, 'b_v': jax.random.normal(ks[8], (D,), jnp.float32) * s, 'Wo': jax.random.normal(ks[9], (D, D), jnp.float32) * s, 'b_o': jax.random.normal(ks[10], (D,), jnp.float32) * s}
    _L0_xattn_all = _L0_xattn_setup()
    _L0_xattn_in = {k: v for k, v in _L0_xattn_all.items() if k in ('Wq', 'b_q', 'Wk', 'b_k', 'Wv', 'b_v', 'Wo', 'b_o')}
    del _L0_xattn_all

    def _L0_ffn_setup():
        import jax, jax.numpy as jnp
        import numpy as np

        def _bitlinear(x, w_latent):
            scale = jax.lax.stop_gradient(jnp.clip(jnp.mean(jnp.abs(w_latent), axis=1, keepdims=True), 1e-05, None))
            tern = jnp.clip(jnp.round(w_latent / scale), -1.0, 1.0)
            w = w_latent + jax.lax.stop_gradient(tern - w_latent)
            return x @ (w * scale).T
        key = jax.random.key(seed)
        ks = jax.random.split(key, 6)
        dim, hidden, rank = (256, 1024, 16)
        B, S = (4, 1024)
        x = jax.random.normal(ks[0], (B, S, dim), dtype=jnp.float32)
        w_fc = 0.02 * jax.random.normal(ks[1], (hidden, dim), dtype=jnp.float32)
        w_proj = 0.02 * jax.random.normal(ks[2], (dim, hidden), dtype=jnp.float32)
        u = 0.02 * jax.random.normal(ks[3], (hidden, rank), dtype=jnp.float32)
        v = 0.02 * jax.random.normal(ks[4], (rank, dim), dtype=jnp.float32)
        fast_b = jax.random.normal(ks[5], (rank, rank), dtype=jnp.float32)
        gate = jnp.float32(0.05)
        return {'x': x, 'fast_b': fast_b, 'w_fc': w_fc, 'w_proj': w_proj, 'u': u, 'v': v, 'gate': gate}
    _L0_ffn_all = _L0_ffn_setup()
    _L0_ffn_in = {k: v for k, v in _L0_ffn_all.items() if k in ('fast_b', 'w_fc', 'w_proj', 'u', 'v', 'gate')}
    del _L0_ffn_all

    def _L1_xattn_setup():
        import jax, jax.numpy as jnp
        import numpy as np
        D_MODEL = 256
        NUM_HEADS = 16
        DEPTH = D_MODEL // NUM_HEADS
        B, LQ, LKV = (4, 256, 512)

        def _xavier(key, shape):
            fan_in, fan_out = (shape[1], shape[0])
            limit = float(np.sqrt(6.0 / (fan_in + fan_out)))
            return jax.random.uniform(key, shape, jnp.float32, -limit, limit)

        def _split_heads(x, b):
            return x.reshape(b, -1, NUM_HEADS, DEPTH).transpose(0, 2, 1, 3)
        key = jax.random.key(seed)
        ks = jax.random.split(key, 6)
        return {'query': jax.random.normal(ks[0], (B, LQ, D_MODEL), jnp.float32), 'value': jax.random.normal(ks[1], (B, LKV, D_MODEL), jnp.float32), 'wq_w': _xavier(ks[2], (D_MODEL, D_MODEL)), 'wk_w': _xavier(ks[3], (D_MODEL, D_MODEL)), 'wv_w': _xavier(ks[4], (D_MODEL, D_MODEL)), 'dense_w': _xavier(ks[5], (D_MODEL, D_MODEL)), 'wq_b': jnp.zeros((D_MODEL,), jnp.float32), 'wk_b': jnp.zeros((D_MODEL,), jnp.float32), 'wv_b': jnp.zeros((D_MODEL,), jnp.float32), 'dense_b': jnp.zeros((D_MODEL,), jnp.float32)}
    _L1_xattn_all = _L1_xattn_setup()
    _L1_xattn_in = {k: v for k, v in _L1_xattn_all.items() if k in ('wq_w', 'wk_w', 'wv_w', 'dense_w', 'wq_b', 'wk_b', 'wv_b', 'dense_b')}
    del _L1_xattn_all

    def _L1_ffn_setup():
        import jax, jax.numpy as jnp
        import numpy as np
        NUM_KEYS = 128
        TOP_K = 8
        NUM_HEADS = 4
        key = jax.random.key(seed)
        ks = jax.random.split(key, 8)
        b, t, d = (1, 512, 256)
        inter = 512
        E, h, ret = (4096, NUM_HEADS, 64)
        s = 0.02
        return {'hidden_states': jax.random.normal(ks[0], (b, t, d), jnp.float32), 'w_queries': jax.random.normal(ks[1], (h * ret, d), jnp.float32) * s, 'keys': jax.random.normal(ks[2], (h, NUM_KEYS, 2, ret // 2), jnp.float32) * s, 'down_embed': jax.random.normal(ks[3], (E, d), jnp.float32) * s, 'up_embed': jax.random.normal(ks[4], (E, d), jnp.float32) * s, 'w_gate': jax.random.normal(ks[5], (inter, d), jnp.float32) * s, 'w_up': jax.random.normal(ks[6], (inter, d), jnp.float32) * s, 'w_down': jax.random.normal(ks[7], (d, inter), jnp.float32) * s}
    _L1_ffn_all = _L1_ffn_setup()
    _L1_ffn_in = {k: v for k, v in _L1_ffn_all.items() if k in ('w_queries', 'keys', 'down_embed', 'up_embed', 'w_gate', 'w_up', 'w_down')}
    del _L1_ffn_all

    def _L2_xattn_setup():
        import jax, jax.numpy as jnp
        import numpy as np
        import math
        B, S, D_MODEL, N_HEAD = (4, 512, 256, 16)
        D_K = D_MODEL // N_HEAD
        ROPE_THETA = 10000.0

        def _rope(x):
            b, h, s, d = x.shape
            inv_freq = ROPE_THETA ** (-jnp.arange(0, d, 2, dtype=jnp.float32) / d)
            ang = jnp.arange(s, dtype=jnp.float32)[:, None] * inv_freq[None, :]
            cos, sin = (jnp.cos(ang), jnp.sin(ang))
            x1, x2 = (x[..., 0::2], x[..., 1::2])
            r1 = x1 * cos - x2 * sin
            r2 = x1 * sin + x2 * cos
            return jnp.stack([r1, r2], axis=-1).reshape(b, h, s, d)

        def _split(x):
            b, s, d = x.shape
            return x.reshape(b, s, N_HEAD, d // N_HEAD).transpose(0, 2, 1, 3)
        key = jax.random.key(seed)
        ks = jax.random.split(key, 7)
        sc = 1.0 / math.sqrt(D_MODEL)
        return {'q': jax.random.normal(ks[0], (B, S, D_MODEL), jnp.float32), 'k': jax.random.normal(ks[1], (B, S, D_MODEL), jnp.float32), 'v': jax.random.normal(ks[2], (B, S, D_MODEL), jnp.float32), 'Wq': jax.random.normal(ks[3], (D_MODEL, D_MODEL), jnp.float32) * sc, 'Wk': jax.random.normal(ks[4], (D_MODEL, D_MODEL), jnp.float32) * sc, 'Wv': jax.random.normal(ks[5], (D_MODEL, D_MODEL), jnp.float32) * sc, 'Wo': jax.random.normal(ks[6], (D_MODEL, D_MODEL), jnp.float32) * sc}
    _L2_xattn_all = _L2_xattn_setup()
    _L2_xattn_in = {k: v for k, v in _L2_xattn_all.items() if k in ('Wq', 'Wk', 'Wv', 'Wo')}
    del _L2_xattn_all

    def _L2_ffn_setup():
        import jax, jax.numpy as jnp
        import numpy as np
        H = 256
        I = 128
        E = 8
        TOP_K = 2
        N_SHARED = 2
        SHARED_I = I * N_SHARED
        SCALE = 2.5
        NORM_TOPK = True
        B, S = (2, 256)

        def _swiglu(x, wg, wu, wd):
            g = x @ wg.T
            u = x @ wu.T
            return jax.nn.silu(g) * u @ wd.T
        key = jax.random.key(seed)
        ks = jax.random.split(key, 8)
        std = 0.02
        return {'hidden_states': jax.random.normal(ks[0], (B, S, H), jnp.float32), 'gate_weight': jax.random.normal(ks[1], (E, H), jnp.float32) * std, 'w_gate': jax.random.normal(ks[2], (E, I, H), jnp.float32) * std, 'w_up': jax.random.normal(ks[3], (E, I, H), jnp.float32) * std, 'w_down': jax.random.normal(ks[4], (E, H, I), jnp.float32) * std, 'ws_gate': jax.random.normal(ks[5], (SHARED_I, H), jnp.float32) * std, 'ws_up': jax.random.normal(ks[6], (SHARED_I, H), jnp.float32) * std, 'ws_down': jax.random.normal(ks[7], (H, SHARED_I), jnp.float32) * std}
    _L2_ffn_all = _L2_ffn_setup()
    _L2_ffn_in = {k: v for k, v in _L2_ffn_all.items() if k in ('gate_weight', 'w_gate', 'w_up', 'w_down', 'ws_gate', 'ws_up', 'ws_down')}
    del _L2_ffn_all

    def _L3_xattn_setup():
        import jax, jax.numpy as jnp
        import numpy as np
        import math
        D_MODEL = 256
        NHEAD = 16
        FACTOR = 1
        B, L = (2, 1024)

        def _autocorr_forward(query, key, value, Wq, bq, Wk, bk, Wv, bv, Wo, bo):
            Bq, Lq, d = query.shape
            Lk = key.shape[1]
            H = NHEAD
            Dk = d // H
            Q = (query @ Wq + bq).reshape(Bq, Lq, H, Dk).transpose(0, 2, 1, 3)
            K = (key @ Wk + bk).reshape(Bq, Lk, H, Dk).transpose(0, 2, 1, 3)
            V = (value @ Wv + bv).reshape(Bq, Lk, H, Dk).transpose(0, 2, 1, 3)
            if Lk > Lq:
                K = K[:, :, :Lq, :]
                V = V[:, :, :Lq, :]
            elif Lq > Lk:
                pad = [(0, 0), (0, 0), (0, Lq - Lk), (0, 0)]
                K = jnp.pad(K, pad)
                V = jnp.pad(V, pad)
            Lloc = Lq
            Qf = jnp.fft.rfft(Q, axis=2)
            Kf = jnp.fft.rfft(K, axis=2)
            corr = jnp.fft.irfft(Qf * jnp.conj(Kf), n=Lloc, axis=2)
            corr_mean = corr.mean(axis=-1)
            top_k = min(max(1, int(FACTOR * math.log(Lloc + 1))), Lloc)
            w, idx = jax.lax.top_k(corr_mean, top_k)
            w = jax.nn.softmax(w, axis=-1)
            ar = jnp.arange(Lloc)
            shifted = (ar[None, None, None, :] + idx[..., None]) % Lloc
            rolled = jnp.take_along_axis(V[:, :, None, :, :], shifted[..., None], axis=3)
            out = jnp.einsum('bhk,bhkld->bhld', w, rolled)
            out = out.transpose(0, 2, 1, 3).reshape(Bq, Lq, d)
            return out @ Wo + bo
        key = jax.random.key(seed)
        ks = jax.random.split(key, 12)
        s = 0.02
        inp = {'query': jax.random.normal(ks[0], (B, L, D_MODEL), dtype=jnp.float32), 'key': jax.random.normal(ks[1], (B, L, D_MODEL), dtype=jnp.float32), 'value': jax.random.normal(ks[2], (B, L, D_MODEL), dtype=jnp.float32), 'Wq': jax.random.normal(ks[3], (D_MODEL, D_MODEL), dtype=jnp.float32) * s, 'bq': jnp.zeros((D_MODEL,), dtype=jnp.float32), 'Wk': jax.random.normal(ks[4], (D_MODEL, D_MODEL), dtype=jnp.float32) * s, 'bk': jnp.zeros((D_MODEL,), dtype=jnp.float32), 'Wv': jax.random.normal(ks[5], (D_MODEL, D_MODEL), dtype=jnp.float32) * s, 'bv': jnp.zeros((D_MODEL,), dtype=jnp.float32), 'Wo': jax.random.normal(ks[6], (D_MODEL, D_MODEL), dtype=jnp.float32) * s, 'bo': jnp.zeros((D_MODEL,), dtype=jnp.float32)}
        return inp
    _L3_xattn_all = _L3_xattn_setup()
    _L3_xattn_in = {k: v for k, v in _L3_xattn_all.items() if k in ('Wq', 'bq', 'Wk', 'bk', 'Wv', 'bv', 'Wo', 'bo')}
    del _L3_xattn_all

    def _L3_ffn_setup():
        import jax, jax.numpy as jnp
        import numpy as np
        TOP_K = 2
        key = jax.random.key(seed)
        k1, k2, k3 = jax.random.split(key, 3)
        B, S, H, E = (4, 512, 256, 8)
        hidden_states = jax.random.normal(k1, (B, S, H), dtype=jnp.float32)
        Wg = jax.random.normal(k2, (H, E), dtype=jnp.float32) * H ** (-0.5)
        We = jax.random.normal(k3, (E, H, H), dtype=jnp.float32) * H ** (-0.5)
        be = jnp.zeros((E, H), dtype=jnp.float32)
        return {'hidden_states': hidden_states, 'Wg': Wg, 'We': We, 'be': be}
    _L3_ffn_all = _L3_ffn_setup()
    _L3_ffn_in = {k: v for k, v in _L3_ffn_all.items() if k in ('Wg', 'We', 'be')}
    del _L3_ffn_all
    return {'x': x, 'ctx_1024': ctx_1024, 'L0_xattn_Wq': _L0_xattn_in['Wq'], 'L0_xattn_b_q': _L0_xattn_in['b_q'], 'L0_xattn_Wk': _L0_xattn_in['Wk'], 'L0_xattn_b_k': _L0_xattn_in['b_k'], 'L0_xattn_Wv': _L0_xattn_in['Wv'], 'L0_xattn_b_v': _L0_xattn_in['b_v'], 'L0_xattn_Wo': _L0_xattn_in['Wo'], 'L0_xattn_b_o': _L0_xattn_in['b_o'], 'L0_ffn_fast_b': _L0_ffn_in['fast_b'], 'L0_ffn_w_fc': _L0_ffn_in['w_fc'], 'L0_ffn_w_proj': _L0_ffn_in['w_proj'], 'L0_ffn_u': _L0_ffn_in['u'], 'L0_ffn_v': _L0_ffn_in['v'], 'L0_ffn_gate': _L0_ffn_in['gate'], 'L1_xattn_wq_w': _L1_xattn_in['wq_w'], 'L1_xattn_wk_w': _L1_xattn_in['wk_w'], 'L1_xattn_wv_w': _L1_xattn_in['wv_w'], 'L1_xattn_dense_w': _L1_xattn_in['dense_w'], 'L1_xattn_wq_b': _L1_xattn_in['wq_b'], 'L1_xattn_wk_b': _L1_xattn_in['wk_b'], 'L1_xattn_wv_b': _L1_xattn_in['wv_b'], 'L1_xattn_dense_b': _L1_xattn_in['dense_b'], 'L1_ffn_w_queries': _L1_ffn_in['w_queries'], 'L1_ffn_keys': _L1_ffn_in['keys'], 'L1_ffn_down_embed': _L1_ffn_in['down_embed'], 'L1_ffn_up_embed': _L1_ffn_in['up_embed'], 'L1_ffn_w_gate': _L1_ffn_in['w_gate'], 'L1_ffn_w_up': _L1_ffn_in['w_up'], 'L1_ffn_w_down': _L1_ffn_in['w_down'], 'L2_xattn_Wq': _L2_xattn_in['Wq'], 'L2_xattn_Wk': _L2_xattn_in['Wk'], 'L2_xattn_Wv': _L2_xattn_in['Wv'], 'L2_xattn_Wo': _L2_xattn_in['Wo'], 'L2_ffn_gate_weight': _L2_ffn_in['gate_weight'], 'L2_ffn_w_gate': _L2_ffn_in['w_gate'], 'L2_ffn_w_up': _L2_ffn_in['w_up'], 'L2_ffn_w_down': _L2_ffn_in['w_down'], 'L2_ffn_ws_gate': _L2_ffn_in['ws_gate'], 'L2_ffn_ws_up': _L2_ffn_in['ws_up'], 'L2_ffn_ws_down': _L2_ffn_in['ws_down'], 'L3_xattn_Wq': _L3_xattn_in['Wq'], 'L3_xattn_bq': _L3_xattn_in['bq'], 'L3_xattn_Wk': _L3_xattn_in['Wk'], 'L3_xattn_bk': _L3_xattn_in['bk'], 'L3_xattn_Wv': _L3_xattn_in['Wv'], 'L3_xattn_bv': _L3_xattn_in['bv'], 'L3_xattn_Wo': _L3_xattn_in['Wo'], 'L3_xattn_bo': _L3_xattn_in['bo'], 'L3_ffn_Wg': _L3_ffn_in['Wg'], 'L3_ffn_We': _L3_ffn_in['We'], 'L3_ffn_be': _L3_ffn_in['be']}

def reference(x, ctx_1024, L0_xattn_Wq, L0_xattn_b_q, L0_xattn_Wk, L0_xattn_b_k, L0_xattn_Wv, L0_xattn_b_v, L0_xattn_Wo, L0_xattn_b_o, L0_ffn_fast_b, L0_ffn_w_fc, L0_ffn_w_proj, L0_ffn_u, L0_ffn_v, L0_ffn_gate, L1_xattn_wq_w, L1_xattn_wk_w, L1_xattn_wv_w, L1_xattn_dense_w, L1_xattn_wq_b, L1_xattn_wk_b, L1_xattn_wv_b, L1_xattn_dense_b, L1_ffn_w_queries, L1_ffn_keys, L1_ffn_down_embed, L1_ffn_up_embed, L1_ffn_w_gate, L1_ffn_w_up, L1_ffn_w_down, L2_xattn_Wq, L2_xattn_Wk, L2_xattn_Wv, L2_xattn_Wo, L2_ffn_gate_weight, L2_ffn_w_gate, L2_ffn_w_up, L2_ffn_w_down, L2_ffn_ws_gate, L2_ffn_ws_up, L2_ffn_ws_down, L3_xattn_Wq, L3_xattn_bq, L3_xattn_Wk, L3_xattn_bk, L3_xattn_Wv, L3_xattn_bv, L3_xattn_Wo, L3_xattn_bo, L3_ffn_Wg, L3_ffn_We, L3_ffn_be):
    import jax
    import jax.numpy as jnp

    def _L0_xattn_ref(q, k, v, Wq, b_q, Wk, b_k, Wv, b_v, Wo, b_o):
        import jax, jax.numpy as jnp
        import numpy as np
        D = 256
        H = 16
        DH = D // H
        B, Tq, _ = q.shape
        Tk = k.shape[1]
        Q = (q @ Wq + b_q).reshape(B, Tq, H, DH)
        K = (k @ Wk + b_k).reshape(B, Tk, H, DH)
        V = (v @ Wv + b_v).reshape(B, Tk, H, DH)
        scores = jnp.einsum('bthd,bshd->bhts', Q, K) / jnp.sqrt(jnp.float32(DH))
        P = jax.nn.softmax(scores, axis=-1)
        out = jnp.einsum('bhts,bshd->bthd', P, V).reshape(B, Tq, D)
        return out @ Wo + b_o

    def _L0_ffn_ref(x, fast_b, w_fc, w_proj, u, v, gate):
        import jax, jax.numpy as jnp
        import numpy as np

        def _bitlinear(x, w_latent):
            scale = jax.lax.stop_gradient(jnp.clip(jnp.mean(jnp.abs(w_latent), axis=1, keepdims=True), 1e-05, None))
            tern = jnp.clip(jnp.round(w_latent / scale), -1.0, 1.0)
            w = w_latent + jax.lax.stop_gradient(tern - w_latent)
            return x @ (w * scale).T
        h = _bitlinear(x, w_fc) + gate * (x @ v.T @ fast_b.T @ u.T)
        r = jnp.maximum(h, 0.0)
        return _bitlinear(r * r, w_proj)

    def _L1_xattn_ref(query, value, wq_w, wk_w, wv_w, dense_w, wq_b, wk_b, wv_b, dense_b):
        import jax, jax.numpy as jnp
        import numpy as np
        D_MODEL = 256
        NUM_HEADS = 16
        DEPTH = D_MODEL // NUM_HEADS
        B, LQ, LKV = (4, 256, 512)

        def _xavier(key, shape):
            fan_in, fan_out = (shape[1], shape[0])
            limit = float(np.sqrt(6.0 / (fan_in + fan_out)))
            return jax.random.uniform(key, shape, jnp.float32, -limit, limit)

        def _split_heads(x, b):
            return x.reshape(b, -1, NUM_HEADS, DEPTH).transpose(0, 2, 1, 3)
        b = query.shape[0]
        q = query @ wq_w.T + wq_b
        k = value @ wk_w.T + wk_b
        v = value @ wv_w.T + wv_b
        q = _split_heads(q, b)
        k = _split_heads(k, b)
        v = _split_heads(v, b)
        scale = jnp.sqrt(jnp.asarray(DEPTH, q.dtype))
        scores = jnp.einsum('bhqd,bhkd->bhqk', q, k) / scale
        attn = jax.nn.softmax(scores, axis=-1)
        ctx = jnp.einsum('bhqk,bhkd->bhqd', attn, v)
        ctx = ctx.transpose(0, 2, 1, 3).reshape(b, -1, D_MODEL)
        return ctx @ dense_w.T + dense_b

    def _L1_ffn_ref(hidden_states, w_queries, keys, down_embed, up_embed, w_gate, w_up, w_down):
        import jax, jax.numpy as jnp
        import numpy as np
        NUM_KEYS = 128
        TOP_K = 8
        NUM_HEADS = 4
        b, t, d = hidden_states.shape
        h, nk, _, n = keys.shape
        k = TOP_K
        q = (hidden_states @ w_queries.T).reshape(b, t, 2, h, n)
        sim = jnp.einsum('btphn,hkpn->pbthk', q, keys)
        sx, ix = jax.lax.top_k(sim[0], k)
        sy, iy = jax.lax.top_k(sim[1], k)
        all_scores = (sx[..., :, None] + sy[..., None, :]).reshape(b, t, h, k * k)
        all_idx = (ix[..., :, None] * nk + iy[..., None, :]).reshape(b, t, h, k * k)
        scores, pos = jax.lax.top_k(all_scores, k)
        indices = jnp.take_along_axis(all_idx, pos, axis=-1)
        de = down_embed[indices]
        ue = up_embed[indices]
        ew = jnp.einsum('btd,bthkd->bthk', hidden_states, de)
        ew = jax.nn.silu(ew) * jax.nn.softmax(scores, axis=-1)
        experts_states = jnp.einsum('bthk,bthkd->btd', ew, ue)
        mlp = jax.nn.silu(hidden_states @ w_gate.T) * (hidden_states @ w_up.T) @ w_down.T
        return mlp + experts_states

    def _L2_xattn_ref(q, k, v, Wq, Wk, Wv, Wo):
        import jax, jax.numpy as jnp
        import numpy as np
        import math
        B, S, D_MODEL, N_HEAD = (4, 512, 256, 16)
        D_K = D_MODEL // N_HEAD
        ROPE_THETA = 10000.0

        def _rope(x):
            b, h, s, d = x.shape
            inv_freq = ROPE_THETA ** (-jnp.arange(0, d, 2, dtype=jnp.float32) / d)
            ang = jnp.arange(s, dtype=jnp.float32)[:, None] * inv_freq[None, :]
            cos, sin = (jnp.cos(ang), jnp.sin(ang))
            x1, x2 = (x[..., 0::2], x[..., 1::2])
            r1 = x1 * cos - x2 * sin
            r2 = x1 * sin + x2 * cos
            return jnp.stack([r1, r2], axis=-1).reshape(b, h, s, d)

        def _split(x):
            b, s, d = x.shape
            return x.reshape(b, s, N_HEAD, d // N_HEAD).transpose(0, 2, 1, 3)
        q = jnp.einsum('bsd,de->bse', q, Wq)
        k = jnp.einsum('bsd,de->bse', k, Wk)
        v = jnp.einsum('bsd,de->bse', v, Wv)
        qh, kh, vh = (_split(q), _split(k), _split(v))
        qh, kh = (_rope(qh), _rope(kh))
        scale = 1.0 / math.sqrt(D_K)
        score = jnp.einsum('bhqd,bhkd->bhqk', qh, kh) * scale
        attn = jax.nn.softmax(score, axis=-1)
        out = jnp.einsum('bhqk,bhkd->bhqd', attn, vh)
        out = out.transpose(0, 2, 1, 3).reshape(q.shape[0], q.shape[1], D_MODEL)
        return jnp.einsum('bsd,de->bse', out, Wo)

    def _L2_ffn_ref(hidden_states, gate_weight, w_gate, w_up, w_down, ws_gate, ws_up, ws_down):
        import jax, jax.numpy as jnp
        import numpy as np
        H = 256
        I = 128
        E = 8
        TOP_K = 2
        N_SHARED = 2
        SHARED_I = I * N_SHARED
        SCALE = 2.5
        NORM_TOPK = True
        B, S = (2, 256)

        def _swiglu(x, wg, wu, wd):
            g = x @ wg.T
            u = x @ wu.T
            return jax.nn.silu(g) * u @ wd.T
        b, s, h = hidden_states.shape
        x = hidden_states.reshape(-1, h)
        shared_out = _swiglu(x, ws_gate, ws_up, ws_down)
        logits = x.astype(jnp.float32) @ gate_weight.astype(jnp.float32).T
        scores = jax.nn.sigmoid(logits)
        topk_w, topk_idx = jax.lax.top_k(scores, TOP_K)
        if TOP_K > 1 and NORM_TOPK:
            topk_w = topk_w / (topk_w.sum(-1, keepdims=True) + 1e-20)
        topk_w = topk_w * SCALE
        onehot = jax.nn.one_hot(topk_idx, E, dtype=topk_w.dtype)
        combine = jnp.einsum('tk,tke->te', topk_w, onehot)
        g = jnp.einsum('th,eih->tei', x, w_gate)
        u = jnp.einsum('th,eih->tei', x, w_up)
        hmid = jax.nn.silu(g) * u
        y = jnp.einsum('tei,ehi->teh', hmid, w_down)
        routed_out = jnp.einsum('te,teh->th', combine, y)
        out = (routed_out + shared_out).reshape(b, s, h)
        return out

    def _L3_xattn_ref(query, key, value, Wq, bq, Wk, bk, Wv, bv, Wo, bo):
        import jax, jax.numpy as jnp
        import numpy as np
        import math
        D_MODEL = 256
        NHEAD = 16
        FACTOR = 1
        B, L = (2, 1024)

        def _autocorr_forward(query, key, value, Wq, bq, Wk, bk, Wv, bv, Wo, bo):
            Bq, Lq, d = query.shape
            Lk = key.shape[1]
            H = NHEAD
            Dk = d // H
            Q = (query @ Wq + bq).reshape(Bq, Lq, H, Dk).transpose(0, 2, 1, 3)
            K = (key @ Wk + bk).reshape(Bq, Lk, H, Dk).transpose(0, 2, 1, 3)
            V = (value @ Wv + bv).reshape(Bq, Lk, H, Dk).transpose(0, 2, 1, 3)
            if Lk > Lq:
                K = K[:, :, :Lq, :]
                V = V[:, :, :Lq, :]
            elif Lq > Lk:
                pad = [(0, 0), (0, 0), (0, Lq - Lk), (0, 0)]
                K = jnp.pad(K, pad)
                V = jnp.pad(V, pad)
            Lloc = Lq
            Qf = jnp.fft.rfft(Q, axis=2)
            Kf = jnp.fft.rfft(K, axis=2)
            corr = jnp.fft.irfft(Qf * jnp.conj(Kf), n=Lloc, axis=2)
            corr_mean = corr.mean(axis=-1)
            top_k = min(max(1, int(FACTOR * math.log(Lloc + 1))), Lloc)
            w, idx = jax.lax.top_k(corr_mean, top_k)
            w = jax.nn.softmax(w, axis=-1)
            ar = jnp.arange(Lloc)
            shifted = (ar[None, None, None, :] + idx[..., None]) % Lloc
            rolled = jnp.take_along_axis(V[:, :, None, :, :], shifted[..., None], axis=3)
            out = jnp.einsum('bhk,bhkld->bhld', w, rolled)
            out = out.transpose(0, 2, 1, 3).reshape(Bq, Lq, d)
            return out @ Wo + bo
        return _autocorr_forward(query, key, value, Wq, bq, Wk, bk, Wv, bv, Wo, bo)

    def _L3_ffn_ref(hidden_states, Wg, We, be):
        import jax, jax.numpy as jnp
        import numpy as np
        TOP_K = 2
        B, S, H = hidden_states.shape
        T = B * S
        x = hidden_states.reshape(T, H)
        probs = jax.nn.softmax(x @ Wg, axis=-1)
        top_vals, top_idx = jax.lax.top_k(probs, TOP_K)
        gates = top_vals / jnp.sum(top_vals, axis=-1, keepdims=True)
        expert_out = jnp.einsum('th,ehd->etd', x, We) + be[:, None, :]
        tok = jnp.arange(T)[:, None]
        sel = expert_out[top_idx, tok, :]
        out = jnp.sum(gates[..., None] * sel, axis=1)
        return out.reshape(B, S, H)
    x = x + _L0_xattn_ref(_layernorm(x, axis=-1), ctx_1024, ctx_1024, L0_xattn_Wq, L0_xattn_b_q, L0_xattn_Wk, L0_xattn_b_k, L0_xattn_Wv, L0_xattn_b_v, L0_xattn_Wo, L0_xattn_b_o)
    x = x + _L0_ffn_ref(_layernorm(x, axis=-1), L0_ffn_fast_b, L0_ffn_w_fc, L0_ffn_w_proj, L0_ffn_u, L0_ffn_v, L0_ffn_gate)
    x = x + _L1_xattn_ref(_layernorm(x, axis=-1), ctx_1024, L1_xattn_wq_w, L1_xattn_wk_w, L1_xattn_wv_w, L1_xattn_dense_w, L1_xattn_wq_b, L1_xattn_wk_b, L1_xattn_wv_b, L1_xattn_dense_b)
    x = x + _L1_ffn_ref(_layernorm(x, axis=-1), L1_ffn_w_queries, L1_ffn_keys, L1_ffn_down_embed, L1_ffn_up_embed, L1_ffn_w_gate, L1_ffn_w_up, L1_ffn_w_down)
    x = x + _L2_xattn_ref(_layernorm(x, axis=-1), ctx_1024, ctx_1024, L2_xattn_Wq, L2_xattn_Wk, L2_xattn_Wv, L2_xattn_Wo)
    x = x + _L2_ffn_ref(_layernorm(x, axis=-1), L2_ffn_gate_weight, L2_ffn_w_gate, L2_ffn_w_up, L2_ffn_w_down, L2_ffn_ws_gate, L2_ffn_ws_up, L2_ffn_ws_down)
    x = x + _L3_xattn_ref(_layernorm(x, axis=-1), ctx_1024, ctx_1024, L3_xattn_Wq, L3_xattn_bq, L3_xattn_Wk, L3_xattn_bk, L3_xattn_Wv, L3_xattn_bv, L3_xattn_Wo, L3_xattn_bo)
    x = x + _L3_ffn_ref(_layernorm(x, axis=-1), L3_ffn_Wg, L3_ffn_We, L3_ffn_be)
    return x

_drawn_inputs = setup_inputs


def setup_inputs(seed=0):
    import zlib

    import numpy as np

    out = dict(_drawn_inputs(seed))
    spreads = {'L1_xattn_wq_b': (0.0, 0.1),
     'L1_xattn_wk_b': (0.0, 0.8),
     'L1_xattn_wv_b': (0.0, 0.1),
     'L1_xattn_dense_b': (0.0, 0.1),
     'L3_xattn_bq': (0.0, 0.8),
     'L3_xattn_bk': (0.0, 0.1),
     'L3_xattn_bv': (0.0, 0.319),
     'L3_xattn_bo': (0.0, 0.1),
     'L3_ffn_be': (0.0, 0.1)}
    factors = {'L0_xattn_Wq': 3.78,
     'L0_xattn_b_q': 8.0,
     'L0_xattn_Wk': 3.043,
     'L0_xattn_b_k': 8.0,
     'L0_xattn_b_v': 2.93,
     'L0_ffn_fast_b': 5.459,
     'L0_ffn_u': 5.796,
     'L0_ffn_v': 5.218,
     'L1_ffn_w_queries': 3.357,
     'L1_ffn_keys': 3.606}
    for name, (base, spread) in spreads.items():
        noise = np.random.default_rng([zlib.crc32(name.encode()), seed]).standard_normal(out[name].shape)
        drawn = base * np.exp(spread * noise) if base else spread * noise
        out[name] = jnp.asarray(drawn.astype(out[name].dtype))
    for name, factor in factors.items():
        out[name] = (out[name] * factor).astype(out[name].dtype)
    return out
```

```python
from contextlib import ExitStack

import concourse.bass as bass
import numpy as np
from concourse import mybir

FP, BF, U32 = mybir.dt.float32, mybir.dt.bfloat16, mybir.dt.uint32
ALU, ACT, AX = mybir.AluOpType, mybir.ActivationFunctionType, mybir.AxisListType

P = 128
STOP = None
B, T, D = 2, 1024, 256
S = 154
H, DH = 16, 16
KT = D // P
NCH, CH = 4, 512
TI = CH // P
SR = S - P
SP_ = 160
G4 = 4
EPS = 1e-5
HID0, RANK = 1024, 16
NKEY, TOPK, PH, NEXP1, INTER = 128, 8, 4, 4096, 512
E2, M2 = 8, 10
E3 = 8
U = SP_ // 16
EXT = T + SP_
TOPC = 6
RING, GRP = 20, 4
NG = PH * TOPK // GRP

ATTN_PACK = dict(wq=KT * D, wk=KT * D, wv=KT * D, wo=G4 * D, bq=2, bk=2, bv=D, bo=D, wqs=KT * D, wks=KT * D)
CORR_PACK = dict(wq=KT * D, wk=KT * D, wv=KT * D, wo=KT * D, bq=2, bk=2, bv=D, bo=D)
FFN0_PACK = dict(fc=8 * D, proj=2 * HID0, ut=HID0, v=D, fbt=RANK, gate=1)
FFN1_PACK = dict(wq=KT * D, keys=2 * 512, wg=KT * INTER, wu=KT * INTER, wd=4 * D)
FFN2_PACK = dict(gate=KT * E2, gu=KT * M2 * 2 * P, down=M2 * D)
FFN3_PACK = dict(gate=KT * E3, we=KT * E3 * D, be=D)
CONST_PACK = dict(ident=P, mask8=8, padrow=1, iota8=8, selh=4 * 32, valid=SP_, iota=T)
SELECT_PACK = dict(selneg=H * P, selrest=G4 * P)
ROPE_PACK = dict(cos=T, sin=T)


def columns(pack):
    at, out = 0, {}
    for name, n in pack.items():
        out[name] = slice(at, at + n)
        at += n
    return out, at


def schedule():
    out = []
    for layer in range(3):
        out.append(("kv", layer, 0))
        out += [("attn", layer, c) for c in range(NCH)]
        if layer == 0:
            out.append(("tern", 0, 0))
        out += [(f"ffn{layer}", layer, c) for c in range(NCH)]
    out.append(("kv3", 3, 0))
    for b in range(B):
        out += [("q3", b, 2 * b), ("q3", b, 2 * b + 1), ("corr", b, 0)]
    out.append(("top", 0, 0))
    out += [("out3", b, 0) for b in range(B)]
    out += [("ffn3", 3, c) for c in range(NCH)]
    return out


def build(nc, io, stop=None):
    phases = schedule()[:stop]
    fronts = [n for n, (kind, _, _) in enumerate(phases) if kind in ("attn", "ffn0", "ffn1", "ffn2", "q3", "ffn3")]
    front_of = {n: f for f, n in enumerate(fronts)}

    def instance(n):
        return sum(p[0] == phases[n][0] for p in phases[:n])

    def next_front(n):
        f = sum(m <= n for m in fronts)
        if f >= len(fronts):
            return None
        m = fronts[f]
        kind, b, _ = phases[n]
        if phases[m][0] == "ffn3" and phases[m - 1][0] == "out3":
            return f if kind == "out3" and b == 1 else None
        return f if n == (fronts[f - 1] if f else 0) else None

    ctx = ExitStack()
    with ctx:
        def sb(name, shape, dt=FP):
            return ctx.enter_context(nc.sbuf_tensor(name, shape, dt))

        def sem(name):
            return ctx.enter_context(nc.semaphore(name))

        x_sb = sb("x_sb", [P, NCH * TI, D])
        xn = [sb(f"xn{i}", [P, TI, D]) for i in range(2)]
        xt = [sb(f"xt{i}", [P, KT, CH]) for i in range(2)]
        stats = sb("stats", [P, TI, 6])
        mv = sb("mv", [P, TI, 2])
        vare = sb("vare", [P, TI])
        rstd = sb("rstd", [P, TI])
        half = sb("half", [P, TI])
        AC, AN = columns(ATTN_PACK)
        CC, CN = columns(CORR_PACK)
        F0, F0N = columns(FFN0_PACK)
        F1, F1N = columns(FFN1_PACK)
        F2, F2N = columns(FFN2_PACK)
        F3, F3N = columns(FFN3_PACK)
        KC, KN = columns(CONST_PACK)
        RC, RN = columns(ROPE_PACK)
        const = sb("const", [P, KN])
        ctxt = sb("ctxt", [P, KT, B * S])
        wattn = sb("wattn", [P, max(AN, CN)])
        wa = sb("wa", [P, max(4096, F2N)])
        wb = sb("wb", [P, max(F0N, F1N, F3N)])
        bufA = sb("bufA", [P, 11008])
        bufB = sb("bufB", [P, 10240])
        selneg = sb("selneg", [P, H, P], BF)
        selrest = sb("selrest", [P, G4, P], BF)
        mt = sb("mt", [P, CH], BF)
        m4 = sb("m4", [P, TI, H])
        bqs = sb("bqs", [P, 2])
        psum = ctx.enter_context(nc.psum_tensor("psum", [P, 8, 512], FP))
        scr1 = nc.dram_tensor("scr_corr", (4, P, T + 16), FP).ap()
        scr2 = nc.dram_tensor("scr_roll", (32, 2 * T), FP).ap()
        scrv = nc.dram_tensor("scr_v", (B, SP_, D), FP).ap()

        def bank(i):
            return psum[:, i, :]

        ident = const[:, KC["ident"]]
        mask8 = const[:, KC["mask8"]]
        padrow = const[:, KC["padrow"]]
        iota8 = const[:, KC["iota8"]]
        SC, SN = columns(SELECT_PACK)
        selraw = bufA[:, 2048:2048 + SN]
        selh = const[:, KC["selh"]].rearrange("p (a m) -> p a m", a=4)
        valid = const[0:1, KC["valid"]]
        iota = const[:, KC["iota"]]

        def w(name, kt=KT, where=wattn, cols=AC):
            return where[:, cols[name]].rearrange("p (k n) -> p k n", k=kt)

        def keys(b, g):
            at = (b * 2 + g) * 8 * SP_
            return bufB[:, at:at + 8 * SP_].rearrange("p (h k) -> p h k", h=8)

        KB_AT = 4 * 8 * SP_
        keysb_all = bufB[:, KB_AT:KB_AT + 4 * 4 * S].bitcast(BF)

        def keysb(b, g):
            at = (b * 2 + g) * 8 * S
            return keysb_all[:, at:at + 8 * S]

        VA_AT = KB_AT + 4 * 4 * S

        def vmain(b):
            return bufB[:, VA_AT + b * 512:VA_AT + (b + 1) * 512]

        def vrest(b):
            at = VA_AT + 1024 + b * 512
            return bufB[:, at:at + 512].rearrange("p (g n) -> p g n", g=G4)

        ld_const, ld_x, ld_ctx, ld_rope = sem("ld_const"), sem("ld_x"), sem("ld_ctx"), sem("ld_rope")
        ld_attn = sem("ld_attn")
        ld_f0, ld_f1, ld_f2, ld_f3 = sem("ld_f0"), sem("ld_f1"), sem("ld_f2"), sem("ld_f3")
        ends = {e: sem(f"end_{e}") for e in ("pe", "act", "dve", "pool")}
        cst = sem("cst")
        fr_var, fr_rstd, fr_xn, fr_tp, fr_ev = (sem(s) for s in ("fr_var", "fr_rstd", "fr_xn", "fr_tp", "fr_ev"))
        kv_k, kv_kt, kv_v, kv_z, kv_ks = (sem(s) for s in ("kv_k", "kv_kt", "kv_v", "kv_z", "kv_ks"))
        at_q, at_qt, at_qb, at_p1, at_mx, at_mt, at_mts = (
            sem(s) for s in ("at_q", "at_qt", "at_qb", "at_p1", "at_mx", "at_mt", "at_mts"))
        at_s2, at_ex, at_pv, at_on, at_wo, at_bo = (sem(s) for s in ("at_s2", "at_ex", "at_pv", "at_on", "at_wo", "at_bo"))
        tn_w, tn_z, tn_zs, tn_u, tn_nat, tn_tp, tn_ev = (
            sem(s) for s in ("tn_w", "tn_z", "tn_zs", "tn_u", "tn_nat", "tn_tp", "tn_ev"))
        f0_h, f0_r, f0_sq, f0_y, f0_x = (sem(s) for s in ("f0_h", "f0_r", "f0_sq", "f0_y", "f0_x"))
        f1_q, f1_qt, f1_sim, f1_tk, f1_g, f1_sg, f1_hm, f1_y, f1_x = (
            sem(s) for s in ("f1_q", "f1_qt", "f1_sim", "f1_tk", "f1_g", "f1_sg", "f1_hm", "f1_y", "f1_x"))
        f1_sc, f1_se, f1_idx, f1_dot, f1_sd, f1_acc = (
            sem(s) for s in ("f1_sc", "f1_se", "f1_idx", "f1_dot", "f1_sd", "f1_acc"))
        gathered = [sem(f"gathered{i}") for i in range(RING // GRP)]
        f2_lg, f2_sc, f2_g, f2_sg, f2_hm, f2_y, f2_x = (
            sem(s) for s in ("f2_lg", "f2_sc", "f2_g", "f2_sg", "f2_hm", "f2_y", "f2_x"))
        f3_lg, f3_ls, f3_ex, f3_gt, f3_gp, f3_gs, f3_b, f3_y, f3_x = (
            sem(s) for s in ("f3_lg", "f3_ls", "f3_ex", "f3_gt", "f3_gp", "f3_gs", "f3_b", "f3_y", "f3_x"))
        k3_k, k3_kt, k3_v, k3_vs, k3_wr, k3_rd, k3_st = (
            sem(s) for s in ("k3_k", "k3_kt", "k3_v", "k3_vs", "k3_wr", "k3_rd", "k3_st"))
        q3_q, q3_s = sem("q3_q"), sem("q3_s")
        co_c, co_s, co_wr, co_rd, co_m = (sem(s) for s in ("co_c", "co_s", "co_wr", "co_rd", "co_m"))
        tp_c, tp_n, tp_e, tp_r, tp_wr, tp_rd = (sem(s) for s in ("tp_c", "tp_n", "tp_e", "tp_r", "tp_wr", "tp_rd"))
        o3_o, o3_s, o3_y, o3_x, o3_bo = (sem(s) for s in ("o3_o", "o3_s", "o3_y", "o3_x", "o3_bo"))
        own_dve, own_act, own_pool = sem("own_dve"), sem("own_act"), sem("own_pool")
        stored = sem("stored")

        block = ctx.enter_context(nc.Block())

        def enter(eng, me, n):
            if n:
                for e, s in ends.items():
                    if e != me:
                        eng.wait_ge(s, n)

        def leave(eng, me):
            eng.drain().then_inc(ends[me], 1)

        class Own:

            def __init__(self, eng, s):
                self.eng, self.s, self.n = eng, s, 0

            def mark(self, ins):
                self.n += 1
                ins.then_inc(self.s, 1)

            def wait(self):
                self.eng.wait_ge(self.s, self.n)

            def link(self, ins):
                self.mark(ins)
                self.wait()

        def A(at, n):
            return bufA[:, at:at + n]

        qt = A(0, 1024).rearrange("p (g n) -> p g n", g=2)
        qb = A(1024, 512).bitcast(BF).rearrange("p (g n) -> p g n", g=2)
        probs = [A(1536 + 2560 * i, 2560).rearrange("p (h n) -> p h n", h=5) for i in range(2)]
        ot = A(6656, 2048).rearrange("p (g n) -> p g n", g=G4)
        den, rec = A(8704, 512), A(9216, 512)
        ropet = A(1536, 1024).rearrange("p (g n) -> p g n", g=2)
        kts = A(0, 2 * 308).rearrange("p (g n) -> p g n", g=2)
        ktr = A(1024, 2 * 308).rearrange("p (g n) -> p g n", g=2)
        rope = sb("rope", [P, RN])
        fc_t = wa[:, 0:2048].rearrange("p (k n) -> p k n", k=KT)
        proj_t = wa[:, 2048:4096].rearrange("p (m n) -> p m n", m=8)
        raw0 = wb[:, 0:F0N]
        fcnat = raw0[:, F0["fc"]].rearrange("p (m n) -> p m n", m=8)
        projnat = raw0[:, F0["proj"]].rearrange("p (o n) -> p o n", o=2)
        TN = 0
        utg = raw0[:, F0["ut"]]
        lowv = A(TN, D)
        absum, hi_th, lo_th, sclip = A(TN + D, 10), A(TN + D + 10, 10), A(TN + D + 20, 10), A(TN + D + 30, 10)
        tplus, tminus = A(TN + D + 64, 1024), A(TN + D + 64 + 1024, 1024)
        hid0r = A(0, 4096).rearrange("p (m n) -> p m n", m=8)
        hid0 = A(4096, 4096).rearrange("p (m n) -> p m n", m=8)

        def f0(name):
            return raw0[:, F0[name]]

        def w1(name, kt=KT):
            return w(name, kt, wb, F1)

        q1 = A(0, 1024).rearrange("p (g n) -> p g n", g=2)
        sg1 = A(1024, 1024).rearrange("p (g n) -> p g n", g=2)
        hm1 = A(2048, 2048).rearrange("p (m n) -> p m n", m=4)
        topv = A(4096, 256).rearrange("p (a r k) -> p a r k", a=2, k=TOPK)
        topi = A(4352, 256).bitcast(U32).rearrange("p (a r k) -> p a r k", a=2, k=TOPK)
        topf = A(4608, 256).rearrange("p (a r k) -> p a r k", a=2, k=TOPK)
        sums = A(4864, 1024).rearrange("p (r i j) -> p r i j", r=16, i=TOPK)
        best = A(5888, 128).rearrange("p (r k) -> p r k", r=16)
        pos = A(6016, 128).bitcast(U32)
        pside = [A(6144 + 128 * z, 128).bitcast(U32) for z in range(2)]
        psidef = [A(6400 + 128 * z, 128) for z in range(2)]
        eq = [A(6656 + 1024 * z, 1024).rearrange("p (r k j) -> p r k j", r=16, k=TOPK) for z in range(2)]
        pick = [A(8704 + 128 * z, 128) for z in range(2)]
        ex1 = A(8960, 128)
        esum, erec = A(9088, 16), A(9104, 16)
        prob1 = A(9120, 128)
        rowid = A(9248, 128).bitcast(U32)
        dots = A(9376, 16).rearrange("p (s j) -> p s j", s=4)
        sdot = A(9392, 16).rearrange("p (s j) -> p s j", s=4)
        ew = A(9408, 16).rearrange("p (s j) -> p s j", s=4)
        junk = A(9424, 4 * D).rearrange("p (s d) -> p s d", s=4)
        rowf = A(10448, 128)
        ring = bufB[:, :].rearrange("p (s n) -> p s n", s=RING)

        def w2(name, kt=KT):
            return w(name, kt, wa, F2)

        sg2 = A(0, 1024).rearrange("p (g n) -> p g n", g=2)
        hm2 = A(1024, 5120).rearrange("p (m n) -> p m n", m=M2)
        sc2 = A(6144, 32)
        tv2 = A(6176, 32).rearrange("p (i k) -> p i k", i=TI)
        ti2 = A(6208, 32).bitcast(U32).rearrange("p (i k) -> p i k", i=TI)
        tf2 = A(6240, 32).rearrange("p (i k) -> p i k", i=TI)
        s2 = [A(6272 + 8 * z, 4) for z in range(4)]
        comb2 = [A(6304 + 32 * z, 32).rearrange("p (i e) -> p i e", i=TI) for z in range(3)]

        def w3(name, kt=KT):
            return w(name, kt, wb, F3)

        ex3 = A(0, 32)
        lg3 = A(32, 32).rearrange("p (i e) -> p i e", i=TI)
        mx3 = A(64, 4)
        tv3 = A(96, 32).rearrange("p (i k) -> p i k", i=TI)
        ti3 = A(128, 32).bitcast(U32).rearrange("p (i k) -> p i k", i=TI)
        tf3 = A(160, 32).rearrange("p (i k) -> p i k", i=TI)
        pr3 = A(192, 32)
        s3 = [A(224 + 8 * z, 4) for z in range(4)]
        comb3 = [A(256 + 32 * z, 32).rearrange("p (i e) -> p i e", i=TI) for z in range(3)]
        gate3 = A(256, 32)
        gatet = A(512, 512)

        ctxr = sb("ctxr", [P, KT, B * SP_])
        k3t = A(0, 2 * B * SP_).rearrange("p (g n) -> p g n", g=2)
        v3m = A(1024, 512).rearrange("p (b n) -> p b n", b=B)
        v3r = A(1536, 512).rearrange("p (b n) -> p b n", b=B)
        v3s = A(2048, 4 * U * 16).rearrange("p (a u d) -> p a u d", a=4, u=U)
        qx = A(0, 2 * EXT).rearrange("p (g n) -> p g n", g=2)
        c1 = [A(2400 + 1040 * g, 1040) for g in range(2)]
        c2 = [A(4480 + 1024 * g, 1024) for g in range(2)]
        cor = A(6528, T)
        rolls = A(0, 4 * (T + SP_))
        ot3 = A(4736, 2048).rearrange("p (g n) -> p g n", g=2)
        topw, topj, topjf, rsum3 = A(7552, 8), A(7560, 8).bitcast(U32), A(7568, 8), A(7576, 8)
        topm = A(7584, 8)
        rollw = [A(7680 + 1024 * z, T) for z in range(2)]
        rollt = [A(9728, T), A(4736, T)]

        def kst(b, g):
            return bufB[:, (2 * b + g) * U * P:(2 * b + g + 1) * U * P].rearrange("p (u n) -> p u n", u=U)

        def vst(b, g):
            at = 4 * U * P + (2 * b + g) * U * P
            return bufB[:, at:at + U * P].rearrange("p (u n) -> p u n", u=U)

        def roll(a):
            return rolls[:, a * (T + SP_):(a + 1) * (T + SP_)]


        @block.tensor
        def _(eng):
            mm = eng.matmul

            def front(f):
                if f is None:
                    return
                i2 = f % 2
                eng.wait_ge(fr_xn, TI * (f + 1))
                if f:
                    eng.wait_ge(fr_ev, KT * f)
                for kt in range(KT):
                    for i in range(TI):
                        ins = eng.transpose(psum[:, 6 + kt, i * P:(i + 1) * P], xn[i2][:, i, kt * P:(kt + 1) * P], ident)
                    ins.then_inc(fr_tp, 1)

            def kv(n, layer):
                enter(eng, "pe", n)
                eng.wait_ge(ld_const, 32)
                eng.wait_ge(ld_ctx, 32)
                eng.wait_ge(ld_attn, 16 * (layer + 1))
                names = ["wk", "wks"] if layer == 2 else ["wk"]
                for r, name in enumerate(names):
                    for g in range(2):
                        for kt in range(KT):
                            ins = mm(psum[:, 2 * r + g, 0:B * S], w(name)[:, kt, g * P:(g + 1) * P], ctxt[:, kt, :],
                                     start=kt == 0, stop=kt == KT - 1)
                ins.then_inc(kv_k, 1)
                bias = wattn[0:1, AC["bv"]]
                for b in range(B):
                    o = psum[:, 4 + b, 0:D]
                    for kt in range(KT):
                        mm(o, ctxt[:, kt, b * S:b * S + P], w("wv")[:, kt, :], start=kt == 0, stop=False)
                    mm(o, valid[:, 0:P], bias, start=False, stop=True)
                    for j in range(4):
                        o = psum[32 * j:32 * j + SR, 4 + b, D:2 * D]
                        for kt in range(KT):
                            mm(o, ctxt[:, kt, b * S + P:(b + 1) * S], w("wv")[:, kt, :], start=kt == 0, stop=False)
                        ins = mm(o, valid[:, 0:SR], bias, start=False, stop=True)
                ins.then_inc(kv_v, 1)
                if n == 0:
                    front(0)

            def attn(n, layer, c):
                k, b, x = instance(n), c // 2, xt[front_of[n] % 2]
                enter(eng, "pe", n)
                eng.wait_ge(fr_ev, KT * (front_of[n] + 1))
                for r, name in enumerate(["wq", "wqs"] if layer == 2 else ["wq"]):
                    for g in range(2):
                        for kt in range(KT):
                            ins = mm(bank(2 * r + g), w(name)[:, kt, g * P:(g + 1) * P], x[:, kt, :],
                                     start=kt == 0, stop=kt == KT - 1)
                ins.then_inc(at_q, 1)
                eng.wait_ge(at_qb, 2 * k + 2)
                eng.wait_ge(at_qt, 2 * k + 2)
                for u in range(16):
                    i, g, hf, pair = u // 4, (u // 2) % 2, u % 2, 2 * (u % 3)
                    if u >= 3:
                        eng.wait_ge(at_mx, 16 * k + u - 2)
                    for z in range(2):
                        at = (hf * 4 + z * 2) * S
                        ins = mm(psum[:, pair + z, 0:2 * S], qb[:, g, i * P:(i + 1) * P], keysb(b, g)[:, at:at + 2 * S],
                                 start=True, stop=True)
                    ins.then_inc(at_p1, 1)
                front(next_front(n))
                eng.wait_ge(at_mx, 16 * k + 16)
                for i in range(TI):
                    ins = eng.transpose(psum[0:H, 0, i * P:(i + 1) * P], m4[:, i, :], ident)
                ins.then_inc(at_mt, 1)
                eng.wait_ge(at_mts, k + 1)

                def weigh(G):
                    eng.wait_ge(at_ex, 12 * k + 3 * G + 3)
                    if G:
                        eng.wait_ge(at_on, 4 * k + G)
                    p = probs[G % 2]
                    mm(bank(5), vrest(b)[:, G, :], p[:, 4, :], start=True, stop=False, skip_group_check=True)
                    for j in range(4):
                        h = 4 * G + j
                        ins = mm(psum[32 * j:32 * j + 32, 5, :], vmain(b)[:, h * 32:h * 32 + 32], p[:, j, :],
                                 start=False, stop=True, skip_group_check=True)
                    ins.then_inc(at_pv, 1)

                for G in range(G4):
                    g = G // 2
                    for a in range(2):
                        if G:
                            eng.wait_ge(at_ex, 12 * k + 3 * (G - 1) + a + 1)
                        for z in range(2):
                            h = 4 * G + 2 * a + z
                            mm(bank(2 * a + z), keys(b, g)[:, h % 8, 0:P], qt[:, g, :], start=True, stop=False)
                            ins = mm(bank(2 * a + z), selneg[:, h, :], mt[:, :], start=False, stop=True)
                        ins.then_inc(at_s2, 1)
                    if G:
                        eng.wait_ge(at_ex, 12 * k + 3 * G)
                    mm(bank(4), selrest[:, G, :], mt[:, :], start=True, stop=False, skip_group_check=True)
                    for j in range(4):
                        ins = mm(psum[32 * j:32 * j + 32, 4, :], keys(b, g)[:, (4 * G + j) % 8, P:SP_], qt[:, g, :],
                                 start=False, stop=True, skip_group_check=True)
                    ins.then_inc(at_s2, 1)
                    if G:
                        weigh(G - 1)
                weigh(G4 - 1)
                eng.wait_ge(at_on, 4 * k + 4)
                wo = w("wo", G4)
                for i in range(TI):
                    for G in range(G4):
                        ins = mm(psum[:, i, 0:D], ot[:, G, i * P:(i + 1) * P], wo[:, G, :], start=G == 0, stop=G == G4 - 1)
                    ins.then_inc(at_wo, 1)

            def tern(n):
                enter(eng, "pe", n)
                eng.wait_ge(ld_f0, 16)
                eng.wait_ge(tn_w, 1)
                mm(psum[0:RANK, 0, 0:D], f0("fbt")[0:RANK, :], f0("v")[0:RANK, :], start=True, stop=True).then_inc(tn_z, 1)
                eng.wait_ge(tn_zs, 1)
                for m in range(8):
                    if m >= 2:
                        eng.wait_ge(tn_nat, m - 1)
                    mm(psum[:, 1 + m % 2, 0:D], utg[0:RANK, m * P:(m + 1) * P], lowv[0:RANK, :],
                       start=True, stop=True).then_inc(tn_u, 1)
                eng.wait_ge(tn_nat, 10)
                for t in range(8):
                    if t >= 2:
                        eng.wait_ge(tn_ev, t - 1)
                    for z in range(4):
                        if t < 4:
                            kt, m = t // 2, 4 * (t % 2) + z
                            src = fcnat[:, m, kt * P:(kt + 1) * P]
                        else:
                            mo = 4 * (t - 4) + z
                            m, o = mo // 2, mo % 2
                            src = projnat[:, o, m * P:(m + 1) * P]
                        ins = eng.transpose(psum[:, 4 + t % 2, z * P:(z + 1) * P], src, ident)
                    ins.then_inc(tn_tp, 1)

            def ffn0(n, c):
                k, x = instance(n), xt[front_of[n] % 2]
                enter(eng, "pe", n)
                eng.wait_ge(fr_ev, KT * (front_of[n] + 1))
                for m in range(8):
                    if m >= 4:
                        eng.wait_ge(f0_r, 8 * k + m - 3)
                    for kt in range(KT):
                        ins = mm(bank(m % 4), fc_t[:, kt, m * P:(m + 1) * P], x[:, kt, :], start=kt == 0, stop=kt == KT - 1)
                    ins.then_inc(f0_h, 1)
                front(next_front(n))
                eng.wait_ge(f0_sq, 8 * k + 8)
                for i in range(TI):
                    if i >= 2:
                        eng.wait_ge(f0_x, 4 * k + i - 1)
                    for m in range(8):
                        ins = mm(psum[:, 4 + i % 2, 0:D], hid0[:, m, i * P:(i + 1) * P], proj_t[:, m, :], start=m == 0, stop=m == 7)
                    ins.then_inc(f0_y, 1)

            def ffn1(n, c):
                k, x = instance(n), xt[front_of[n] % 2]
                enter(eng, "pe", n)
                eng.wait_ge(ld_f1, 16)
                eng.wait_ge(fr_ev, KT * (front_of[n] + 1))
                for p in range(2):
                    for kt in range(KT):
                        ins = mm(bank(p), w1("wq")[:, kt, p * P:(p + 1) * P], x[:, kt, :], start=kt == 0, stop=kt == KT - 1)
                    ins.then_inc(f1_q, 1)
                eng.wait_ge(f1_qt, 2 * k + 2)
                for i in range(TI):
                    if i >= 2:
                        eng.wait_ge(f1_tk, 4 * k + i - 1)
                    for p in range(2):
                        ins = mm(bank(2 * (i % 2) + p), q1[:, p, i * P:(i + 1) * P], w1("keys")[:, p, :], start=True, stop=True)
                    ins.then_inc(f1_sim, 1)
                for m in range(4):
                    if m:
                        eng.wait_ge(f1_hm, 4 * k + m)
                    for r, name in enumerate(("wg", "wu")):
                        for kt in range(KT):
                            ins = mm(bank(4 + r), w1(name)[:, kt, m * P:(m + 1) * P], x[:, kt, :], start=kt == 0, stop=kt == KT - 1)
                    ins.then_inc(f1_g, 1)
                eng.wait_ge(f1_tk, 4 * k + 4)
                eng.wait_ge(f1_hm, 4 * k + 4)
                for i in range(TI):
                    for m in range(4):
                        ins = mm(psum[:, i, 0:D], hm1[:, m, i * P:(i + 1) * P], w1("wd", 4)[:, m, :], start=m == 0, stop=m == 3)
                    ins.then_inc(f1_y, 1)
                front(next_front(n))

            def ffn2(n, c):
                k, x = instance(n), xt[front_of[n] % 2]
                enter(eng, "pe", n)
                eng.wait_ge(ld_f2, 16)
                eng.wait_ge(fr_ev, KT * (front_of[n] + 1))
                for i in range(TI):
                    for kt in range(KT):
                        ins = mm(psum[:, 5, i * E2:(i + 1) * E2], x[:, kt, i * P:(i + 1) * P], w2("gate")[:, kt, :],
                                 start=kt == 0, stop=kt == KT - 1)
                ins.then_inc(f2_lg, 1)
                gu = w2("gu").rearrange("p k (m r n) -> p k m r n", m=M2, r=2)
                for m in range(M2):
                    if m >= 2:
                        eng.wait_ge(f2_hm, M2 * k + m - 1)
                    for r in range(2):
                        for kt in range(KT):
                            ins = mm(bank(2 * (m % 2) + r), gu[:, kt, m, r, :], x[:, kt, :], start=kt == 0, stop=kt == KT - 1)
                    ins.then_inc(f2_g, 1)
                front(next_front(n))
                eng.wait_ge(f2_hm, M2 * (k + 1))
                down = w2("down", M2)
                for y in range(TI * 9):
                    i, e = y // 9, y % 9
                    if y >= 5:
                        eng.wait_ge(f2_x, TI * 9 * k + y - 4)
                    ms = (8, 9) if e == 8 else (e,)
                    for m in ms:
                        ins = mm(psum[:, y % 5, 0:D], hm2[:, m, i * P:(i + 1) * P], down[:, m, :], start=m == ms[0], stop=m == ms[-1])
                    ins.then_inc(f2_y, 1)

            def ffn3(n, c):
                k, x = instance(n), xt[front_of[n] % 2]
                enter(eng, "pe", n)
                eng.wait_ge(ld_f3, 16)
                eng.wait_ge(fr_ev, KT * (front_of[n] + 1))
                for i in range(TI):
                    for kt in range(KT):
                        ins = mm(psum[:, 5, i * E3:(i + 1) * E3], x[:, kt, i * P:(i + 1) * P], w3("gate")[:, kt, :],
                                 start=kt == 0, stop=kt == KT - 1)
                ins.then_inc(f3_lg, 1)
                for y in range(TI * 4):
                    i, e = y // 4, y % 4
                    if y >= 4:
                        eng.wait_ge(f3_x, TI * 4 * k + y - 3)
                    for kt in range(KT):
                        ins = mm(bank(y % 4), x[:, kt, i * P:(i + 1) * P], w3("we")[:, kt, e * 512:(e + 1) * 512],
                                 start=kt == 0, stop=kt == KT - 1)
                    ins.then_inc(f3_y, 1)
                    if y == 3:
                        eng.wait_ge(f3_gt, k + 1)
                        for t in range(TI):
                            ins = eng.transpose(psum[0:E3, 4, t * P:(t + 1) * P], gate3[:, t * E3:(t + 1) * E3], ident)
                        ins.then_inc(f3_gp, 1)
                front(next_front(n))
                eng.wait_ge(f3_gs, k + 1)
                for i in range(TI):
                    ins = mm(psum[:, 4 + i // 2, (i % 2) * D:(i % 2 + 1) * D], gatet[0:E3, i * P:(i + 1) * P],
                             wb[0:E3, F3["be"]], start=True, stop=True)
                ins.then_inc(f3_b, 1)

            def kv3(n):
                enter(eng, "pe", n)
                eng.wait_ge(ld_attn, 16 * 4)
                eng.wait_ge(ld_ctx, 32)
                for g in range(2):
                    for kt in range(KT):
                        ins = mm(psum[:, g, 0:B * S], w("wk", KT, wattn, CC)[:, kt, g * P:(g + 1) * P], ctxt[:, kt, :],
                                 start=kt == 0, stop=kt == KT - 1)
                ins.then_inc(k3_k, 1)
                for b in range(B):
                    for r, (a, z) in enumerate(((0, P), (P, SP_))):
                        o = psum[0:z - a, 2 + b, r * D:(r + 1) * D]
                        for kt in range(KT):
                            mm(o, ctxr[:, kt, b * SP_ + a:b * SP_ + z], w("wv", KT, wattn, CC)[:, kt, :], start=kt == 0, stop=False)
                        ins = mm(o, valid[:, a:z], wattn[0:1, CC["bv"]], start=False, stop=True)
                ins.then_inc(k3_v, 1)

            def q3(n, c):
                k, x = instance(n), xt[front_of[n] % 2]
                enter(eng, "pe", n)
                eng.wait_ge(fr_ev, KT * (front_of[n] + 1))
                for g in range(2):
                    for kt in range(KT):
                        ins = mm(bank(g), w("wq", KT, wattn, CC)[:, kt, g * P:(g + 1) * P], x[:, kt, :], start=kt == 0, stop=kt == KT - 1)
                ins.then_inc(q3_q, 1)
                front(next_front(n))

            def corr(n, b):
                enter(eng, "pe", n)
                for g in range(2):
                    for N in range(2):
                        for u in range(U):
                            ins = mm(bank(2 * g + N), kst(b, g)[:, u, :], qx[:, g, 16 * u + N * 512:16 * u + N * 512 + 512],
                                     start=u == 0, stop=u == U - 1)
                    ins.then_inc(co_c, 1)
                eng.wait_ge(co_rd, 32 * (b + 1))
                for g in range(2):
                    a = 2 * b + g
                    for N in range(2):
                        ins = mm(psum[0:32, 4 + N, :], selh[:, a, :], c2[g][:, N * 512:(N + 1) * 512], start=a == 0, stop=a == 3,
                                 skip_group_check=True)
                ins.then_inc(co_m, 1)

            def out3(n, b):
                enter(eng, "pe", n)
                eng.wait_ge(tp_rd, 16 * 4)
                for g in range(2):
                    for N in range(2):
                        for u in range(U):
                            at = SP_ - 16 * u + N * 512
                            ins = mm(bank(2 * g + N), vst(b, g)[:, u, :], roll(2 * b + g)[:, at:at + 512],
                                     start=u == 0, stop=u == U - 1)
                        ins.then_inc(o3_o, 1)
                front(next_front(n))
                eng.wait_ge(o3_s, 4 * b + 4)
                for i in range(8):
                    if i >= 2:
                        eng.wait_ge(o3_x, 8 * b + i - 1)
                    for g in range(2):
                        ins = mm(psum[:, 4 + i % 2, 0:D], ot3[:, g, i * P:(i + 1) * P], w("wo", KT, wattn, CC)[:, g, :],
                                 start=g == 0, stop=g == 1)
                    ins.then_inc(o3_y, 1)

            for n, (kind, layer, c) in enumerate(phases):
                {"kv": lambda: kv(n, layer), "attn": lambda: attn(n, layer, c), "tern": lambda: tern(n),
                 "ffn0": lambda: ffn0(n, c), "ffn1": lambda: ffn1(n, c), "ffn2": lambda: ffn2(n, c), "ffn3": lambda: ffn3(n, c),
                 "kv3": lambda: kv3(n), "q3": lambda: q3(n, c), "corr": lambda: corr(n, layer), "top": lambda: enter(eng, "pe", n),
                 "out3": lambda: out3(n, layer)}[kind]()
                leave(eng, "pe")

        @block.scalar
        def _(eng):
            act = eng.activation
            own = Own(eng, own_act)

            def front(f):
                if f is None:
                    return
                for kt in range(KT):
                    eng.wait_ge(fr_tp, KT * f + kt + 1)
                    act(xt[f % 2][:, kt, :], bank(6 + kt), ACT.Copy).then_inc(fr_ev, 1)

            def kv(n, layer):
                enter(eng, "act", n)
                eng.wait_ge(kv_k, layer + 1)
                for g in range(2):
                    act(kts[:, g, :], psum[:, g, 0:B * S], ACT.Identity, bias=wattn[:, AC["bk"].start + g:AC["bk"].start + g + 1])\
                        .then_inc(kv_kt, 1)
                if layer < 2:
                    act(bqs[:, :], wattn[:, AC["bq"]], ACT.Copy, scale=0.25).then_inc(kv_kt, 1)
                if n == 0:
                    front(0)

            def attn(n, layer, c):
                k, b = instance(n), c // 2
                enter(eng, "act", n)
                if layer == 2:
                    for g in range(2):
                        eng.wait_ge(at_qt, 2 * k + g + 1)
                        act(qb[:, g, :], qt[:, g, :], ACT.Copy).then_inc(at_qb, 1)
                else:
                    eng.wait_ge(at_q, k + 1)
                    for g in range(2):
                        act(qb[:, g, :], bank(g), ACT.Identity, bias=bqs[:, g:g + 1], scale=0.25).then_inc(at_qb, 1)
                        act(qt[:, g, :], bank(g), ACT.Identity, bias=bqs[:, g:g + 1], scale=0.25).then_inc(at_qt, 1)
                front(next_front(n))
                eng.wait_ge(at_mt, k + 1)
                act(mt[0:H, :], psum[0:H, 0, :], ACT.Copy).then_inc(at_mts, 1)
                for G in range(G4):
                    p = probs[G % 2]
                    if G >= 2:
                        eng.wait_ge(at_pv, 4 * k + G - 1)
                    for a in range(2):
                        eng.wait_ge(at_s2, 12 * k + 3 * G + a + 1)
                        act(p[:, 2 * a:2 * a + 2, :], psum[:, 2 * a:2 * a + 2, :], ACT.Exp).then_inc(at_ex, 1)
                    eng.wait_ge(at_s2, 12 * k + 3 * G + 3)
                    act(p[:, 4, :], bank(4), ACT.Exp, bias=padrow).then_inc(at_ex, 1)

            def tern(n):
                enter(eng, "act", n)
                eng.wait_ge(tn_z, 1)
                act(lowv[0:RANK, :], psum[0:RANK, 0, 0:D], ACT.Copy).then_inc(tn_zs, 1)
                for t in range(8):
                    eng.wait_ge(tn_tp, t + 1)
                    if t < 4:
                        kt, m = t // 2, 4 * (t % 2)
                        dst = fc_t[:, kt, m * P:(m + 4) * P]
                    else:
                        m = 2 * (t - 4)
                        dst = proj_t[:, m:m + 2, :].rearrange("p m n -> p (m n)")
                    act(dst, bank(4 + t % 2), ACT.Copy).then_inc(tn_ev, 1)

            def ffn0(n, c):
                k = instance(n)
                enter(eng, "act", n)
                for m in range(8):
                    eng.wait_ge(f0_h, 8 * k + m + 1)
                    act(hid0r[:, m, :], bank(m % 4), ACT.Relu).then_inc(f0_r, 1)
                front(next_front(n))

            def ffn1(n, c):
                k = instance(n)
                enter(eng, "act", n)
                for p in range(2):
                    eng.wait_ge(f1_q, 2 * k + p + 1)
                    act(q1[:, p, :], bank(p), ACT.Copy).then_inc(f1_qt, 1)
                for m in range(4):
                    eng.wait_ge(f1_g, 4 * k + m + 1)
                    act(sg1[:, m % 2, :], bank(4), ACT.Silu).then_inc(f1_sg, 1)
                eng.wait_ge(f1_sc, k + 1)
                act(ex1[:, :], ex1[:, :], ACT.Exp).then_inc(f1_se, 1)
                front(next_front(n))
                for g in range(TI * NG):
                    eng.wait_ge(f1_dot, TI * NG * k + g + 1)
                    act(sdot[:, g % 4, :], dots[:, g % 4, :], ACT.Silu).then_inc(f1_sd, 1)

            def ffn2(n, c):
                k = instance(n)
                enter(eng, "act", n)
                eng.wait_ge(f2_lg, k + 1)
                act(sc2[:, :], psum[:, 5, 0:TI * E2], ACT.Sigmoid).then_inc(f2_sc, 1)
                for m in range(M2):
                    eng.wait_ge(f2_g, M2 * k + m + 1)
                    if m >= 2:
                        eng.wait_ge(f2_hm, M2 * k + m - 1)
                    act(sg2[:, m % 2, :], bank(2 * (m % 2)), ACT.Silu).then_inc(f2_sg, 1)
                front(next_front(n))

            def ffn3(n, c):
                k = instance(n)
                enter(eng, "act", n)
                eng.wait_ge(f3_ls, k + 1)
                act(ex3[:, :], ex3[:, :], ACT.Exp).then_inc(f3_ex, 1)
                eng.wait_ge(f3_gp, k + 1)
                act(gatet[0:E3, :], psum[0:E3, 4, :], ACT.Copy).then_inc(f3_gs, 1)
                front(next_front(n))

            def kv3(n):
                enter(eng, "act", n)
                eng.wait_ge(k3_k, 1)
                for g in range(2):
                    for b in range(B):
                        act(k3t[:, g, b * SP_:b * SP_ + S], psum[:, g, b * S:(b + 1) * S], ACT.Identity,
                            bias=wattn[:, CC["bk"].start + g:CC["bk"].start + g + 1]).then_inc(k3_kt, 1)
                eng.wait_ge(k3_v, 1)
                for b in range(B):
                    act(v3m[:, b, :], psum[:, 2 + b, 0:D], ACT.Copy).then_inc(k3_vs, 1)
                    act(v3r[0:32, b, :], psum[0:32, 2 + b, D:2 * D], ACT.Copy).then_inc(k3_vs, 1)

            def q3(n, c):
                k = instance(n)
                enter(eng, "act", n)
                eng.wait_ge(q3_q, k + 1)
                at = (c % 2) * CH
                for g in range(2):
                    bias = wattn[:, CC["bq"].start + g:CC["bq"].start + g + 1]
                    act(qx[:, g, at:at + CH], bank(g), ACT.Identity, bias=bias)
                    if c % 2 == 0:
                        act(qx[:, g, T:EXT], psum[:, g, 0:SP_], ACT.Identity, bias=bias)
                front(next_front(n))

            def corr(n, b):
                enter(eng, "act", n)
                for g in range(2):
                    eng.wait_ge(co_c, 2 * b + g + 1)
                    act(c1[g][:, 0:T], psum[:, 2 * g:2 * g + 2, :].rearrange("p a n -> p (a n)"), ACT.Copy).then_inc(co_s, 1)
                    act(c1[g][:, T:T + 16], psum[:, 2 * g, 0:16], ACT.Copy).then_inc(co_s, 1)

            def top(n):
                enter(eng, "act", n)
                eng.wait_ge(tp_n, 1)
                act(topw[0:32, 0:8], topw[0:32, 0:8], ACT.Exp).then_inc(tp_e, 1)

            def out3(n, b):
                enter(eng, "act", n)
                for g in range(2):
                    for N in range(2):
                        eng.wait_ge(o3_o, 4 * b + 2 * g + N + 1)
                        act(ot3[:, g, N * 512:(N + 1) * 512], bank(2 * g + N), ACT.Copy).then_inc(o3_s, 1)
                front(next_front(n))

            for n, (kind, layer, c) in enumerate(phases):
                {"kv": lambda: kv(n, layer), "attn": lambda: attn(n, layer, c), "tern": lambda: tern(n),
                 "ffn0": lambda: ffn0(n, c), "ffn1": lambda: ffn1(n, c), "ffn2": lambda: ffn2(n, c), "ffn3": lambda: ffn3(n, c),
                 "kv3": lambda: kv3(n), "q3": lambda: q3(n, c), "corr": lambda: corr(n, layer), "top": lambda: top(n),
                 "out3": lambda: out3(n, layer)}[kind]()
                leave(eng, "act")

        @block.vector
        def _(eng):
            own = Own(eng, own_dve)
            tt, ts, stt = eng.tensor_tensor, eng.tensor_scalar, eng.scalar_tensor_tensor

            def cast(ap, shape):
                return ap.broadcast_to(shape)

            def front(f):
                if f is None:
                    return
                c = phases[fronts[f]][2]
                for i in range(TI):
                    own.mark(eng.bn_stats(stats[:, i, :], x_sb[:, c * TI + i, :]))
                own.wait()
                for i in range(TI):
                    own.mark(eng.bn_aggr(mv[:, i, :], stats[:, i, :]))
                own.wait()
                ts(vare[:, :], mv[:, :, 1], EPS, None, ALU.add).then_inc(fr_var, 1)
                eng.wait_ge(fr_rstd, f + 1)
                for i in range(TI):
                    ts(xn[f % 2][:, i, :], x_sb[:, c * TI + i, :], mv[:, i, 0:1], rstd[:, i:i + 1], ALU.subtract, ALU.mult)\
                        .then_inc(fr_xn, 1)

            def add_x(c, i, src):
                return tt(x_sb[:, c * TI + i, :], x_sb[:, c * TI + i, :], src, ALU.add)

            def kv(n, layer):
                enter(eng, "dve", n)
                if n == 0:
                    eng.wait_ge(ld_x, 16)
                    front(0)
                eng.wait_ge(kv_kt, (3, 6, 8)[layer])
                if layer == 2:
                    eng.wait_ge(ld_rope, 16)
                    cos, sin = rope[:, 0:S], rope[:, T:T + S]
                    for g in range(2):
                        for b in range(B):
                            at = slice(b * S, (b + 1) * S)
                            own.mark(tt(kts[:, g, at], kts[:, g, at], cos, ALU.mult))
                            own.mark(tt(ktr[:, g, at], psum[:, 2 + g, at], sin, ALU.mult))
                    own.wait()
                    own.link(tt(kts, kts, ktr, ALU.add))
                for b in range(B):
                    for g in range(2):
                        own.mark(eng.memset(keys(b, g)[:, :, S:SP_], 0.0))
                        own.mark(tt(keys(b, g)[:, :, 0:S], cast(kts[:, g, b * S:(b + 1) * S].unsqueeze(1), [P, 8, S]),
                                    cast(mask8.unsqueeze(2), [P, 8, S]), ALU.mult))
                own.wait()
                for b in range(B):
                    for g in range(2):
                        eng.tensor_copy(keysb(b, g).rearrange("p (h k) -> p h k", h=8), keys(b, g)[:, :, 0:S])
                eng.wait_ge(kv_v, layer + 1)
                eng.wait_ge(kv_z, layer + 1)
                for b in range(B):
                    eng.tensor_copy(vmain(b).rearrange("p (h n) -> p h n", h=H)[:, :, 0:DH],
                                    psum[:, 4 + b, 0:D].rearrange("p (h d) -> p h d", h=H))
                    for j in range(4):
                        r = slice(32 * j, 32 * j + SR)
                        eng.tensor_copy(vrest(b)[r, :, j * 32:j * 32 + DH],
                                        psum[r, 4 + b, D:2 * D].rearrange("p (g j d) -> p g j d", g=G4, j=4)[:, :, j, :])

            def attn(n, layer, c):
                k = instance(n)
                enter(eng, "dve", n)
                if layer == 2:
                    eng.wait_ge(at_q, k + 1)
                    at = (c % 2) * CH
                    cos, sin = rope[:, at:at + CH], rope[:, T + at:T + at + CH]
                    for g in range(2):
                        own.mark(stt(qt[:, g, :], bank(g), 0.25, cos, ALU.mult, ALU.mult))
                        own.link(stt(ropet[:, g, :], bank(2 + g), 0.25, sin, ALU.mult, ALU.mult))
                        tt(qt[:, g, :], qt[:, g, :], ropet[:, g, :], ALU.add).then_inc(at_qt, 1)
                front(next_front(n))
                for u in range(16):
                    i, g, hf, pair = u // 4, (u // 2) % 2, u % 2, 2 * (u % 3)
                    eng.wait_ge(at_p1, 16 * k + u + 1)
                    eng.reduce_max(m4[:, i, g * 8 + hf * 4:g * 8 + hf * 4 + 4].rearrange("p (a b) -> p a b", a=2),
                                   psum[:, pair:pair + 2, 0:2 * S].rearrange("p a (b s) -> p a b s", b=2), AX.X)\
                        .then_inc(at_mx, 1)
                for G in range(G4):
                    eng.wait_ge(at_pv, 4 * k + G + 1)
                    own.link(eng.reciprocal(den, bank(5)))
                    own.link(eng.stream_shuffle(rec, den, [16] * 32))
                    tt(ot[:, G, :], bank(5), rec, ALU.mult).then_inc(at_on, 1)
                if layer < 2:
                    eng.wait_ge(at_bo, k + 1)
                for i in range(TI):
                    eng.wait_ge(at_wo, 4 * k + i + 1)
                    add_x(c, i, psum[:, i, 0:D])

            def tern(n):
                enter(eng, "dve", n)
                eng.wait_ge(ld_f0, 16)
                ts(utg[0:RANK, :], utg[0:RANK, :], f0("gate")[0:RANK, :], None, ALU.mult).then_inc(tn_w, 1)
                own.mark(eng.tensor_reduce(absum[:, 0:8], fcnat, AX.X, ALU.add, apply_absolute_value=True))
                own.link(eng.tensor_reduce(absum[:, 8:10], projnat, AX.X, ALU.add, apply_absolute_value=True))
                own.mark(ts(sclip[:, 0:8], absum[:, 0:8], 1.0 / D, 1e-5, ALU.mult, ALU.max))
                own.link(ts(sclip[:, 8:10], absum[:, 8:10], 1.0 / HID0, 1e-5, ALU.mult, ALU.max))
                own.mark(ts(hi_th, sclip, 0.5, None, ALU.mult))
                own.link(ts(lo_th, sclip, -0.5, None, ALU.mult))
                for r in range(10):
                    nat, n_ = (fcnat[:, r, :], D) if r < 8 else (projnat[:, r - 8, :], HID0)
                    own.mark(ts(tplus[:, 0:n_], nat, hi_th[:, r:r + 1], sclip[:, r:r + 1], ALU.is_gt, ALU.mult))
                    own.link(ts(tminus[:, 0:n_], nat, lo_th[:, r:r + 1], sclip[:, r:r + 1], ALU.is_lt, ALU.mult))
                    if r < 8:
                        own.link(tt(nat, tplus[:, 0:n_], tminus[:, 0:n_], ALU.subtract))
                        eng.wait_ge(tn_u, r + 1)
                        tt(nat, nat, psum[:, 1 + r % 2, 0:D], ALU.add).then_inc(tn_nat, 1)
                    else:
                        tt(nat, tplus[:, 0:n_], tminus[:, 0:n_], ALU.subtract).then_inc(tn_nat, 1)
                        eng.wait_ge(tn_nat, r + 1)

            def ffn0(n, c):
                k = instance(n)
                enter(eng, "dve", n)
                front(next_front(n))
                for m in range(8):
                    eng.wait_ge(f0_r, 8 * k + m + 1)
                    tt(hid0[:, m, :], hid0r[:, m, :], hid0r[:, m, :], ALU.mult).then_inc(f0_sq, 1)
                for i in range(TI):
                    eng.wait_ge(f0_y, 4 * k + i + 1)
                    add_x(c, i, psum[:, 4 + i % 2, 0:D]).then_inc(f0_x, 1)

            def ffn1(n, c):
                k, xnc = instance(n), xn[front_of[n] % 2]
                enter(eng, "dve", n)
                front(next_front(n))
                for i in range(TI):
                    eng.wait_ge(f1_sim, 4 * k + i + 1)
                    for p in range(2):
                        for h in range(PH):
                            own.mark(eng.max(topv[:, p, i * PH + h, :], psum[:, 2 * (i % 2) + p, h * NKEY:(h + 1) * NKEY]))
                    own.wait()
                    for p in range(2):
                        for h in range(PH):
                            ins = eng.max_index(topi[:, p, i * PH + h, :], topv[:, p, i * PH + h, :],
                                                psum[:, 2 * (i % 2) + p, h * NKEY:(h + 1) * NKEY])
                    ins.then_inc(f1_tk, 1)
                for m in range(4):
                    eng.wait_ge(f1_sg, 4 * k + m + 1)
                    tt(hm1[:, m, :], sg1[:, m % 2, :], bank(5), ALU.mult).then_inc(f1_hm, 1)
                eng.wait_ge(f1_tk, 4 * k + 4)
                own.mark(eng.tensor_copy(topf, topi))
                R = 16
                own.link(tt(sums, cast(topv[:, 0].unsqueeze(3), [P, R, 8, 8]), cast(topv[:, 1].unsqueeze(2), [P, R, 8, 8]), ALU.add))
                for r in range(R):
                    own.mark(eng.max(best[:, r, :], sums[:, r].rearrange("p i j -> p (i j)")))
                own.wait()
                ex = ex1.rearrange("p (r k) -> p r k", r=R)
                tt(ex, best, cast(best[:, :, 0:1], [P, R, 8]), ALU.subtract).then_inc(f1_sc, 1)
                for r in range(R):
                    own.mark(eng.max_index(pos[:, r * 8:r * 8 + 8], best[:, r, :], sums[:, r].rearrange("p i j -> p (i j)")))
                own.wait()
                own.mark(ts(pside[0], pos, 3, None, ALU.logical_shift_right))
                own.link(ts(pside[1], pos, 7, None, ALU.bitwise_and))
                for z in range(2):
                    own.mark(eng.tensor_copy(psidef[z], pside[z]))
                own.wait()
                for z in range(2):
                    own.mark(tt(eq[z].rearrange("p r k j -> p (r k) j"), cast(psidef[z].unsqueeze(2), [P, P, 8]),
                                cast(iota8.unsqueeze(1), [P, P, 8]), ALU.is_equal))
                own.wait()
                for z in range(2):
                    own.mark(tt(eq[z], eq[z], cast(topf[:, z].unsqueeze(2), [P, R, 8, 8]), ALU.mult))
                own.wait()
                for z in range(2):
                    own.mark(eng.reduce_sum(pick[z], eq[z].rearrange("p r k j -> p (r k) j"), AX.X))
                own.wait()
                own.link(stt(rowf, pick[0], float(NKEY), pick[1], ALU.mult, ALU.add))
                ts(rowid, rowf, float(NEXP1 - 1), None, ALU.min).then_inc(f1_idx, 1)
                eng.wait_ge(f1_se, k + 1)
                own.link(eng.reduce_sum(esum, ex, AX.X))
                own.link(eng.reciprocal(erec, esum))
                own.mark(tt(prob1.rearrange("p (r k) -> p r k", r=R), ex, cast(erec.unsqueeze(2), [P, R, 8]), ALU.mult))
                for i in range(TI):
                    eng.wait_ge(f1_y, 4 * k + i + 1)
                    own.mark(add_x(c, i, psum[:, i, 0:D]))
                own.wait()

                def accumulate(g):
                    i, base = g // NG, GRP * ((TI * NG * k + g) % (RING // GRP))
                    eng.wait_ge(f1_sd, TI * NG * k + g + 1)
                    own.link(tt(ew[:, g % 4, :], sdot[:, g % 4, :], prob1[:, g * GRP:(g + 1) * GRP], ALU.mult))
                    for j in range(GRP):
                        ins = stt(x_sb[:, c * TI + i, :], ring[:, base + j, D:2 * D], ew[:, g % 4, j:j + 1],
                                  x_sb[:, c * TI + i, :], ALU.mult, ALU.add)
                        if j < GRP - 1:
                            own.link(ins)
                    ins.then_inc(f1_acc, 1)

                for g in range(TI * NG):
                    G = TI * NG * k + g
                    i, base = g // NG, GRP * (G % (RING // GRP))
                    eng.wait_ge(gathered[G % (RING // GRP)], 16 * GRP * (G // (RING // GRP) + 1))
                    if G:
                        eng.wait_ge(f1_dot, G)
                    for j in range(GRP):
                        ins = eng.tensor_tensor_reduce(junk[:, j, :], xnc[:, i, :], ring[:, base + j, 0:D], 1.0, 0.0,
                                                       ALU.mult, ALU.add, dots[:, g % 4, j:j + 1])
                    ins.then_inc(f1_dot, 1)
                    if g:
                        accumulate(g - 1)
                        eng.wait_ge(f1_acc, G)
                accumulate(TI * NG - 1)

            def ffn2(n, c):
                k = instance(n)
                enter(eng, "dve", n)
                front(next_front(n))
                eng.wait_ge(f2_sc, k + 1)
                best_two(sc2, tv2, ti2, tf2)
                own.link(tt(s2[0], tv2[:, :, 0], tv2[:, :, 1], ALU.add))
                own.link(ts(s2[1], s2[0], 1e-20, None, ALU.add))
                own.link(eng.reciprocal(s2[2], s2[1]))
                own.link(ts(s2[3], s2[2], 2.5, None, ALU.mult))
                spread(comb2, tv2, tf2, s2[3])
                for m in range(M2):
                    eng.wait_ge(f2_sg, M2 * k + m + 1)
                    tt(hm2[:, m, :], sg2[:, m % 2, :], bank(2 * (m % 2) + 1), ALU.mult).then_inc(f2_hm, 1)
                for y in range(TI * 9):
                    i, e, K = y // 9, y % 9, TI * 9 * k + y
                    eng.wait_ge(f2_y, K + 1)
                    if e:
                        eng.wait_ge(f2_x, K)
                    src = psum[:, y % 5, 0:D]
                    ins = add_x(c, i, src) if e == 8 else stt(
                        x_sb[:, c * TI + i, :], src, comb2[0][:, i, e:e + 1], x_sb[:, c * TI + i, :], ALU.mult, ALU.add)
                    ins.then_inc(f2_x, 1)

            def best_two(src, tv, ti, tf):
                for i in range(TI):
                    own.mark(eng.max(tv[:, i, :], src[:, i * 8:(i + 1) * 8]))
                own.wait()
                for i in range(TI):
                    own.mark(eng.max_index(ti[:, i, :], tv[:, i, :], src[:, i * 8:(i + 1) * 8]))
                own.wait()
                own.link(eng.tensor_copy(tf, ti))

            def spread(comb, tv, tf, scale):
                shape = [P, TI, 8]
                for r in range(2):
                    own.mark(tt(comb[r], cast(tf[:, :, r:r + 1], shape), cast(iota8.unsqueeze(1), shape), ALU.is_equal))
                own.wait()
                for r in range(2):
                    own.mark(tt(comb[r], comb[r], cast(tv[:, :, r:r + 1], shape), ALU.mult))
                own.wait()
                own.link(tt(comb[2], comb[0], comb[1], ALU.add))
                own.link(tt(comb[0], comb[2], cast(scale.unsqueeze(2), shape), ALU.mult))

            def ffn3(n, c):
                k = instance(n)
                enter(eng, "dve", n)
                front(next_front(n))
                eng.wait_ge(f3_lg, k + 1)
                lg = psum[:, 5, 0:TI * E3].rearrange("p (i e) -> p i e", i=TI)
                shape = [P, TI, E3]
                ex = ex3.rearrange("p (i e) -> p i e", i=TI)
                own.link(eng.reduce_max(mx3, lg, AX.X))
                tt(ex, lg, cast(mx3.unsqueeze(2), shape), ALU.subtract).then_inc(f3_ls, 1)
                eng.wait_ge(f3_ex, k + 1)
                own.link(eng.reduce_sum(s3[0], ex, AX.X))
                own.link(eng.reciprocal(s3[1], s3[0]))
                own.link(tt(pr3.rearrange("p (i e) -> p i e", i=TI), ex, cast(s3[1].unsqueeze(2), shape), ALU.mult))
                best_two(pr3, tv3, ti3, tf3)
                own.link(tt(s3[2], tv3[:, :, 0], tv3[:, :, 1], ALU.add))
                own.link(eng.reciprocal(s3[3], s3[2]))
                spread(comb3, tv3, tf3, s3[3])
                eng.sem_inc(f3_gt, 1)
                for y in range(TI * 4):
                    i, K = y // 4, TI * 4 * k + y
                    eng.wait_ge(f3_y, K + 1)
                    if y % 4:
                        eng.wait_ge(f3_x, K)
                    for r in range(2):
                        e = 2 * (y % 4) + r
                        ins = stt(x_sb[:, c * TI + i, :], psum[:, y % 4, r * D:(r + 1) * D], comb3[0][:, i, e:e + 1],
                                  x_sb[:, c * TI + i, :], ALU.mult, ALU.add)
                        if r == 0:
                            own.link(ins)
                    ins.then_inc(f3_x, 1)
                eng.wait_ge(f3_x, TI * 4 * (k + 1))
                eng.wait_ge(f3_b, k + 1)
                for i in range(TI):
                    add_x(c, i, psum[:, 4 + i // 2, (i % 2) * D:(i % 2 + 1) * D])

            def kv3(n):
                enter(eng, "dve", n)
                for g in range(2):
                    for b in range(B):
                        own.mark(eng.memset(k3t[:, g, b * SP_ + S:(b + 1) * SP_], 0.0))
                own.wait()
                eng.wait_ge(k3_kt, 4)
                shape = [P, U, 8, 16]
                mask = cast(mask8.unsqueeze(1).unsqueeze(3), shape)
                for b in range(B):
                    for g in range(2):
                        src = k3t[:, g, b * SP_:(b + 1) * SP_].rearrange("p (u s) -> p u s", u=U)
                        tt(kst(b, g).rearrange("p u (h s) -> p u h s", h=8), cast(src.unsqueeze(2), shape), mask, ALU.mult)
                eng.wait_ge(k3_rd, 16 * 32)
                for b in range(B):
                    for g in range(2):
                        tt(vst(b, g).rearrange("p u (h d) -> p u h d", h=8), cast(v3s[:, 2 * b + g].unsqueeze(2), shape), mask, ALU.mult)

            def top(n):
                enter(eng, "dve", n)
                r = slice(0, 32)
                eng.wait_ge(co_m, 2)
                own.link(eng.tensor_copy(cor[r, :], psum[r, 4:6, :].rearrange("p a n -> p (a n)")))
                own.link(eng.max(topm[r, :], cor[r, :]))
                own.mark(eng.max_index(topj[r, :], topm[r, :], cor[r, :]))
                tt(topw[r, :], topm[r, :], cast(topm[r, 0:1], [32, 8]), ALU.subtract).then_inc(tp_n, 1)
                own.wait()
                own.link(eng.tensor_copy(topjf[r, :], topj[r, :]))
                own.link(ts(topjf[r, :], topjf[r, :], -1.0, float(T), ALU.mult, ALU.add))
                own.link(ts(topm[r, :], topjf[r, :], float(T), float(T), ALU.is_ge, ALU.mult))
                own.link(tt(topjf[r, :], topjf[r, :], topm[r, :], ALU.subtract))
                eng.wait_ge(tp_e, 1)
                own.link(eng.reduce_sum(rsum3[r, 0:1], topw[r, 0:TOPC], AX.X))
                own.link(eng.reciprocal(rsum3[r, 1:2], rsum3[r, 0:1]))
                own.link(ts(topw[r, :], topw[r, :], rsum3[r, 1:2], None, ALU.mult))
                for k in range(TOPC):
                    out = rollw[0] if k == 0 else rollt[k % 2]
                    own.link(ts(out[r, :], iota[r, :], topjf[r, k:k + 1], topw[r, k:k + 1], ALU.is_equal, ALU.mult))
                    if k:
                        own.link(tt(rollw[0][r, :], rollw[0][r, :], out[r, :], ALU.add))
                eng.sem_inc(tp_r, 1)

            def out3(n, b):
                enter(eng, "dve", n)
                front(next_front(n))
                eng.wait_ge(o3_bo, b + 1)
                for i in range(8):
                    eng.wait_ge(o3_y, 8 * b + i + 1)
                    add_x(2 * b, i, psum[:, 4 + i % 2, 0:D]).then_inc(o3_x, 1)

            def q3(n):
                enter(eng, "dve", n)
                front(next_front(n))

            for n, (kind, layer, c) in enumerate(phases):
                {"kv": lambda: kv(n, layer), "attn": lambda: attn(n, layer, c), "tern": lambda: tern(n),
                 "ffn0": lambda: ffn0(n, c), "ffn1": lambda: ffn1(n, c), "ffn2": lambda: ffn2(n, c), "ffn3": lambda: ffn3(n, c),
                 "kv3": lambda: kv3(n), "q3": lambda: q3(n), "corr": lambda: enter(eng, "dve", n), "top": lambda: top(n),
                 "out3": lambda: out3(n, layer)}[kind]()
                leave(eng, "dve")

        @block.gpsimd
        def _(eng):
            own = Own(eng, own_pool)

            def front(f):
                if f is None:
                    return
                eng.wait_ge(fr_var, f + 1)
                eng.tensor_tensor(rstd[:, :], vare[:, :], half[:, :], ALU.pow).then_inc(fr_rstd, 1)

            def bias(c, tiles):
                row = wattn[:, AC["bo"]] if tiles == TI else wattn[:, CC["bo"]]
                for i in range(tiles):
                    t = c * TI + i
                    ins = eng.tensor_tensor(x_sb[:, t, :], x_sb[:, t, :], row, ALU.add)
                return ins

            own.mark(eng.memset(half[:, :], -0.5))
            own.mark(eng.memset(mt[:, :], 0.0))
            own.wait()
            for n, (kind, layer, c) in enumerate(phases):
                enter(eng, "pool", n)
                if kind == "kv":
                    if n == 0:
                        eng.wait_ge(ld_const, 32)
                        own.mark(eng.tensor_copy(selneg[:, :, :].rearrange("p a n -> p (a n)"), selraw[:, SC["selneg"]]))
                        own.mark(eng.tensor_copy(selrest[:, :, :].rearrange("p a n -> p (a n)"), selraw[:, SC["selrest"]]))
                        front(0)
                    for b in range(B):
                        own.mark(eng.memset(vmain(b).rearrange("p (h n) -> p h n", h=H)[:, :, DH:32], 1.0))
                        own.mark(eng.memset(vrest(b), 0.0))
                    own.wait()
                    for b in range(B):
                        for j in range(4):
                            ins = eng.memset(vrest(b)[32 * j:32 * j + SR, :, j * 32 + DH:j * 32 + 32], 1.0)
                    ins.then_inc(kv_z, 1)
                if kind in ("attn", "ffn0", "ffn1", "ffn2", "ffn3", "q3", "out3"):
                    front(next_front(n))
                if kind == "attn" and layer < 2:
                    bias(c, TI).then_inc(at_bo, 1)
                if kind == "out3":
                    bias(2 * layer, 8).then_inc(o3_bo, 1)
                if kind == "ffn1":
                    k = instance(n)
                    eng.wait_ge(f1_idx, k + 1)
                    for g in range(TI * NG):
                        G = TI * NG * k + g
                        s = G % (RING // GRP)
                        if G >= RING // GRP:
                            eng.wait_ge(f1_acc, G - RING // GRP + 1)
                        for j in range(GRP):
                            eng.indirect_dma_start(ring[:, s * GRP + j, :], None, io["table"],
                                                   bass.IndirectOffsetOnAxis(ap=rowid[:, g * GRP + j:g * GRP + j + 1], axis=0))\
                                .then_inc(gathered[s], 16)
                leave(eng, "pool")

        @block.sync
        def _(eng):
            loads = {}

            def load(dst, src, s):
                loads[s.name] = (s, loads.get(s.name, (s, 0))[1] + 16)
                eng.dma_start(dst, src).then_inc(s, 16)

            def last(kind, layer):
                ns = [n for n, p in enumerate(phases) if p[0] == kind and p[1] == layer]
                return max(ns) if ns else None

            def after(n):
                for s in ends.values():
                    eng.wait_ge(s, n + 1)

            load(x_sb[:, :, :], io["x"].rearrange("(i p) d -> p i d", p=P), ld_x)
            load(const[:, :], io["const"], ld_const)
            load(selraw, io["select"], ld_const)
            load(ctxt[:, :, :].rearrange("p k n -> p (k n)"), io["ctxt"], ld_ctx)
            load(wattn[:, 0:AN], io["attn0"], ld_attn)
            load(ctxr[:, :, :].rearrange("p k n -> p (k n)"), io["ctxr"], ld_ctx)
            load(wb[:, 0:F0N], io["ffn0"], ld_f0)
            load(rope[:, :], io["rope"], ld_rope)
            for n, (kind, layer, c) in enumerate(phases):
                if kind == "kv3":
                    enter(eng, "sp", n)
                    eng.wait_ge(k3_vs, 4)
                    for b in range(B):
                        eng.dma_start(scrv[b, 0:P, :], v3m[:, b, :]).then_inc(k3_wr, 16)
                        eng.dma_start(scrv[b, P:SP_, :], v3r[0:32, b, :]).then_inc(k3_wr, 16)
                    eng.wait_ge(k3_wr, 16 * 4)
                    for b in range(B):
                        for g in range(2):
                            src = scrv[b].rearrange("(u s) (a h d) -> a h s u d", s=16, a=2, d=DH)[g]
                            for h in range(8):
                                eng.dma_start(v3s[h * 16:(h + 1) * 16, 2 * b + g], src[h]).then_inc(k3_rd, 16)
                if kind == "corr":
                    for g in range(2):
                        a = 2 * layer + g
                        eng.wait_ge(co_s, 4 * layer + 2 * g + 2)
                        eng.dma_start(scr1[a], c1[g]).then_inc(co_wr, 16)
                    for g in range(2):
                        a = 2 * layer + g
                        eng.wait_ge(co_wr, 16 * 2 * (layer + 1))
                        src = bass.AP(scr1.tensor, a * P * (T + 16), [[16 * (T + 16), 8], [T + 17, 16], [1, T]])
                        eng.dma_start(c2[g], src).then_inc(co_rd, 16)
                if kind == "top":
                    eng.wait_ge(tp_r, 1)
                    for z in range(2):
                        eng.dma_start(scr2[:, z * T:(z + 1) * T], rollw[0][0:32, :]).then_inc(tp_wr, 16)
                    eng.wait_ge(tp_wr, 32)
                    for a in range(4):
                        src = bass.AP(scr2.tensor, 8 * a * 2 * T + T - SP_ - 15, [[2 * T, 8], [1, 16], [1, T + SP_]])
                        eng.dma_start(roll(a), src).then_inc(tp_rd, 16)
                if kind == "ffn3" or (stop is not None and n == len(phases) - 1):
                    eng.wait_ge(ends["dve"], n + 1)
                    for q in ([c] if kind == "ffn3" else range(NCH)):
                        eng.dma_start(io["out"].rearrange("(i p) d -> p i d", p=P)[:, q * TI:(q + 1) * TI, :],
                                      x_sb[:, q * TI:(q + 1) * TI, :]).then_inc(stored, 16)
                if kind == "attn" and n == last("attn", layer):
                    after(n)
                    if layer < 2:
                        load(wattn[:, 0:AN], io[f"attn{layer + 1}"], ld_attn)
                    else:
                        load(wattn[:, 0:CN], io["corr"], ld_attn)
                if kind == "tern":
                    after(n)
                    load(wb[:, 0:F1N], io["ffn1"], ld_f1)
                if n == last("ffn0", 0):
                    after(n)
                    load(wa[:, 0:F2N], io["ffn2"], ld_f2)
                if n == last("ffn1", 1):
                    after(n)
                    load(wb[:, 0:F3N], io["ffn3"], ld_f3)
            eng.wait_ge(stored, 16 * NCH)
            for s, count in loads.values():
                eng.wait_ge(s, count)


def packed(widths, **arrays):
    cols, n = columns(widths)
    out = np.zeros((P, n), np.float32)
    for name, a in arrays.items():
        a = np.asarray(a, np.float32).reshape(a.shape[0], -1)
        out[:a.shape[0], cols[name]] = a
    return out


def by_rows(w):
    w = np.asarray(w)
    return w.reshape(-1, P, w.shape[1]).transpose(1, 0, 2)


def swapped(w):
    return np.asarray(w).reshape(D, -1, 2)[:, :, ::-1].reshape(D, D)


def head_rows(w):
    out = np.zeros((H, 32, D), np.float32)
    out[:, :DH] = np.asarray(w).reshape(H, DH, D)
    return by_rows(out.reshape(H * 32, D))


def per_feature(b):
    return np.asarray(b).reshape(2, P).T


def on_all(row):
    return np.broadcast_to(np.asarray(row).reshape(1, -1), (P, np.size(row)))


def constants():
    p = np.arange(P)
    selneg = np.zeros((P, H, P), np.float32)
    selneg[np.arange(H), np.arange(H), :] = -1.0
    selrest = np.zeros((P, G4, 4, 32), np.float32)
    for h in range(H):
        selrest[h, h // 4, h % 4, :] = -1.0
    selh = np.zeros((P, 4, 32), np.float32)
    for a in range(4):
        selh[p, a, 8 * a + p // 16] = 1.0 / DH
    mask8 = (p[:, None] // 16 == np.arange(8)[None]).astype(np.float32)
    padrow = np.where(p % 32 < SR, 0.0, -3e38).astype(np.float32)[:, None]
    token = np.arange(SP_) // 16 * 16 + 15 - np.arange(SP_) % 16
    valid = on_all((token < S).astype(np.float32))
    const = packed(CONST_PACK, ident=np.eye(P, dtype=np.float32), mask8=mask8, padrow=padrow,
                   iota8=on_all(np.arange(8, dtype=np.float32)), selh=selh,
                   valid=valid, iota=on_all(np.arange(T, dtype=np.float32)))
    inv = (np.float32(10000.0) ** (-np.arange(0, DH, 2, dtype=np.float32) / np.float32(DH))).astype(np.float32)
    ang = (np.arange(T, dtype=np.float32)[None, :] * inv[:, None]).astype(np.float32)
    d = p % DH
    sign = np.where(d % 2 == 0, -1.0, 1.0).astype(np.float32)
    rope = packed(ROPE_PACK, cos=np.cos(ang)[d // 2], sin=np.sin(ang)[d // 2] * sign[:, None])
    return const, rope, packed(SELECT_PACK, selneg=selneg, selrest=selrest)


def kernel(**inputs):
    import concourse.bacc as _bacc
    from concourse.bass_utils import run_bass_kernel_spmd as _run

    a = {k: np.asarray(v) for k, v in inputs.items()}
    zero = np.zeros(D, np.float32)

    def attention(wq, wk, wv, wo, bq, bk, bv, bo):
        return packed(ATTN_PACK, wq=by_rows(wq), wk=by_rows(wk), wv=by_rows(wv), wo=head_rows(wo), bq=per_feature(bq),
                      bk=per_feature(bk), bv=on_all(bv), bo=on_all(bo), wqs=by_rows(swapped(wq)), wks=by_rows(swapped(wk)))

    l0, l1, l2, l3 = ({k[9:]: v for k, v in a.items() if k.startswith(f"L{i}_xattn")} for i in range(4))
    f0, f1, f2, f3 = ({k[7:]: v for k, v in a.items() if k.startswith(f"L{i}_ffn")} for i in range(4))
    arrays = {"x": a["x"].reshape(B * T, D)}
    ctx = a["ctx_1024"]
    arrays["ctxt"] = by_rows(ctx.reshape(B * S, D).T).reshape(P, -1)
    rev = np.zeros((B, SP_, D), np.float32)
    rev[:, :S] = ctx
    rev = rev.reshape(B, U, 16, D)[:, :, ::-1].reshape(B * SP_, D)
    arrays["ctxr"] = by_rows(rev.T).reshape(P, -1)
    arrays["attn0"] = attention(l0["Wq"], l0["Wk"], l0["Wv"], l0["Wo"], l0["b_q"], l0["b_k"], l0["b_v"], l0["b_o"])
    arrays["attn1"] = attention(l1["wq_w"].T, l1["wk_w"].T, l1["wv_w"].T, l1["dense_w"].T,
                                l1["wq_b"], l1["wk_b"], l1["wv_b"], l1["dense_b"])
    arrays["attn2"] = attention(l2["Wq"], l2["Wk"], l2["Wv"], l2["Wo"], zero, zero, zero, zero)
    arrays["corr"] = packed(CORR_PACK, wq=by_rows(l3["Wq"]), wk=by_rows(l3["Wk"]), wv=by_rows(l3["Wv"]), wo=by_rows(l3["Wo"]),
                            bq=per_feature(l3["bq"]), bk=per_feature(l3["bk"]), bv=on_all(l3["bv"]), bo=on_all(l3["bo"]))
    arrays["ffn0"] = packed(FFN0_PACK, fc=by_rows(f0["w_fc"]), proj=by_rows(f0["w_proj"]), ut=f0["u"].T, v=f0["v"],
                            fbt=f0["fast_b"].T, gate=on_all(f0["gate"]))
    keys = np.zeros((2, PH, 32, PH, NKEY), np.float32)
    for h in range(PH):
        keys[:, h, :, h, :] = f1["keys"][h].transpose(1, 2, 0)
    arrays["ffn1"] = packed(FFN1_PACK, wq=by_rows(f1["w_queries"].T), keys=keys.reshape(2, P, 512).transpose(1, 0, 2),
                            wg=by_rows(f1["w_gate"].T), wu=by_rows(f1["w_up"].T), wd=by_rows(f1["w_down"].T))
    arrays["table"] = np.concatenate([f1["down_embed"], f1["up_embed"]], axis=1)
    gu = np.stack([np.concatenate([f2["w_gate"], f2["ws_gate"].reshape(2, P, D)]),
                   np.concatenate([f2["w_up"], f2["ws_up"].reshape(2, P, D)])], axis=1)
    down = np.concatenate([f2["w_down"].transpose(2, 0, 1), f2["ws_down"].T.reshape(2, P, D).transpose(1, 0, 2)], axis=1)
    arrays["ffn2"] = packed(FFN2_PACK, gate=by_rows(f2["gate_weight"].T), gu=by_rows(gu.reshape(-1, D).T), down=down)
    arrays["ffn3"] = packed(FFN3_PACK, gate=by_rows(f3["Wg"]), we=by_rows(f3["We"].transpose(1, 0, 2).reshape(D, -1)), be=f3["be"])
    arrays["const"], arrays["rope"], arrays["select"] = constants()

    nc = _bacc.Bacc("TRN2", target_bir_lowering=False, num_devices=1)
    ins, io = {}, {}
    for name, v in arrays.items():
        ins[f"in_{name}"] = np.ascontiguousarray(v)
        io[name] = nc.dram_tensor(f"in_{name}", v.shape, FP, kind="ExternalInput").ap()
    io["out"] = nc.dram_tensor("out", (B * T, D), FP, kind="ExternalOutput").ap()
    build(nc, io, STOP)
    r = _run(nc, [ins], core_ids=[0])
    return r.results[0]["out"].reshape(B, T, D)
```

```python
from contextlib import ExitStack

import concourse.bass as bass
import numpy as np
from concourse import mybir

FP, BF, U32 = mybir.dt.float32, mybir.dt.bfloat16, mybir.dt.uint32
ALU, ACT, AX = mybir.AluOpType, mybir.ActivationFunctionType, mybir.AxisListType

P = 128
STOP = None
B, T, D = 2, 1024, 256
S = 154
H, DH = 16, 16
KT = D // P
NCH, CH = 4, 512
TI = CH // P
SR = S - P
SP_ = 160
G4 = 4
EPS = 1e-5
HID0, RANK = 1024, 16
NKEY, TOPK, PH, NEXP1, INTER = 128, 8, 4, 4096, 512
E2, M2 = 8, 10
E3 = 8
U = SP_ // 16
EXT = T + SP_
TOPC = 6
RING, GRP = 20, 4
NG = PH * TOPK // GRP
Q_PARTS, K_PARTS = (0, 0, 0, 1, 1, 1, 2), (0, 1, 2, 0, 1, 2, 0)
NB = len(Q_PARTS)
MROW = NB * DH
SWAP = [lane ^ 1 for lane in range(32)]
MAX_UNITS = [(i, h, min(h + 6, H)) for i in range(TI) for h in range(0, H, 6)]
NU = len(MAX_UNITS)

STEPS = dict(kv=(1, 1, 2), attn=(0, 3, 3, 0, 1, 1, 2), ffn1=(1, 1, 1, 1, 1, 1, 2), ffn2=(1, (0, 1) * 5, 1, 2))

ATTN_PACK = dict(wq=KT * D, wk=KT * D, wv=KT * D, wo=KT * D, bq=2, bk=2, bv=D, bo=D)
CORR_PACK = ATTN_PACK
FFN0_PACK = dict(fc=8 * D, proj=2 * HID0, ut=HID0, v=D, fbt=RANK, gate=1)
FFN1_PACK = dict(wq=KT * D, keys=2 * 512, wg=KT * INTER, wu=KT * INTER, wd=4 * D)
FFN2_PACK = dict(gate=KT * E2, gu=KT * M2 * 2 * P, down=M2 * D)
FFN3_PACK = dict(gate=KT * E3, we=KT * E3 * D, be=D)
CONST_PACK = dict(ident=P, mask8=8, padrow=1, iota8=8, selh=4 * 32, valid=SP_)
LATE_PACK = dict(iota=T, ctxr=KT * B * SP_)
ROPE_PACK = dict(cos=T, sin=T)


def columns(pack):
    at, out = 0, {}
    for name, n in pack.items():
        out[name] = slice(at, at + n)
        at += n
    return out, at


def schedule():
    out = [("kv", 0, 0)] + [("attn", 0, c) for c in range(NCH)]
    out += [("tern", 0, 0)] + [("ffn0", 0, c) for c in range(NCH)]
    out += [("kv", 1, 0), ("attn", 1, 0), ("attn", 1, 1)]
    for c in range(2, NCH):
        out += [("ffn1", 1, c - 2), ("attn", 1, c)]
    out += [("ffn1", 1, NCH - 2), ("ffn1", 1, NCH - 1), ("kv", 2, 0)]
    for c in range(0, NCH, 2):
        out += [("attn", 2, c), ("attn", 2, c + 1), ("ffn2", 2, c), ("ffn2", 2, c + 1)]
    out.insert(-1, ("kv3", 3, 0))
    for b in range(B):
        out += [("q3", b, 2 * b), ("q3", b, 2 * b + 1), ("corr", b, 0)]
    out.append(("top", 0, 0))
    out += [("out3", b, 0) for b in range(B)]
    out += [("ffn3", 3, c) for c in range(NCH)]
    return out


def build(nc, io, stop=None):
    phases = schedule()[:stop]
    fronts = [n for n, (kind, _, _) in enumerate(phases) if kind in ("attn", "ffn0", "ffn1", "ffn2", "q3", "ffn3")]
    front_of = {n: f for f, n in enumerate(fronts)}

    def instance(n):
        return sum(p[0] == phases[n][0] for p in phases[:n])

    def next_front(n):
        f = sum(m <= n for m in fronts)
        if f >= len(fronts):
            return None
        m = fronts[f]
        kind, b, _ = phases[n]
        if phases[m][0] == "ffn3" and phases[m - 1][0] == "out3":
            return f if kind == "out3" and b == 1 else None
        return f if n == (fronts[f - 1] if f else 0) else None

    def stack_of(n):
        return n + 1 if n + 1 < len(phases) and phases[n + 1][0] == "attn" else None

    def stacks_before(f):
        return sum(phases[m][0] == "attn" for m in fronts[:f])

    ctx = ExitStack()
    with ctx:
        def sb(name, shape, dt=FP):
            return ctx.enter_context(nc.sbuf_tensor(name, shape, dt))

        def sem(name):
            return ctx.enter_context(nc.semaphore(name))

        x_sb = sb("x_sb", [P, NCH * TI, D])
        xa = sb("xa", [P, TI, D])
        xg = [sb(f"xg{i}", [P, TI, D]) for i in range(3)]
        xt = sb("xt", [P, KT, CH])
        stats = sb("stats", [P, TI, 6])
        mv = sb("mv", [P, TI, 2])
        vare, stdev, rstd = sb("vare", [P, TI]), sb("stdev", [P, TI]), sb("rstd", [P, TI])
        AC, AN = columns(ATTN_PACK)
        CC, CN = columns(CORR_PACK)
        F0, F0N = columns(FFN0_PACK)
        F1, F1N = columns(FFN1_PACK)
        F2, F2N = columns(FFN2_PACK)
        F3, F3N = columns(FFN3_PACK)
        KC, KN = columns(CONST_PACK)
        RN, (LC, LN) = columns(ROPE_PACK)[1], columns(LATE_PACK)
        const = sb("const", [P, KN])
        ctxt = sb("ctxt", [P, KT, B * S])
        wattn = sb("wattn", [P, max(AN, CN)])
        wf = sb("wf", [P, max(4096, F1N, F2N, F3N)])
        bufA = sb("bufA", [P, 8832])
        bufB = sb("bufB", [P, 10240])
        ringb = sb("ring", [P, RING * 2 * D])
        prob = [sb(f"prob{z}", [P, P]) for z in range(3)]
        rowid = [sb(f"rowid{z}", [P, P], U32) for z in range(3)]
        mt = sb("mt", [H, CH], BF)
        m4 = sb("m4", [P, TI, H])
        bqs = sb("bqs", [P, 2])
        psum = ctx.enter_context(nc.psum_tensor("psum", [P, 8, 512], FP))
        scrq = nc.dram_tensor("scr_queries", (3, D, CH), BF).ap()
        scrk = nc.dram_tensor("scr_keys", (3, D, B * SP_), BF).ap()
        scr1 = nc.dram_tensor("scr_corr", (4, P, T + 16), FP).ap()
        scr2 = nc.dram_tensor("scr_roll", (32, 2 * T), FP).ap()
        scrv = nc.dram_tensor("scr_v", (B, SP_, D), FP).ap()

        def bank(i):
            return psum[:, i, :]

        ident = const[:, KC["ident"]]
        mask8 = const[:, KC["mask8"]]
        padrow = const[:, KC["padrow"]]
        iota8 = const[:, KC["iota8"]]
        selh = const[:, KC["selh"]].rearrange("p (a m) -> p a m", a=4)
        valid = const[0:1, KC["valid"]]

        def w(name, kt=KT, where=wattn, cols=AC):
            return where[:, cols[name]].rearrange("p (k n) -> p k n", k=kt)

        def keys(b):
            at = b * H * SP_ // 2
            return bufB[:, at:at + H * SP_ // 2].bitcast(BF).rearrange("p (h k) -> p h k", h=H)

        VA_AT = H * SP_
        QS_AT = VA_AT + 4 * 512
        QP_AT = QS_AT + H * CH // 2
        queries = bufB[:, QS_AT:QP_AT].bitcast(BF).rearrange("p (h n) -> p h n", h=H)
        qparts = bufB[:, QP_AT:QP_AT + 3 * CH].bitcast(BF).rearrange("p (z g n) -> p z g n", z=3, g=2)

        def vmain(b):
            return bufB[:, VA_AT + b * 512:VA_AT + (b + 1) * 512]

        def vrest(b):
            at = VA_AT + 1024 + b * 512
            return bufB[:, at:at + 512].rearrange("p (g n) -> p g n", g=G4)

        ld_const, ld_x, ld_ctx, ld_rope = sem("ld_const"), sem("ld_x"), sem("ld_ctx"), sem("ld_rope")
        ld_attn = sem("ld_attn")
        ld_f0, ld_f1, ld_f2, ld_f3 = sem("ld_f0"), sem("ld_f1"), sem("ld_f2"), sem("ld_f3")
        ends = {e: sem(f"end_{e}") for e in ("pe", "act", "dve")}
        ld_late = sem("ld_late")
        fr_var, fr_std, fr_xn, fr_tp, fr_ev = (sem(s) for s in ("fr_var", "fr_std", "fr_xn", "fr_tp", "fr_ev"))
        kv_k, kv_kt, kv_v, kv_z, kv_m, kv_p, kv_wr, kv_rd = (
            sem(s) for s in ("kv_k", "kv_kt", "kv_v", "kv_z", "kv_m", "kv_p", "kv_wr", "kv_rd"))
        sk_q, sk_f, sk_p, sk_wr, sk_rd = (sem(s) for s in ("sk_q", "sk_f", "sk_p", "sk_wr", "sk_rd"))
        at_p1, at_mx, at_mt, at_mts, at_mr, at_s2, at_ex, at_pv = (
            sem(s) for s in ("at_p1", "at_mx", "at_mt", "at_mts", "at_mr", "at_s2", "at_ex", "at_pv"))
        at_ou, at_tt, at_on, at_tb, at_ot, at_wo, at_bo = (
            sem(s) for s in ("at_ou", "at_tt", "at_on", "at_tb", "at_ot", "at_wo", "at_bo"))
        tn_w, tn_z, tn_zs, tn_u, tn_nat, tn_tp, tn_ev = (
            sem(s) for s in ("tn_w", "tn_z", "tn_zs", "tn_u", "tn_nat", "tn_tp", "tn_ev"))
        f0_h, f0_r, f0_sq, f0_y, f0_x = (sem(s) for s in ("f0_h", "f0_r", "f0_sq", "f0_y", "f0_x"))
        f1_q, f1_qt, f1_sim, f1_tk, f1_g, f1_sg, f1_hm, f1_y, f1_x = (
            sem(s) for s in ("f1_q", "f1_qt", "f1_sim", "f1_tk", "f1_g", "f1_sg", "f1_hm", "f1_y", "f1_x"))
        f1_sc, f1_se, f1_idx, f1_dot, f1_sd, f1_acc = (
            sem(s) for s in ("f1_sc", "f1_se", "f1_idx", "f1_dot", "f1_sd", "f1_acc"))
        gathered = [sem(f"gathered{i}") for i in range(RING // GRP)]
        f2_lg, f2_sc, f2_g, f2_sg, f2_hm, f2_y, f2_x = (
            sem(s) for s in ("f2_lg", "f2_sc", "f2_g", "f2_sg", "f2_hm", "f2_y", "f2_x"))
        f3_lg, f3_ls, f3_ex, f3_gt, f3_gp, f3_gs, f3_b, f3_y, f3_x = (
            sem(s) for s in ("f3_lg", "f3_ls", "f3_ex", "f3_gt", "f3_gp", "f3_gs", "f3_b", "f3_y", "f3_x"))
        k3_k, k3_kt, k3_v, k3_vs, k3_wr, k3_rd, k3_st = (
            sem(s) for s in ("k3_k", "k3_kt", "k3_v", "k3_vs", "k3_wr", "k3_rd", "k3_st"))
        q3_q, q3_s = sem("q3_q"), sem("q3_s")
        co_c, co_s, co_wr, co_rd, co_m = (sem(s) for s in ("co_c", "co_s", "co_wr", "co_rd", "co_m"))
        tp_c, tp_n, tp_e, tp_r, tp_wr, tp_rd = (sem(s) for s in ("tp_c", "tp_n", "tp_e", "tp_r", "tp_wr", "tp_rd"))
        o3_o, o3_s, o3_y, o3_x, o3_bo = (sem(s) for s in ("o3_o", "o3_s", "o3_y", "o3_x", "o3_bo"))
        own_dve, own_act, own_pool = sem("own_dve"), sem("own_act"), sem("own_pool")
        stored, end_pool = sem("stored"), sem("end_pool")

        block = ctx.enter_context(nc.Block())

        def normed(f):
            kind, _, c = phases[fronts[f]]
            return xg[c % 3] if kind == "ffn1" else xa

        def enter(eng, me, n):
            if n:
                for e, s in ends.items():
                    if e != me:
                        eng.wait_ge(s, n)

        def leave(eng, me):
            eng.drain().then_inc(ends[me], 1)

        class Gather:

            def __init__(self):
                self.named = self.taken = 0

            def take(self, count):
                first = self.taken
                self.taken = min(self.named, first + count)
                return range(first, self.taken)

            def rest(self, c):
                return self.take(max(0, (c + 1) * TI * NG - self.taken))

        class Own:

            def __init__(self, eng, s):
                self.eng, self.s, self.n = eng, s, 0

            def mark(self, ins):
                self.n += 1
                ins.then_inc(self.s, 1)

            def wait(self):
                self.eng.wait_ge(self.s, self.n)

            def link(self, ins):
                self.mark(ins)
                self.wait()

        def A(at, n):
            return bufA[:, at:at + n]

        probs = [A(2560 * i, 2560).rearrange("p (h n) -> p h n", h=5) for i in range(2)]
        oun = A(5120, 2048).rearrange("p (g n) -> p g n", g=G4)
        oden = A(7168, TI * H).rearrange("p (i h) -> p i h", i=TI)
        onorm = A(0, 1024).rearrange("p (i n) -> p i n", i=TI)
        ot = A(1024, 1024).rearrange("p (g n) -> p g n", g=2)
        qf = A(7296, 1024).rearrange("p (g n) -> p g n", g=2)
        qsw = A(8320, 512)
        kts = A(0, 2 * B * SP_).rearrange("p (g b s) -> p g b s", g=2, b=B)
        ksw = A(1024, 2 * B * SP_).rearrange("p (g b s) -> p g b s", g=2, b=B)
        kparts = A(2048, 3 * B * SP_).bitcast(BF).rearrange("p (z g b s) -> p z g b s", z=3, g=2, b=B)
        rope = sb("rope", [P, max(RN, LN)])
        late = rope
        iota = late[:, LC["iota"]]
        ctxr = late[:, LC["ctxr"]].rearrange("p (k n) -> p k n", k=KT)
        fc_t = wf[:, 0:2048].rearrange("p (k n) -> p k n", k=KT)
        proj_t = wf[:, 2048:4096].rearrange("p (m n) -> p m n", m=8)
        raw0 = ringb[:, 0:F0N]
        fcnat = raw0[:, F0["fc"]].rearrange("p (m n) -> p m n", m=8)
        projnat = raw0[:, F0["proj"]].rearrange("p (o n) -> p o n", o=2)
        TN = 0
        utg = raw0[:, F0["ut"]]
        lowv = A(TN, D)
        absum, hi_th, lo_th, sclip = A(TN + D, 10), A(TN + D + 10, 10), A(TN + D + 20, 10), A(TN + D + 30, 10)
        tplus, tminus = A(TN + D + 64, 1024), A(TN + D + 64 + 1024, 1024)
        hid0r = A(0, 4096).rearrange("p (m n) -> p m n", m=8)
        hid0 = A(4096, 4096).rearrange("p (m n) -> p m n", m=8)

        def f0(name):
            return raw0[:, F0[name]]

        def w1(name, kt=KT):
            return w(name, kt, wf, F1)

        q1 = A(0, 1024).rearrange("p (g n) -> p g n", g=2)
        sg1 = A(1024, 1024).rearrange("p (g n) -> p g n", g=2)
        hm1 = A(2048, 2048).rearrange("p (m n) -> p m n", m=4)
        topv = A(4096, 256).rearrange("p (a r k) -> p a r k", a=2, k=TOPK)
        topi = A(4352, 256).bitcast(U32).rearrange("p (a r k) -> p a r k", a=2, k=TOPK)
        topf = A(4608, 256).rearrange("p (a r k) -> p a r k", a=2, k=TOPK)
        sums = A(4864, 1024).rearrange("p (r i j) -> p r i j", r=16, i=TOPK)
        best = A(6912, 128).rearrange("p (r k) -> p r k", r=16)
        pos = A(0, 128).bitcast(U32)
        pside = [A(128 + 128 * z, 128).bitcast(U32) for z in range(2)]
        psidef = [A(384 + 128 * z, 128) for z in range(2)]
        pick = [A(640 + 128 * z, 128) for z in range(2)]
        rowf = A(896, 128)
        eq = [A(4864 + 1024 * z, 1024).rearrange("p (r k j) -> p r k j", r=16, k=TOPK) for z in range(2)]
        ex1 = A(7040, 128)
        esum, erec = A(7168, 16), A(7184, 16)
        dots, sdot, ew = (sb(s, [P, 4, GRP]) for s in ("dots", "sdot", "ew"))
        ring = ringb[:, :].rearrange("p (s n) -> p s n", s=RING)

        def w2(name, kt=KT):
            return w(name, kt, wf, F2)

        sg2 = A(0, 1024).rearrange("p (g n) -> p g n", g=2)
        hm2 = A(1024, 5120).rearrange("p (m n) -> p m n", m=M2)
        sc2 = A(6144, 32)
        tv2 = A(6176, 32).rearrange("p (i k) -> p i k", i=TI)
        ti2 = A(6208, 32).bitcast(U32).rearrange("p (i k) -> p i k", i=TI)
        tf2 = A(6240, 32).rearrange("p (i k) -> p i k", i=TI)
        s2 = [A(6272 + 8 * z, 4) for z in range(4)]
        comb2 = [A(6304 + 32 * z, 32).rearrange("p (i e) -> p i e", i=TI) for z in range(3)]

        def w3(name, kt=KT):
            return w(name, kt, wf, F3)

        ex3 = A(0, 32)
        lg3 = A(32, 32).rearrange("p (i e) -> p i e", i=TI)
        mx3 = A(64, 4)
        tv3 = A(96, 32).rearrange("p (i k) -> p i k", i=TI)
        ti3 = A(128, 32).bitcast(U32).rearrange("p (i k) -> p i k", i=TI)
        tf3 = A(160, 32).rearrange("p (i k) -> p i k", i=TI)
        pr3 = A(192, 32)
        s3 = [A(224 + 8 * z, 4) for z in range(4)]
        comb3 = [A(256 + 32 * z, 32).rearrange("p (i e) -> p i e", i=TI) for z in range(3)]
        gate3 = A(256, 32)
        gatet = A(512, 512)

        k3t = A(0, 2 * B * SP_).rearrange("p (g n) -> p g n", g=2)
        v3m, v3r = (ringb[:, at:at + 512].rearrange("p (b n) -> p b n", b=B) for at in (7168, 7680))
        v3s = ringb[:, 8192:8192 + 4 * U * 16].rearrange("p (a u d) -> p a u d", a=4, u=U)
        qx = A(0, 2 * EXT).rearrange("p (g n) -> p g n", g=2)
        c1 = [ringb[:, 1040 * g:1040 * (g + 1)] for g in range(2)]
        c2 = [ringb[:, 2080 + T * a:2080 + T * (a + 1)] for a in range(4)]
        cor = A(6528, T)
        rolls = A(0, 4 * (T + SP_))
        ot3 = A(4736, 2048).rearrange("p (g n) -> p g n", g=2)
        topw, topj, topjf, rsum3 = A(7552, 8), A(7560, 8).bitcast(U32), A(7568, 8), A(7576, 8)
        topm = A(7584, 8)
        rollw, rollt = ringb[:, 0:T], [ringb[:, (1 + z) * T:(2 + z) * T] for z in range(2)]

        def kst(b, g):
            return bufB[:, (2 * b + g) * U * P:(2 * b + g + 1) * U * P].rearrange("p (u n) -> p u n", u=U)

        def vst(b, g):
            at = 4 * U * P + (2 * b + g) * U * P
            return bufB[:, at:at + U * P].rearrange("p (u n) -> p u n", u=U)

        def roll(a):
            return rolls[:, a * (T + SP_):(a + 1) * (T + SP_)]


        @block.tensor
        def _(eng):
            mm = eng.matmul

            def front(f):
                if f is None:
                    return
                eng.wait_ge(fr_xn, TI * (f + 1))
                if f:
                    eng.wait_ge(fr_ev, KT * f)
                if stacks_before(f):
                    eng.wait_ge(sk_p, stacks_before(f))
                for kt in range(KT):
                    for i in range(TI):
                        ins = eng.transpose(psum[:, 6 + kt, i * P:(i + 1) * P], normed(f)[:, i, kt * P:(kt + 1) * P], ident)
                    ins.then_inc(fr_tp, 1)

            def stack(n):
                if n is None:
                    return
                f = front_of[n]
                eng.wait_ge(fr_ev, KT * (f + 1))
                for g in range(2):
                    for kt in range(KT):
                        ins = mm(bank(6 + g), w("wq")[:, kt, g * P:(g + 1) * P], xt[:, kt, :], start=kt == 0, stop=kt == KT - 1)
                ins.then_inc(sk_q, 1)

            def kv(n, layer):
                enter(eng, "pe", n)
                eng.wait_ge(ld_const, 16)
                eng.wait_ge(ld_ctx, 16)
                eng.wait_ge(ld_attn, 16 * (layer + 1))
                for g in range(2):
                    for kt in range(KT):
                        ins = mm(psum[:, g, 0:B * S], w("wk")[:, kt, g * P:(g + 1) * P], ctxt[:, kt, :],
                                 start=kt == 0, stop=kt == KT - 1)
                ins.then_inc(kv_k, 1)
                bias = wattn[0:1, AC["bv"]]
                for b in range(B):
                    o = psum[:, 4 + b, 0:D]
                    for kt in range(KT):
                        mm(o, ctxt[:, kt, b * S:b * S + P], w("wv")[:, kt, :], start=kt == 0, stop=False)
                    mm(o, valid[:, 0:P], bias, start=False, stop=True)
                    for j in range(4):
                        o = psum[32 * j:32 * j + SR, 4 + b, D:2 * D]
                        for kt in range(KT):
                            mm(o, ctxt[:, kt, b * S + P:(b + 1) * S], w("wv")[:, kt, :], start=kt == 0, stop=False)
                        ins = mm(o, valid[:, 0:SR], bias, start=False, stop=True)
                ins.then_inc(kv_v, 1)
                if n == 0:
                    front(0)
                stack(stack_of(n))

            def attn(n, layer, c):
                k, b = instance(n), c // 2
                enter(eng, "pe", n)
                eng.wait_ge(kv_rd, 16 * B * NB * (layer + 1))
                eng.wait_ge(sk_rd, 16 * NB * (k + 1))
                for u, (i, h0, h1) in enumerate(MAX_UNITS):
                    pair = 2 * (u % 3)
                    if u >= 3:
                        eng.wait_ge(at_mx, NU * k + u - 2)
                    for h in range(h0, h1):
                        z, at = (h - h0) // 3, (h - h0) % 3 * S
                        ins = mm(psum[:, pair + z, at:at + S], queries[0:MROW, h, i * P:(i + 1) * P], keys(b)[0:MROW, h, 0:S],
                                 start=True, stop=True)
                    ins.then_inc(at_p1, 1)
                eng.wait_ge(at_mx, NU * (k + 1))
                for i in range(TI):
                    ins = eng.transpose(psum[0:H, 0, i * P:(i + 1) * P], m4[:, i, :], ident)
                ins.then_inc(at_mt, 1)
                eng.wait_ge(at_mts, k + 1)
                eng.wait_ge(at_mr, 16 * (k + 1))

                def weigh(G):
                    eng.wait_ge(at_ex, 12 * k + 3 * G + 3)
                    if G:
                        eng.wait_ge(at_ou, 4 * k + G)
                    p = probs[G % 2]
                    mm(bank(5), vrest(b)[:, G, :], p[:, 4, :], start=True, stop=False, skip_group_check=True)
                    for j in range(4):
                        h = 4 * G + j
                        ins = mm(psum[32 * j:32 * j + 32, 5, :], vmain(b)[:, h * 32:h * 32 + 32], p[:, j, :],
                                 start=False, stop=True, skip_group_check=True)
                    ins.then_inc(at_pv, 1)

                for G in range(G4):
                    for a in range(2):
                        if G:
                            eng.wait_ge(at_ex, 12 * k + 3 * (G - 1) + a + 1)
                        for z in range(2):
                            ins = mm(bank(2 * a + z), keys(b)[0:MROW + 1, 4 * G + 2 * a + z, 0:P],
                                     queries[0:MROW + 1, 4 * G + 2 * a + z, :], start=True, stop=True)
                        ins.then_inc(at_s2, 1)
                    if G:
                        eng.wait_ge(at_ex, 12 * k + 3 * G)
                    for j in range(4):
                        ins = mm(psum[32 * j:32 * j + 32, 4, :], keys(b)[0:MROW + 1, 4 * G + j, P:SP_],
                                 queries[0:MROW + 1, 4 * G + j, :], start=True, stop=True, skip_group_check=True)
                    ins.then_inc(at_s2, 1)
                    if G:
                        weigh(G - 1)
                    if G == 0:
                        front(next_front(n))
                    if G == 1:
                        stack(stack_of(n))
                weigh(G4 - 1)
                eng.wait_ge(at_ou, 4 * (k + 1))
                for i in range(TI):
                    for G in range(G4):
                        ins = eng.transpose(psum[:, i, G * P:(G + 1) * P], oun[:, G, i * P:(i + 1) * P], ident)
                    ins.then_inc(at_tt, 1)
                for i in range(TI):
                    eng.wait_ge(at_on, 4 * k + i + 1)
                    for g in range(2):
                        ins = eng.transpose(psum[:, 4 + g, i * P:(i + 1) * P], onorm[:, i, g * P:(g + 1) * P], ident)
                ins.then_inc(at_tb, 1)
                eng.wait_ge(at_ot, 2 * (k + 1))
                for i in range(TI):
                    for g in range(2):
                        ins = mm(psum[:, i, 0:D], ot[:, g, i * P:(i + 1) * P], w("wo")[:, g, :],
                                 start=g == 0, stop=g == 1 and layer != 1)
                    if layer == 1:
                        ins = mm(psum[:, i, 0:D], valid[:, 0:P], wattn[0:1, AC["bo"]], start=False, stop=True)
                    ins.then_inc(at_wo, 1)

            def tern(n):
                enter(eng, "pe", n)
                eng.wait_ge(ld_f0, 16)
                eng.wait_ge(tn_w, 1)
                mm(psum[0:RANK, 0, 0:D], f0("fbt")[0:RANK, :], f0("v")[0:RANK, :], start=True, stop=True).then_inc(tn_z, 1)
                eng.wait_ge(tn_zs, 1)
                for m in range(8):
                    if m >= 2:
                        eng.wait_ge(tn_nat, m - 1)
                    mm(psum[:, 1 + m % 2, 0:D], utg[0:RANK, m * P:(m + 1) * P], lowv[0:RANK, :],
                       start=True, stop=True).then_inc(tn_u, 1)
                eng.wait_ge(tn_nat, 10)
                for t in range(8):
                    if t >= 2:
                        eng.wait_ge(tn_ev, t - 1)
                    for z in range(4):
                        if t < 4:
                            kt, m = t // 2, 4 * (t % 2) + z
                            src = fcnat[:, m, kt * P:(kt + 1) * P]
                        else:
                            mo = 4 * (t - 4) + z
                            m, o = mo // 2, mo % 2
                            src = projnat[:, o, m * P:(m + 1) * P]
                        ins = eng.transpose(psum[:, 4 + t % 2, z * P:(z + 1) * P], src, ident)
                    ins.then_inc(tn_tp, 1)

            def ffn0(n, c):
                k, x = instance(n), xt
                enter(eng, "pe", n)
                eng.wait_ge(fr_ev, KT * (front_of[n] + 1))
                for m in range(8):
                    if m >= 4:
                        eng.wait_ge(f0_r, 8 * k + m - 3)
                    for kt in range(KT):
                        ins = mm(bank(m % 4), fc_t[:, kt, m * P:(m + 1) * P], x[:, kt, :], start=kt == 0, stop=kt == KT - 1)
                    ins.then_inc(f0_h, 1)
                front(next_front(n))
                eng.wait_ge(f0_sq, 8 * k + 8)
                for i in range(TI):
                    if i >= 2:
                        eng.wait_ge(f0_x, 4 * k + i - 1)
                    for m in range(8):
                        ins = mm(psum[:, 4 + i % 2, 0:D], hid0[:, m, i * P:(i + 1) * P], proj_t[:, m, :], start=m == 0, stop=m == 7)
                    ins.then_inc(f0_y, 1)

            def ffn1(n, c):
                k, x = instance(n), xt
                enter(eng, "pe", n)
                eng.wait_ge(ld_f1, 16)
                eng.wait_ge(fr_ev, KT * (front_of[n] + 1))
                for p in range(2):
                    for kt in range(KT):
                        ins = mm(bank(p), w1("wq")[:, kt, p * P:(p + 1) * P], x[:, kt, :], start=kt == 0, stop=kt == KT - 1)
                    ins.then_inc(f1_q, 1)
                eng.wait_ge(f1_qt, 2 * k + 2)

                def similarities(i):
                    if i >= 2:
                        eng.wait_ge(f1_tk, 4 * k + i - 1)
                    for p in range(2):
                        ins = mm(bank(2 * (i % 2) + p), q1[:, p, i * P:(i + 1) * P], w1("keys")[:, p, :], start=True, stop=True)
                    ins.then_inc(f1_sim, 1)

                similarities(0)
                similarities(1)
                for m in range(4):
                    if m:
                        eng.wait_ge(f1_hm, 4 * k + m)
                    for r, name in enumerate(("wg", "wu")):
                        for kt in range(KT):
                            ins = mm(bank(4 + r), w1(name)[:, kt, m * P:(m + 1) * P], x[:, kt, :], start=kt == 0, stop=kt == KT - 1)
                    ins.then_inc(f1_g, 1)
                    if m < 2:
                        similarities(m + 2)
                front(next_front(n))
                stack(stack_of(n))
                eng.wait_ge(f1_tk, 4 * k + 4)
                eng.wait_ge(f1_hm, 4 * k + 4)
                for i in range(TI):
                    for m in range(4):
                        ins = mm(psum[:, i, 0:D], hm1[:, m, i * P:(i + 1) * P], w1("wd", 4)[:, m, :], start=m == 0, stop=m == 3)
                    ins.then_inc(f1_y, 1)

            def ffn2(n, c):
                k, x = instance(n), xt
                enter(eng, "pe", n)
                eng.wait_ge(ld_f2, 16)
                eng.wait_ge(fr_ev, KT * (front_of[n] + 1))
                for i in range(TI):
                    for kt in range(KT):
                        ins = mm(psum[:, 5, i * E2:(i + 1) * E2], x[:, kt, i * P:(i + 1) * P], w2("gate")[:, kt, :],
                                 start=kt == 0, stop=kt == KT - 1)
                ins.then_inc(f2_lg, 1)
                gu = w2("gu").rearrange("p k (m r n) -> p k m r n", m=M2, r=2)
                for m in range(M2):
                    if m >= 2:
                        eng.wait_ge(f2_hm, M2 * k + m - 1)
                    for r in range(2):
                        for kt in range(KT):
                            ins = mm(bank(2 * (m % 2) + r), gu[:, kt, m, r, :], x[:, kt, :], start=kt == 0, stop=kt == KT - 1)
                    ins.then_inc(f2_g, 1)
                front(next_front(n))
                stack(stack_of(n))
                eng.wait_ge(f2_hm, M2 * (k + 1))
                down = w2("down", M2)
                for y in range(TI * 9):
                    i, e = y // 9, y % 9
                    if y >= 5:
                        eng.wait_ge(f2_x, TI * 9 * k + y - 4)
                    ms = (8, 9) if e == 8 else (e,)
                    for m in ms:
                        ins = mm(psum[:, y % 5, 0:D], hm2[:, m, i * P:(i + 1) * P], down[:, m, :], start=m == ms[0], stop=m == ms[-1])
                    ins.then_inc(f2_y, 1)

            def ffn3(n, c):
                k, x = instance(n), xt
                enter(eng, "pe", n)
                eng.wait_ge(ld_f3, 16)
                eng.wait_ge(fr_ev, KT * (front_of[n] + 1))
                for i in range(TI):
                    for kt in range(KT):
                        ins = mm(psum[:, 5, i * E3:(i + 1) * E3], x[:, kt, i * P:(i + 1) * P], w3("gate")[:, kt, :],
                                 start=kt == 0, stop=kt == KT - 1)
                ins.then_inc(f3_lg, 1)
                for y in range(TI * 4):
                    i, e = y // 4, y % 4
                    if y >= 4:
                        eng.wait_ge(f3_x, TI * 4 * k + y - 3)
                    for kt in range(KT):
                        ins = mm(bank(y % 4), x[:, kt, i * P:(i + 1) * P], w3("we")[:, kt, e * 512:(e + 1) * 512],
                                 start=kt == 0, stop=kt == KT - 1)
                    ins.then_inc(f3_y, 1)
                    if y == 3:
                        eng.wait_ge(f3_gt, k + 1)
                        for t in range(TI):
                            ins = eng.transpose(psum[0:E3, 4, t * P:(t + 1) * P], gate3[:, t * E3:(t + 1) * E3], ident)
                        ins.then_inc(f3_gp, 1)
                front(next_front(n))
                eng.wait_ge(f3_gs, k + 1)
                for i in range(TI):
                    ins = mm(psum[:, 4 + i // 2, (i % 2) * D:(i % 2 + 1) * D], gatet[0:E3, i * P:(i + 1) * P],
                             wf[0:E3, F3["be"]], start=True, stop=True)
                ins.then_inc(f3_b, 1)

            def kv3(n):
                enter(eng, "pe", n)
                eng.wait_ge(ld_attn, 16 * 4)
                eng.wait_ge(ld_late, 16)
                for g in range(2):
                    for kt in range(KT):
                        ins = mm(psum[:, g, 0:B * S], w("wk", KT, wattn, CC)[:, kt, g * P:(g + 1) * P], ctxt[:, kt, :],
                                 start=kt == 0, stop=kt == KT - 1)
                ins.then_inc(k3_k, 1)
                for b in range(B):
                    for r, (a, z) in enumerate(((0, P), (P, SP_))):
                        o = psum[0:z - a, 2 + b, r * D:(r + 1) * D]
                        for kt in range(KT):
                            mm(o, ctxr[:, kt, b * SP_ + a:b * SP_ + z], w("wv", KT, wattn, CC)[:, kt, :], start=kt == 0, stop=False)
                        ins = mm(o, valid[:, a:z], wattn[0:1, CC["bv"]], start=False, stop=True)
                ins.then_inc(k3_v, 1)

            def q3(n, c):
                k, x = instance(n), xt
                enter(eng, "pe", n)
                eng.wait_ge(fr_ev, KT * (front_of[n] + 1))
                for g in range(2):
                    for kt in range(KT):
                        ins = mm(bank(g), w("wq", KT, wattn, CC)[:, kt, g * P:(g + 1) * P], x[:, kt, :], start=kt == 0, stop=kt == KT - 1)
                ins.then_inc(q3_q, 1)
                front(next_front(n))

            def corr(n, b):
                enter(eng, "pe", n)
                for g in range(2):
                    for N in range(2):
                        for u in range(U):
                            ins = mm(bank(2 * g + N), kst(b, g)[:, u, :], qx[:, g, 16 * u + N * 512:16 * u + N * 512 + 512],
                                     start=u == 0, stop=u == U - 1)
                    ins.then_inc(co_c, 1)

            def top(n):
                enter(eng, "pe", n)
                eng.wait_ge(co_rd, 32 * B)
                for a in range(2 * B):
                    for N in range(2):
                        ins = mm(psum[0:32, 4 + N, :], selh[:, a, :], c2[a][:, N * 512:(N + 1) * 512], start=a == 0, stop=a == 3,
                                 skip_group_check=True)
                ins.then_inc(co_m, 1)

            def out3(n, b):
                enter(eng, "pe", n)
                eng.wait_ge(tp_rd, 16 * 4)
                for g in range(2):
                    for N in range(2):
                        for u in range(U):
                            at = SP_ - 16 * u + N * 512
                            ins = mm(bank(2 * g + N), vst(b, g)[:, u, :], roll(2 * b + g)[:, at:at + 512],
                                     start=u == 0, stop=u == U - 1)
                        ins.then_inc(o3_o, 1)
                front(next_front(n))
                eng.wait_ge(o3_s, 4 * b + 4)
                for i in range(8):
                    if i >= 2:
                        eng.wait_ge(o3_x, 8 * b + i - 1)
                    for g in range(2):
                        ins = mm(psum[:, 4 + i % 2, 0:D], ot3[:, g, i * P:(i + 1) * P], w("wo", KT, wattn, CC)[:, g, :],
                                 start=g == 0, stop=g == 1)
                    ins.then_inc(o3_y, 1)

            for n, (kind, layer, c) in enumerate(phases):
                {"kv": lambda: kv(n, layer), "attn": lambda: attn(n, layer, c), "tern": lambda: tern(n),
                 "ffn0": lambda: ffn0(n, c), "ffn1": lambda: ffn1(n, c), "ffn2": lambda: ffn2(n, c), "ffn3": lambda: ffn3(n, c),
                 "kv3": lambda: kv3(n), "q3": lambda: q3(n, c), "corr": lambda: corr(n, layer), "top": lambda: top(n),
                 "out3": lambda: out3(n, layer)}[kind]()
                leave(eng, "pe")

        @block.scalar
        def _(eng):
            act = eng.activation
            own = Own(eng, own_act)

            def front(f):
                if f is None:
                    return
                for kt in range(KT):
                    eng.wait_ge(fr_tp, KT * f + kt + 1)
                    act(xt[:, kt, :], bank(6 + kt), ACT.Copy).then_inc(fr_ev, 1)

            def stack(n):
                if n is None or phases[n][1] == 2:
                    return
                eng.wait_ge(sk_q, instance(n) + 1)
                for g in range(2):
                    act(qf[:, g, :], bank(6 + g), ACT.Identity, bias=bqs[:, g:g + 1], scale=0.25).then_inc(sk_f, 1)
                    act(qparts[:, 0, g, :], bank(6 + g), ACT.Identity, bias=bqs[:, g:g + 1], scale=0.25).then_inc(sk_f, 1)

            gather = Gather()

            def gather_steps(groups):
                for g in groups:
                    eng.wait_ge(f1_dot, g + 1)
                    if g >= 4:
                        eng.wait_ge(f1_acc, g - 3)
                    act(sdot[:, g % 4, :], dots[:, g % 4, :], ACT.Silu).then_inc(f1_sd, 1)

            def deviation(f):
                if f is None:
                    return
                kind, layer, c = phases[fronts[f]]
                if (kind, layer) == ("attn", 2):
                    gather_steps(gather.rest(c))
                if kind == "ffn1" and c >= 3:
                    gather_steps(gather.rest(c - 3))
                eng.wait_ge(fr_var, f + 1)
                act(stdev[:, :], vare[:, :], ACT.Sqrt).then_inc(fr_std, 1)

            def kv(n, layer):
                enter(eng, "act", n)
                if n == 0:
                    deviation(0)
                eng.wait_ge(kv_k, layer + 1)
                for g in range(2):
                    act(kts[:, g, :, 0:S], psum[:, g, 0:B * S].rearrange("p (b s) -> p b s", b=B), ACT.Identity,
                        bias=wattn[:, AC["bk"].start + g:AC["bk"].start + g + 1]).then_inc(kv_kt, 1)
                if layer < 2:
                    own.link(act(bqs[:, :], wattn[:, AC["bq"]], ACT.Copy, scale=0.25))
                gather_steps(gather.take(STEPS["kv"][0]))
                if n == 0:
                    front(0)
                stack(stack_of(n))
                gather_steps(gather.take(STEPS["kv"][1]))

            def attn(n, layer, c):
                k = instance(n)
                enter(eng, "act", n)
                gather_steps(gather.take(STEPS["attn"][0]))
                eng.wait_ge(at_mt, k + 1)
                act(mt[0:H, :], psum[0:H, 0, :], ACT.Copy).then_inc(at_mts, 1)
                deviation(next_front(n))
                before = gather.take(STEPS["attn"][1])

                def unload(G):
                    eng.wait_ge(at_pv, 4 * k + G + 1)
                    act(oun[:, G, :], bank(5), ACT.Copy).then_inc(at_ou, 1)

                for G in range(G4):
                    p = probs[G % 2]
                    if G >= 2:
                        eng.wait_ge(at_pv, 4 * k + G - 1)
                    for a in range(2):
                        eng.wait_ge(at_s2, 12 * k + 3 * G + a + 1)
                        act(p[:, 2 * a:2 * a + 2, :], psum[:, 2 * a:2 * a + 2, :], ACT.Exp).then_inc(at_ex, 1)
                    eng.wait_ge(at_s2, 12 * k + 3 * G + 3)
                    act(p[:, 4, :], bank(4), ACT.Exp, bias=padrow).then_inc(at_ex, 1)
                    if G:
                        unload(G - 1)
                    if G == 0:
                        front(next_front(n))
                        gather_steps(before[0:1])
                    if G == 1:
                        gather_steps(before[1:])
                        stack(stack_of(n))
                        after_ = gather.take(STEPS["attn"][2])
                    if G == 2:
                        gather_steps(after_[0:1])
                unload(G4 - 1)
                gather_steps(after_[1:])
                gather_steps(gather.take(STEPS["attn"][3]))
                eng.wait_ge(at_tb, k + 1)
                for g in range(2):
                    act(ot[:, g, :], bank(4 + g), ACT.Copy).then_inc(at_ot, 1)
                gather_steps(gather.take(STEPS["attn"][4]))
                gather_steps(gather.take(STEPS["attn"][5]))

            def tern(n):
                enter(eng, "act", n)
                eng.wait_ge(tn_z, 1)
                act(lowv[0:RANK, :], psum[0:RANK, 0, 0:D], ACT.Copy).then_inc(tn_zs, 1)
                for t in range(8):
                    eng.wait_ge(tn_tp, t + 1)
                    if t < 4:
                        kt, m = t // 2, 4 * (t % 2)
                        dst = fc_t[:, kt, m * P:(m + 4) * P]
                    else:
                        m = 2 * (t - 4)
                        dst = proj_t[:, m:m + 2, :].rearrange("p m n -> p (m n)")
                    act(dst, bank(4 + t % 2), ACT.Copy).then_inc(tn_ev, 1)

            def ffn0(n, c):
                k = instance(n)
                enter(eng, "act", n)
                deviation(next_front(n))
                for m in range(8):
                    eng.wait_ge(f0_h, 8 * k + m + 1)
                    act(hid0r[:, m, :], bank(m % 4), ACT.Relu).then_inc(f0_r, 1)
                front(next_front(n))

            def ffn1(n, c):
                k = instance(n)
                enter(eng, "act", n)
                deviation(next_front(n))
                for p in range(2):
                    eng.wait_ge(f1_q, 2 * k + p + 1)
                    act(q1[:, p, :], bank(p), ACT.Copy).then_inc(f1_qt, 1)
                gather_steps(gather.take(STEPS["ffn1"][0]))
                for m in range(4):
                    eng.wait_ge(f1_g, 4 * k + m + 1)
                    act(sg1[:, m % 2, :], bank(4), ACT.Silu).then_inc(f1_sg, 1)
                    if m == 1:
                        gather_steps(gather.take(STEPS["ffn1"][1]))
                gather_steps(gather.take(STEPS["ffn1"][2]))
                front(next_front(n))
                eng.wait_ge(f1_sc, k + 1)
                act(ex1[:, :], ex1[:, :], ACT.Exp).then_inc(f1_se, 1)
                stack(stack_of(n))
                gather_steps(gather.take(STEPS["ffn1"][3]))
                gather_steps(gather.take(STEPS["ffn1"][4]))
                gather.named += TI * NG
                gather_steps(gather.take(STEPS["ffn1"][5]))

            def ffn2(n, c):
                k = instance(n)
                enter(eng, "act", n)
                deviation(next_front(n))
                eng.wait_ge(f2_lg, k + 1)
                act(sc2[:, :], psum[:, 5, 0:TI * E2], ACT.Sigmoid).then_inc(f2_sc, 1)
                gather_steps(gather.take(STEPS["ffn2"][0]))
                for m in range(M2):
                    eng.wait_ge(f2_g, M2 * k + m + 1)
                    if m >= 2:
                        eng.wait_ge(f2_hm, M2 * k + m - 1)
                    act(sg2[:, m % 2, :], bank(2 * (m % 2)), ACT.Silu).then_inc(f2_sg, 1)
                    if m:
                        gather_steps(gather.take(STEPS["ffn2"][1][m - 1]))
                gather_steps(gather.take(STEPS["ffn2"][1][M2 - 1]))
                front(next_front(n))
                stack(stack_of(n))
                for _ in range(TI):
                    gather_steps(gather.take(STEPS["ffn2"][2]))

            def ffn3(n, c):
                k = instance(n)
                enter(eng, "act", n)
                deviation(next_front(n))
                eng.wait_ge(f3_ls, k + 1)
                act(ex3[:, :], ex3[:, :], ACT.Exp).then_inc(f3_ex, 1)
                eng.wait_ge(f3_gp, k + 1)
                act(gatet[0:E3, :], psum[0:E3, 4, :], ACT.Copy).then_inc(f3_gs, 1)
                front(next_front(n))

            def kv3(n):
                enter(eng, "act", n)
                eng.wait_ge(k3_k, 1)
                for g in range(2):
                    for b in range(B):
                        act(k3t[:, g, b * SP_:b * SP_ + S], psum[:, g, b * S:(b + 1) * S], ACT.Identity,
                            bias=wattn[:, CC["bk"].start + g:CC["bk"].start + g + 1]).then_inc(k3_kt, 1)
                eng.wait_ge(k3_v, 1)
                for b in range(B):
                    act(v3m[:, b, :], psum[:, 2 + b, 0:D], ACT.Copy).then_inc(k3_vs, 1)
                    act(v3r[0:32, b, :], psum[0:32, 2 + b, D:2 * D], ACT.Copy).then_inc(k3_vs, 1)

            def q3(n, c):
                k = instance(n)
                enter(eng, "act", n)
                deviation(next_front(n))
                eng.wait_ge(q3_q, k + 1)
                at = (c % 2) * CH
                for g in range(2):
                    bias = wattn[:, CC["bq"].start + g:CC["bq"].start + g + 1]
                    act(qx[:, g, at:at + CH], bank(g), ACT.Identity, bias=bias)
                    if c % 2 == 0:
                        act(qx[:, g, T:EXT], psum[:, g, 0:SP_], ACT.Identity, bias=bias)
                front(next_front(n))

            def corr(n, b):
                enter(eng, "act", n)
                if b:
                    eng.wait_ge(co_wr, 32 * b)
                for g in range(2):
                    eng.wait_ge(co_c, 2 * b + g + 1)
                    act(c1[g][:, 0:T], psum[:, 2 * g:2 * g + 2, :].rearrange("p a n -> p (a n)"), ACT.Copy).then_inc(co_s, 1)
                    act(c1[g][:, T:T + 16], psum[:, 2 * g, 0:16], ACT.Copy).then_inc(co_s, 1)

            def top(n):
                enter(eng, "act", n)
                eng.wait_ge(tp_n, 1)
                act(topw[0:32, 0:8], topw[0:32, 0:8], ACT.Exp).then_inc(tp_e, 1)

            def out3(n, b):
                enter(eng, "act", n)
                deviation(next_front(n))
                for g in range(2):
                    for N in range(2):
                        eng.wait_ge(o3_o, 4 * b + 2 * g + N + 1)
                        act(ot3[:, g, N * 512:(N + 1) * 512], bank(2 * g + N), ACT.Copy).then_inc(o3_s, 1)
                front(next_front(n))

            for n, (kind, layer, c) in enumerate(phases):
                {"kv": lambda: kv(n, layer), "attn": lambda: attn(n, layer, c), "tern": lambda: tern(n),
                 "ffn0": lambda: ffn0(n, c), "ffn1": lambda: ffn1(n, c), "ffn2": lambda: ffn2(n, c), "ffn3": lambda: ffn3(n, c),
                 "kv3": lambda: kv3(n), "q3": lambda: q3(n, c), "corr": lambda: corr(n, layer), "top": lambda: top(n),
                 "out3": lambda: out3(n, layer)}[kind]()
                leave(eng, "act")
                gather_steps(gather.take(STEPS[kind][-1] if kind in STEPS else 0))

        @block.vector
        def _(eng):
            own = Own(eng, own_dve)
            tt, ts, stt = eng.tensor_tensor, eng.tensor_scalar, eng.scalar_tensor_tensor

            def cast(ap, shape):
                return ap.broadcast_to(shape)

            gather, added = Gather(), []

            def accumulate():
                g = len(added)
                c, i, base, s = g // (TI * NG), g // NG % TI, GRP * (g % (RING // GRP)), g % 4
                x, at = x_sb[:, c * TI + i, :], g % (TI * NG) * GRP
                eng.wait_ge(f1_sd, g + 1)
                own.link(tt(ew[:, s, :], sdot[:, s, :], prob[c % 3][:, at:at + GRP], ALU.mult))
                if g:
                    eng.wait_ge(f1_acc, g)
                for j in range(GRP):
                    ins = stt(x, ring[:, base + j, D:2 * D], ew[:, s, j:j + 1], x, ALU.mult, ALU.add)
                    if j < GRP - 1:
                        own.link(ins)
                ins.then_inc(f1_acc, 1)
                added.append(g)

            def gather_steps(groups):
                for g in groups:
                    c, i, base = g // (TI * NG), g // NG % TI, GRP * (g % (RING // GRP))
                    eng.wait_ge(gathered[g % (RING // GRP)], 16 * GRP * (g // (RING // GRP) + 1))
                    for j in range(GRP):
                        row = ring[:, base + j, 0:D]
                        ins = eng.tensor_tensor_reduce(row, xg[c % 3][:, i, :], row, 1.0, 0.0, ALU.mult, ALU.add, dots[:, g % 4, j:j + 1])
                    ins.then_inc(f1_dot, 1)
                    if g > len(added):
                        accumulate()

            def gather_all(c):
                if c < 0:
                    return
                gather_steps(gather.rest(c))
                if len(added) < (c + 1) * TI * NG:
                    accumulate()
                eng.wait_ge(f1_acc, (c + 1) * TI * NG)

            def front(f):
                if f is None:
                    return
                kind, layer, c = phases[fronts[f]]
                if (kind, layer) == ("attn", 2):
                    gather_all(c)
                if kind == "ffn1":
                    gather_all(c - 3)
                for i in range(TI):
                    own.mark(eng.bn_stats(stats[:, i, :], x_sb[:, c * TI + i, :]))
                own.wait()
                for i in range(TI):
                    own.mark(eng.bn_aggr(mv[:, i, :], stats[:, i, :]))
                own.wait()
                ts(vare[:, :], mv[:, :, 1], EPS, None, ALU.add).then_inc(fr_var, 1)
                eng.wait_ge(fr_std, f + 1)
                own.link(eng.reciprocal(rstd[:, :], stdev[:, :]))
                if f:
                    eng.wait_ge(fr_tp, KT * f)
                for i in range(TI):
                    ts(normed(f)[:, i, :], x_sb[:, c * TI + i, :], mv[:, i, 0:1], rstd[:, i:i + 1], ALU.subtract, ALU.mult)\
                        .then_inc(fr_xn, 1)

            def add_x(c, i, src):
                return tt(x_sb[:, c * TI + i, :], x_sb[:, c * TI + i, :], src, ALU.add)

            def split(src, parts):
                own.link(tt(src, src, parts[0], ALU.subtract))
                own.link(eng.tensor_copy(parts[1], src))
                return tt(parts[2], src, parts[1], ALU.subtract)

            def stack(n):
                if n is None:
                    return
                k, (_, layer, c) = instance(n), phases[n]
                if layer == 2:
                    eng.wait_ge(sk_q, k + 1)
                    at = (c % 2) * CH
                    cos, sin = rope[:, at:at + CH], rope[:, T + at:T + at + CH]
                    for g in range(2):
                        own.mark(stt(qf[:, g, :], bank(6 + g), 0.25, cos, ALU.mult, ALU.mult))
                        own.link(eng.stream_shuffle(qsw, bank(6 + g), SWAP))
                        own.link(stt(qsw, qsw, 0.25, sin, ALU.mult, ALU.mult))
                        own.link(tt(qf[:, g, :], qf[:, g, :], qsw, ALU.add))
                    own.link(eng.tensor_copy(qparts[:, 0], qf))
                else:
                    eng.wait_ge(sk_f, 4 * (k + 1))
                split(qf, [qparts[:, z] for z in range(3)]).then_inc(sk_p, 1)

            def kv(n, layer):
                enter(eng, "dve", n)
                if n == 0:
                    eng.wait_ge(ld_x, 16)
                    front(0)
                for b in range(B):
                    ins = eng.memset(keys(b)[96:P], -1.0)
                    own.mark(ins)
                own.mark(eng.memset(kts[:, :, :, S:SP_], 0.0))
                own.wait()
                eng.sem_inc(kv_m, 1)
                gather_steps(gather.take(STEPS["kv"][0]))
                eng.wait_ge(kv_kt, 2 * (layer + 1))
                if layer == 2:
                    eng.wait_ge(ld_rope, 16)
                    cos, sin = (cast(rope[:, a:a + S].unsqueeze(1), [P, B, S]) for a in (0, T))
                    own.link(eng.stream_shuffle(ksw.rearrange("p g b s -> p (g b s)"), kts.rearrange("p g b s -> p (g b s)"), SWAP))
                    for g in range(2):
                        own.mark(tt(kts[:, g, :, 0:S], kts[:, g, :, 0:S], cos, ALU.mult))
                        own.mark(tt(ksw[:, g, :, 0:S], ksw[:, g, :, 0:S], sin, ALU.mult))
                    own.wait()
                    own.link(tt(kts, kts, ksw, ALU.add))
                own.link(eng.tensor_copy(kparts[:, 0], kts))
                split(kts, [kparts[:, z] for z in range(3)]).then_inc(kv_p, 1)
                stack(stack_of(n))
                eng.wait_ge(kv_v, layer + 1)
                eng.wait_ge(kv_z, 1)
                for b in range(B):
                    eng.tensor_copy(vmain(b).rearrange("p (h n) -> p h n", h=H)[:, :, 0:DH],
                                    psum[:, 4 + b, 0:D].rearrange("p (h d) -> p h d", h=H))
                    for j in range(4):
                        r = slice(32 * j, 32 * j + SR)
                        eng.tensor_copy(vrest(b)[r, :, j * 32:j * 32 + DH],
                                        psum[r, 4 + b, D:2 * D].rearrange("p (g j d) -> p g j d", g=G4, j=4)[:, :, j, :])
                gather_steps(gather.take(STEPS["kv"][1]))

            def attn(n, layer, c):
                k = instance(n)
                enter(eng, "dve", n)
                for u, (i, h0, h1) in enumerate(MAX_UNITS):
                    pair, nh = 2 * (u % 3), h1 - h0
                    eng.wait_ge(at_p1, NU * k + u + 1)
                    if nh == 6:
                        eng.reduce_max(m4[:, i, h0:h1].rearrange("p (a b) -> p a b", a=2),
                                       psum[:, pair:pair + 2, 0:3 * S].rearrange("p a (b s) -> p a b s", b=3), AX.X).then_inc(at_mx, 1)
                    else:
                        own.mark(eng.reduce_max(m4[:, i, h0:h0 + 3], psum[:, pair, 0:3 * S].rearrange("p (b s) -> p b s", b=3), AX.X))
                        own.mark(eng.reduce_max(m4[:, i, h0 + 3:h1], psum[:, pair + 1, 0:(nh - 3) * S].rearrange("p (b s) -> p b s", b=nh - 3), AX.X))
                        own.wait()
                        eng.sem_inc(at_mx, 1)
                    if u == 5:
                        gather_steps(gather.take(STEPS["attn"][0]))
                front(next_front(n))

                gather_steps(gather.take(STEPS["attn"][1]))
                stack(stack_of(n))
                gather_steps(gather.take(STEPS["attn"][2]))
                for i in range(TI):
                    eng.wait_ge(at_tt, 4 * k + i + 1)
                    sums_and_values = psum[:, i, :].rearrange("p (h n) -> p h n", h=H)
                    own.link(eng.reciprocal(oden[:, i, :], sums_and_values[:, :, DH]))
                    tt(onorm[:, i, :].rearrange("p (h d) -> p h d", h=H), sums_and_values[:, :, 0:DH],
                       cast(oden[:, i, :].unsqueeze(2), [P, H, DH]), ALU.mult).then_inc(at_on, 1)
                    if i == 1:
                        gather_steps(gather.take(STEPS["attn"][3]))
                gather_steps(gather.take(STEPS["attn"][4]))
                if layer == 0:
                    eng.wait_ge(at_bo, k + 1)
                for i in range(TI):
                    eng.wait_ge(at_wo, 4 * k + i + 1)
                    own.mark(add_x(c, i, psum[:, i, 0:D]))
                gather_steps(gather.take(STEPS["attn"][5]))

            def tern(n):
                enter(eng, "dve", n)
                eng.wait_ge(ld_f0, 16)
                ts(utg[0:RANK, :], utg[0:RANK, :], f0("gate")[0:RANK, :], None, ALU.mult).then_inc(tn_w, 1)
                own.mark(eng.tensor_reduce(absum[:, 0:8], fcnat, AX.X, ALU.add, apply_absolute_value=True))
                own.link(eng.tensor_reduce(absum[:, 8:10], projnat, AX.X, ALU.add, apply_absolute_value=True))
                own.mark(ts(sclip[:, 0:8], absum[:, 0:8], 1.0 / D, 1e-5, ALU.mult, ALU.max))
                own.link(ts(sclip[:, 8:10], absum[:, 8:10], 1.0 / HID0, 1e-5, ALU.mult, ALU.max))
                own.mark(ts(hi_th, sclip, 0.5, None, ALU.mult))
                own.link(ts(lo_th, sclip, -0.5, None, ALU.mult))
                for r in range(10):
                    nat, n_ = (fcnat[:, r, :], D) if r < 8 else (projnat[:, r - 8, :], HID0)
                    own.mark(ts(tplus[:, 0:n_], nat, hi_th[:, r:r + 1], sclip[:, r:r + 1], ALU.is_gt, ALU.mult))
                    own.link(ts(tminus[:, 0:n_], nat, lo_th[:, r:r + 1], sclip[:, r:r + 1], ALU.is_lt, ALU.mult))
                    if r < 8:
                        own.link(tt(nat, tplus[:, 0:n_], tminus[:, 0:n_], ALU.subtract))
                        eng.wait_ge(tn_u, r + 1)
                        tt(nat, nat, psum[:, 1 + r % 2, 0:D], ALU.add).then_inc(tn_nat, 1)
                    else:
                        tt(nat, tplus[:, 0:n_], tminus[:, 0:n_], ALU.subtract).then_inc(tn_nat, 1)
                        eng.wait_ge(tn_nat, r + 1)

            def ffn0(n, c):
                k = instance(n)
                enter(eng, "dve", n)
                front(next_front(n))
                for m in range(8):
                    eng.wait_ge(f0_r, 8 * k + m + 1)
                    tt(hid0[:, m, :], hid0r[:, m, :], hid0r[:, m, :], ALU.mult).then_inc(f0_sq, 1)
                for i in range(TI):
                    eng.wait_ge(f0_y, 4 * k + i + 1)
                    add_x(c, i, psum[:, 4 + i % 2, 0:D]).then_inc(f0_x, 1)

            def ffn1(n, c):
                k = instance(n)
                enter(eng, "dve", n)
                front(next_front(n))
                gather_steps(gather.take(STEPS["ffn1"][0]))
                for i in range(TI):
                    eng.wait_ge(f1_sim, 4 * k + i + 1)
                    for p in range(2):
                        for h in range(PH):
                            own.mark(eng.max(topv[:, p, i * PH + h, :], psum[:, 2 * (i % 2) + p, h * NKEY:(h + 1) * NKEY]))
                    own.wait()
                    for p in range(2):
                        for h in range(PH):
                            ins = eng.max_index(topi[:, p, i * PH + h, :], topv[:, p, i * PH + h, :],
                                                psum[:, 2 * (i % 2) + p, h * NKEY:(h + 1) * NKEY])
                    ins.then_inc(f1_tk, 1)
                    eng.wait_ge(f1_sg, 4 * k + i + 1)
                    tt(hm1[:, i, :], sg1[:, i % 2, :], bank(5), ALU.mult).then_inc(f1_hm, 1)
                    if i % 2:
                        gather_steps(gather.take(STEPS["ffn1"][1 + i // 2]))
                eng.wait_ge(f1_tk, 4 * k + 4)
                own.mark(eng.tensor_copy(topf, topi))
                R = 16
                own.link(tt(sums, cast(topv[:, 0].unsqueeze(3), [P, R, 8, 8]), cast(topv[:, 1].unsqueeze(2), [P, R, 8, 8]), ALU.add))
                for r in range(R):
                    own.mark(eng.max(best[:, r, :], sums[:, r].rearrange("p i j -> p (i j)")))
                own.wait()
                ex = ex1.rearrange("p (r k) -> p r k", r=R)
                tt(ex, best, cast(best[:, :, 0:1], [P, R, 8]), ALU.subtract).then_inc(f1_sc, 1)
                for r in range(R):
                    own.mark(eng.max_index(pos[:, r * 8:r * 8 + 8], best[:, r, :], sums[:, r].rearrange("p i j -> p (i j)")))
                own.wait()
                stack(stack_of(n))
                gather_steps(gather.take(STEPS["ffn1"][3]))
                own.mark(ts(pside[0], pos, 3, None, ALU.logical_shift_right))
                own.link(ts(pside[1], pos, 7, None, ALU.bitwise_and))
                for z in range(2):
                    own.mark(eng.tensor_copy(psidef[z], pside[z]))
                own.wait()
                for z in range(2):
                    own.mark(tt(eq[z].rearrange("p r k j -> p (r k) j"), cast(psidef[z].unsqueeze(2), [P, P, 8]),
                                cast(iota8.unsqueeze(1), [P, P, 8]), ALU.is_equal))
                own.wait()
                for z in range(2):
                    own.mark(tt(eq[z], eq[z], cast(topf[:, z].unsqueeze(2), [P, R, 8, 8]), ALU.mult))
                own.wait()
                for z in range(2):
                    own.mark(eng.reduce_sum(pick[z], eq[z].rearrange("p r k j -> p (r k) j"), AX.X))
                own.wait()
                own.link(stt(rowf, pick[0], float(NKEY), pick[1], ALU.mult, ALU.add))
                gather_steps(gather.take(STEPS["ffn1"][4]))
                ts(rowid[c % 3][:, :], rowf, float(NEXP1 - 1), None, ALU.min).then_inc(f1_idx, 1)
                eng.wait_ge(f1_se, k + 1)
                own.link(eng.reduce_sum(esum, ex, AX.X))
                own.link(eng.reciprocal(erec, esum))
                tt(prob[c % 3][:, :].rearrange("p (r k) -> p r k", r=R), ex, cast(erec.unsqueeze(2), [P, R, 8]), ALU.mult).then_inc(f1_idx, 1)
                for i in range(TI):
                    eng.wait_ge(f1_y, 4 * k + i + 1)
                    own.mark(add_x(c, i, psum[:, i, 0:D]))
                own.wait()
                gather.named += TI * NG
                gather_steps(gather.take(STEPS["ffn1"][5]))

            def ffn2(n, c):
                k = instance(n)
                enter(eng, "dve", n)
                front(next_front(n))
                gather_steps(gather.take(STEPS["ffn2"][0]))
                eng.wait_ge(f2_sc, k + 1)
                best_two(sc2, tv2, ti2, tf2)
                own.link(tt(s2[0], tv2[:, :, 0], tv2[:, :, 1], ALU.add))
                own.link(ts(s2[1], s2[0], 1e-20, None, ALU.add))
                own.link(eng.reciprocal(s2[2], s2[1]))
                own.link(ts(s2[3], s2[2], 2.5, None, ALU.mult))
                spread(comb2, tv2, tf2, s2[3])
                for m in range(M2):
                    eng.wait_ge(f2_sg, M2 * k + m + 1)
                    tt(hm2[:, m, :], sg2[:, m % 2, :], bank(2 * (m % 2) + 1), ALU.mult).then_inc(f2_hm, 1)
                    gather_steps(gather.take(STEPS["ffn2"][1][m]))
                stack(stack_of(n))
                for y in range(TI * 9):
                    i, e, K = y // 9, y % 9, TI * 9 * k + y
                    eng.wait_ge(f2_y, K + 1)
                    if e:
                        eng.wait_ge(f2_x, K)
                    src = psum[:, y % 5, 0:D]
                    ins = add_x(c, i, src) if e == 8 else stt(
                        x_sb[:, c * TI + i, :], src, comb2[0][:, i, e:e + 1], x_sb[:, c * TI + i, :], ALU.mult, ALU.add)
                    ins.then_inc(f2_x, 1)
                    if e == 8:
                        gather_steps(gather.take(STEPS["ffn2"][2]))

            def best_two(src, tv, ti, tf):
                for i in range(TI):
                    own.mark(eng.max(tv[:, i, :], src[:, i * 8:(i + 1) * 8]))
                own.wait()
                for i in range(TI):
                    own.mark(eng.max_index(ti[:, i, :], tv[:, i, :], src[:, i * 8:(i + 1) * 8]))
                own.wait()
                own.link(eng.tensor_copy(tf, ti))

            def spread(comb, tv, tf, scale):
                shape = [P, TI, 8]
                for r in range(2):
                    own.mark(tt(comb[r], cast(tf[:, :, r:r + 1], shape), cast(iota8.unsqueeze(1), shape), ALU.is_equal))
                own.wait()
                for r in range(2):
                    own.mark(tt(comb[r], comb[r], cast(tv[:, :, r:r + 1], shape), ALU.mult))
                own.wait()
                own.link(tt(comb[2], comb[0], comb[1], ALU.add))
                own.link(tt(comb[0], comb[2], cast(scale.unsqueeze(2), shape), ALU.mult))

            def ffn3(n, c):
                k = instance(n)
                enter(eng, "dve", n)
                front(next_front(n))
                eng.wait_ge(f3_lg, k + 1)
                lg = psum[:, 5, 0:TI * E3].rearrange("p (i e) -> p i e", i=TI)
                shape = [P, TI, E3]
                ex = ex3.rearrange("p (i e) -> p i e", i=TI)
                own.link(eng.reduce_max(mx3, lg, AX.X))
                tt(ex, lg, cast(mx3.unsqueeze(2), shape), ALU.subtract).then_inc(f3_ls, 1)
                eng.wait_ge(f3_ex, k + 1)
                own.link(eng.reduce_sum(s3[0], ex, AX.X))
                own.link(eng.reciprocal(s3[1], s3[0]))
                own.link(tt(pr3.rearrange("p (i e) -> p i e", i=TI), ex, cast(s3[1].unsqueeze(2), shape), ALU.mult))
                best_two(pr3, tv3, ti3, tf3)
                own.link(tt(s3[2], tv3[:, :, 0], tv3[:, :, 1], ALU.add))
                own.link(eng.reciprocal(s3[3], s3[2]))
                spread(comb3, tv3, tf3, s3[3])
                eng.sem_inc(f3_gt, 1)
                for y in range(TI * 4):
                    i, K = y // 4, TI * 4 * k + y
                    eng.wait_ge(f3_y, K + 1)
                    if y % 4:
                        eng.wait_ge(f3_x, K)
                    for r in range(2):
                        e = 2 * (y % 4) + r
                        ins = stt(x_sb[:, c * TI + i, :], psum[:, y % 4, r * D:(r + 1) * D], comb3[0][:, i, e:e + 1],
                                  x_sb[:, c * TI + i, :], ALU.mult, ALU.add)
                        if r == 0:
                            own.link(ins)
                    ins.then_inc(f3_x, 1)
                eng.wait_ge(f3_x, TI * 4 * (k + 1))
                eng.wait_ge(f3_b, k + 1)
                for i in range(TI):
                    add_x(c, i, psum[:, 4 + i // 2, (i % 2) * D:(i % 2 + 1) * D])

            def kv3(n):
                enter(eng, "dve", n)
                for g in range(2):
                    for b in range(B):
                        own.mark(eng.memset(k3t[:, g, b * SP_ + S:(b + 1) * SP_], 0.0))
                own.wait()
                eng.wait_ge(k3_kt, 4)
                shape = [P, U, 8, 16]
                mask = cast(mask8.unsqueeze(1).unsqueeze(3), shape)
                for b in range(B):
                    for g in range(2):
                        src = k3t[:, g, b * SP_:(b + 1) * SP_].rearrange("p (u s) -> p u s", u=U)
                        tt(kst(b, g).rearrange("p u (h s) -> p u h s", h=8), cast(src.unsqueeze(2), shape), mask, ALU.mult)

            def top(n):
                enter(eng, "dve", n)
                r = slice(0, 32)
                eng.wait_ge(co_m, 1)
                own.link(eng.tensor_copy(cor[r, :], psum[r, 4:6, :].rearrange("p a n -> p (a n)")))
                own.link(eng.max(topm[r, :], cor[r, :]))
                own.mark(eng.max_index(topj[r, :], topm[r, :], cor[r, :]))
                tt(topw[r, :], topm[r, :], cast(topm[r, 0:1], [32, 8]), ALU.subtract).then_inc(tp_n, 1)
                own.wait()
                own.link(eng.tensor_copy(topjf[r, :], topj[r, :]))
                own.link(ts(topjf[r, :], topjf[r, :], -1.0, float(T), ALU.mult, ALU.add))
                own.link(ts(topm[r, :], topjf[r, :], float(T), float(T), ALU.is_ge, ALU.mult))
                own.link(tt(topjf[r, :], topjf[r, :], topm[r, :], ALU.subtract))
                eng.wait_ge(tp_e, 1)
                own.link(eng.reduce_sum(rsum3[r, 0:1], topw[r, 0:TOPC], AX.X))
                own.link(eng.reciprocal(rsum3[r, 1:2], rsum3[r, 0:1]))
                own.link(ts(topw[r, :], topw[r, :], rsum3[r, 1:2], None, ALU.mult))
                for k in range(TOPC):
                    out = rollw if k == 0 else rollt[k % 2]
                    own.link(ts(out[r, :], iota[r, :], topjf[r, k:k + 1], topw[r, k:k + 1], ALU.is_equal, ALU.mult))
                    if k:
                        own.link(tt(rollw[r, :], rollw[r, :], out[r, :], ALU.add))
                eng.sem_inc(tp_r, 1)

            def out3(n, b):
                enter(eng, "dve", n)
                front(next_front(n))
                eng.wait_ge(o3_bo, b + 1)
                for i in range(8):
                    eng.wait_ge(o3_y, 8 * b + i + 1)
                    add_x(2 * b, i, psum[:, 4 + i % 2, 0:D]).then_inc(o3_x, 1)

            def q3(n):
                enter(eng, "dve", n)
                front(next_front(n))
                if instance(n) == 0:
                    shape = [P, U, 8, 16]
                    mask = cast(mask8.unsqueeze(1).unsqueeze(3), shape)
                    eng.wait_ge(k3_rd, 16 * 32)
                    for b in range(B):
                        for g in range(2):
                            tt(vst(b, g).rearrange("p u (h d) -> p u h d", h=8), cast(v3s[:, 2 * b + g].unsqueeze(2), shape), mask, ALU.mult)

            for n, (kind, layer, c) in enumerate(phases):
                {"kv": lambda: kv(n, layer), "attn": lambda: attn(n, layer, c), "tern": lambda: tern(n),
                 "ffn0": lambda: ffn0(n, c), "ffn1": lambda: ffn1(n, c), "ffn2": lambda: ffn2(n, c), "ffn3": lambda: ffn3(n, c),
                 "kv3": lambda: kv3(n), "q3": lambda: q3(n), "corr": lambda: enter(eng, "dve", n), "top": lambda: top(n),
                 "out3": lambda: out3(n, layer)}[kind]()
                leave(eng, "dve")
                gather_steps(gather.take(STEPS[kind][-1] if kind in STEPS else 0))

        @block.gpsimd
        def _(eng):
            own = Own(eng, own_pool)
            for b in range(B):
                own.mark(eng.memset(vmain(b).rearrange("p (h n) -> p h n", h=H)[:, :, DH:32], 1.0))
                own.mark(eng.memset(vrest(b), 0.0))
            own.wait()
            for b in range(B):
                for j in range(4):
                    ins = eng.memset(vrest(b)[32 * j:32 * j + SR, :, j * 32 + DH:j * 32 + 32], 1.0)
            ins.then_inc(kv_z, 1)

            def add_bias(kind, layer, signal):
                for n, (kind_, layer_, c) in enumerate(phases):
                    if kind_ == kind and layer_ in layer:
                        enter(eng, "pool", n)
                        tiles = range(c * TI, (c + 1) * TI) if kind == "attn" else range(8 * layer_, 8 * layer_ + 8)
                        for t in tiles:
                            ins = eng.tensor_tensor(x_sb[:, t, :], x_sb[:, t, :], wattn[:, AC["bo"]], ALU.add)
                        ins.then_inc(signal, 1)

            add_bias("attn", (0,), at_bo)

            def fetch(g):
                c, s, at = g // (TI * NG), g % (RING // GRP), g % (TI * NG) * GRP
                if at == 0:
                    eng.wait_ge(f1_idx, 2 * (c + 1))
                if g >= RING // GRP:
                    eng.wait_ge(f1_acc, g - RING // GRP + 1)
                for j in range(GRP):
                    eng.indirect_dma_start(ring[:, s * GRP + j, :], None, io["table"],
                                           bass.IndirectOffsetOnAxis(ap=rowid[c % 3][:, at + j:at + j + 1], axis=0))\
                        .then_inc(gathered[s], 16)

            for g in range(sum(p[0] == "ffn1" for p in phases) * TI * NG):
                fetch(g)
            add_bias("out3", (0, 1), o3_bo)
            eng.drain().then_inc(end_pool, 1)

        @block.sync
        def _(eng):
            loads = {}

            def load(dst, src, s):
                loads[s.name] = (s, loads.get(s.name, (s, 0))[1] + 16)
                eng.dma_start(dst, src).then_inc(s, 16)

            def last(kind, layer):
                ns = [n for n, p in enumerate(phases) if p[0] == kind and p[1] == layer]
                return max(ns) if ns else None

            def after(n):
                for s in ends.values():
                    eng.wait_ge(s, n + 1)

            def stack(n):
                if n is None:
                    return
                k = instance(n)
                eng.wait_ge(sk_p, k + 1)
                eng.dma_start(scrq.rearrange("z (g p) n -> p (z g) n", p=P),
                              qparts.rearrange("p z g n -> p (z g) n")).then_inc(sk_wr, 16)
                eng.wait_ge(sk_wr, 16 * (k + 1))
                if k:
                    eng.wait_ge(at_s2, 12 * k)
                for z in range(NB):
                    eng.dma_start(queries[z * DH:(z + 1) * DH], scrq[Q_PARTS[z]].rearrange("(h d) n -> d h n", d=DH))\
                        .then_inc(sk_rd, 16)

            load(x_sb[:, :, :], io["x"].rearrange("(i p) d -> p i d", p=P), ld_x)
            load(const[:, :], io["const"], ld_const)
            load(ctxt[:, :, :].rearrange("p k n -> p (k n)"), io["ctxt"], ld_ctx)
            load(wattn[:, 0:AN], io["attn0"], ld_attn)
            load(raw0, io["ffn0"], ld_f0)
            load(rope[:, :], io["rope"], ld_rope)
            for n, (kind, layer, c) in enumerate(phases):
                if kind == "kv":
                    enter(eng, "sp", n)
                    eng.wait_ge(kv_p, layer + 1)
                    eng.dma_start(scrk.rearrange("z (g p) n -> p (z g) n", p=P),
                                  kparts.rearrange("p z g b s -> p (z g) (b s)")).then_inc(kv_wr, 16)
                    eng.wait_ge(kv_wr, 16 * (layer + 1))
                    eng.wait_ge(kv_m, layer + 1)
                    for z in range(NB):
                        for b in range(B):
                            src = scrk[K_PARTS[z]].rearrange("(h d) (b s) -> b d h s", d=DH, b=B)[b]
                            eng.dma_start(keys(b)[z * DH:(z + 1) * DH], src).then_inc(kv_rd, 16)
                if kind == "attn":
                    k = instance(n)
                    eng.wait_ge(at_mts, k + 1)
                    eng.dma_start(queries[MROW:MROW + 1], mt[:, :]).then_inc(at_mr, 16)
                stack(stack_of(n))
                if kind == "kv3":
                    enter(eng, "sp", n)
                    eng.wait_ge(k3_vs, 4)
                    for b in range(B):
                        eng.dma_start(scrv[b, 0:P, :], v3m[:, b, :]).then_inc(k3_wr, 16)
                        eng.dma_start(scrv[b, P:SP_, :], v3r[0:32, b, :]).then_inc(k3_wr, 16)
                    eng.wait_ge(k3_wr, 16 * 4)
                    for b in range(B):
                        for g in range(2):
                            src = scrv[b].rearrange("(u s) (a h d) -> a h s u d", s=16, a=2, d=DH)[g]
                            for h in range(8):
                                eng.dma_start(v3s[h * 16:(h + 1) * 16, 2 * b + g], src[h]).then_inc(k3_rd, 16)
                if kind == "corr":
                    for g in range(2):
                        a = 2 * layer + g
                        eng.wait_ge(co_s, 4 * layer + 2 * g + 2)
                        eng.dma_start(scr1[a], c1[g]).then_inc(co_wr, 16)
                    for g in range(2):
                        a = 2 * layer + g
                        eng.wait_ge(co_wr, 16 * 2 * (layer + 1))
                        src = bass.AP(scr1.tensor, a * P * (T + 16), [[16 * (T + 16), 8], [T + 17, 16], [1, T]])
                        eng.dma_start(c2[a], src).then_inc(co_rd, 16)
                if kind == "top":
                    eng.wait_ge(tp_r, 1)
                    for z in range(2):
                        eng.dma_start(scr2[:, z * T:(z + 1) * T], rollw[0:32, :]).then_inc(tp_wr, 16)
                    eng.wait_ge(tp_wr, 32)
                    for a in range(4):
                        src = bass.AP(scr2.tensor, 8 * a * 2 * T + T - SP_ - 15, [[2 * T, 8], [1, 16], [1, T + SP_]])
                        eng.dma_start(roll(a), src).then_inc(tp_rd, 16)
                if kind == "ffn3" or (stop is not None and n == len(phases) - 1):
                    eng.wait_ge(ends["dve"], n + 1)
                    for q in ([c] if kind == "ffn3" else range(NCH)):
                        eng.dma_start(io["out"].rearrange("(i p) d -> p i d", p=P)[:, q * TI:(q + 1) * TI, :],
                                      x_sb[:, q * TI:(q + 1) * TI, :]).then_inc(stored, 16)
                if kind == "attn" and n == last("attn", layer):
                    after(n)
                    if layer < 2:
                        load(wattn[:, 0:AN], io[f"attn{layer + 1}"], ld_attn)
                    else:
                        load(wattn[:, 0:CN], io["corr"], ld_attn)
                if n == last("attn", 2):
                    load(late[:, 0:LN], io["late"], ld_late)
                if n == last("ffn0", 0):
                    after(n)
                    load(wf[:, 0:F1N], io["ffn1"], ld_f1)
                if n == last("ffn1", 1):
                    after(n)
                    load(wf[:, 0:F2N], io["ffn2"], ld_f2)
                if n == last("ffn2", 2):
                    after(n)
                    load(wf[:, 0:F3N], io["ffn3"], ld_f3)
            eng.wait_ge(end_pool, 1)
            eng.wait_ge(stored, 16 * NCH)
            for s, count in loads.values():
                eng.wait_ge(s, count)


def packed(widths, **arrays):
    cols, n = columns(widths)
    out = np.zeros((P, n), np.float32)
    for name, a in arrays.items():
        a = np.asarray(a, np.float32).reshape(a.shape[0], -1)
        out[:a.shape[0], cols[name]] = a
    return out


def by_rows(w):
    w = np.asarray(w)
    return w.reshape(-1, P, w.shape[1]).transpose(1, 0, 2)


def per_feature(b):
    return np.asarray(b).reshape(2, P).T


def on_all(row):
    return np.broadcast_to(np.asarray(row).reshape(1, -1), (P, np.size(row)))


def constants():
    p = np.arange(P)
    selh = np.zeros((P, 4, 32), np.float32)
    for a in range(4):
        selh[p, a, 8 * a + p // 16] = 1.0 / DH
    mask8 = (p[:, None] // 16 == np.arange(8)[None]).astype(np.float32)
    padrow = np.where(p % 32 < SR, 0.0, -3e38).astype(np.float32)[:, None]
    token = np.arange(SP_) // 16 * 16 + 15 - np.arange(SP_) % 16
    valid = on_all((token < S).astype(np.float32))
    const = packed(CONST_PACK, ident=np.eye(P, dtype=np.float32), mask8=mask8, padrow=padrow,
                   iota8=on_all(np.arange(8, dtype=np.float32)), selh=selh,
                   valid=valid)
    inv = (np.float32(10000.0) ** (-np.arange(0, DH, 2, dtype=np.float32) / np.float32(DH))).astype(np.float32)
    ang = (np.arange(T, dtype=np.float32)[None, :] * inv[:, None]).astype(np.float32)
    d = p % DH
    sign = np.where(d % 2 == 0, -1.0, 1.0).astype(np.float32)
    rope = packed(ROPE_PACK, cos=np.cos(ang)[d // 2], sin=np.sin(ang)[d // 2] * sign[:, None])
    return const, rope


def kernel(**inputs):
    import concourse.bacc as _bacc
    from concourse.bass_utils import run_bass_kernel_spmd as _run

    a = {k: np.asarray(v) for k, v in inputs.items()}
    zero = np.zeros(D, np.float32)

    def attention(wq, wk, wv, wo, bq, bk, bv, bo):
        return packed(ATTN_PACK, wq=by_rows(wq), wk=by_rows(wk), wv=by_rows(wv), wo=by_rows(wo), bq=per_feature(bq),
                      bk=per_feature(bk), bv=on_all(bv), bo=on_all(bo))

    l0, l1, l2, l3 = ({k[9:]: v for k, v in a.items() if k.startswith(f"L{i}_xattn")} for i in range(4))
    f0, f1, f2, f3 = ({k[7:]: v for k, v in a.items() if k.startswith(f"L{i}_ffn")} for i in range(4))
    arrays = {"x": a["x"].reshape(B * T, D)}
    ctx = a["ctx_1024"]
    arrays["ctxt"] = by_rows(ctx.reshape(B * S, D).T).reshape(P, -1)
    rev = np.zeros((B, SP_, D), np.float32)
    rev[:, :S] = ctx
    rev = rev.reshape(B, U, 16, D)[:, :, ::-1].reshape(B * SP_, D)
    arrays["late"] = packed(LATE_PACK, iota=on_all(np.arange(T, dtype=np.float32)), ctxr=by_rows(rev.T))
    arrays["attn0"] = attention(l0["Wq"], l0["Wk"], l0["Wv"], l0["Wo"], l0["b_q"], l0["b_k"], l0["b_v"], l0["b_o"])
    arrays["attn1"] = attention(l1["wq_w"].T, l1["wk_w"].T, l1["wv_w"].T, l1["dense_w"].T,
                                l1["wq_b"], l1["wk_b"], l1["wv_b"], l1["dense_b"])
    arrays["attn2"] = attention(l2["Wq"], l2["Wk"], l2["Wv"], l2["Wo"], zero, zero, zero, zero)
    arrays["corr"] = packed(CORR_PACK, wq=by_rows(l3["Wq"]), wk=by_rows(l3["Wk"]), wv=by_rows(l3["Wv"]), wo=by_rows(l3["Wo"]),
                            bq=per_feature(l3["bq"]), bk=per_feature(l3["bk"]), bv=on_all(l3["bv"]), bo=on_all(l3["bo"]))
    arrays["ffn0"] = packed(FFN0_PACK, fc=by_rows(f0["w_fc"]), proj=by_rows(f0["w_proj"]), ut=f0["u"].T, v=f0["v"],
                            fbt=f0["fast_b"].T, gate=on_all(f0["gate"]))
    keys = np.zeros((2, PH, 32, PH, NKEY), np.float32)
    for h in range(PH):
        keys[:, h, :, h, :] = f1["keys"][h].transpose(1, 2, 0)
    arrays["ffn1"] = packed(FFN1_PACK, wq=by_rows(f1["w_queries"].T), keys=keys.reshape(2, P, 512).transpose(1, 0, 2),
                            wg=by_rows(f1["w_gate"].T), wu=by_rows(f1["w_up"].T), wd=by_rows(f1["w_down"].T))
    arrays["table"] = np.concatenate([f1["down_embed"], f1["up_embed"]], axis=1)
    gu = np.stack([np.concatenate([f2["w_gate"], f2["ws_gate"].reshape(2, P, D)]),
                   np.concatenate([f2["w_up"], f2["ws_up"].reshape(2, P, D)])], axis=1)
    down = np.concatenate([f2["w_down"].transpose(2, 0, 1), f2["ws_down"].T.reshape(2, P, D).transpose(1, 0, 2)], axis=1)
    arrays["ffn2"] = packed(FFN2_PACK, gate=by_rows(f2["gate_weight"].T), gu=by_rows(gu.reshape(-1, D).T), down=down)
    arrays["ffn3"] = packed(FFN3_PACK, gate=by_rows(f3["Wg"]), we=by_rows(f3["We"].transpose(1, 0, 2).reshape(D, -1)), be=f3["be"])
    arrays["const"], arrays["rope"] = constants()

    nc = _bacc.Bacc("TRN2", target_bir_lowering=False, num_devices=1)
    ins, io = {}, {}
    for name, v in arrays.items():
        ins[f"in_{name}"] = np.ascontiguousarray(v)
        io[name] = nc.dram_tensor(f"in_{name}", v.shape, FP, kind="ExternalInput").ap()
    io["out"] = nc.dram_tensor("out", (B * T, D), FP, kind="ExternalOutput").ap()
    build(nc, io, STOP)
    r = _run(nc, [ins], core_ids=[0])
    return r.results[0]["out"].reshape(B, T, D)
```

```python
from contextlib import ExitStack

import concourse.bass as bass
import numpy as np
from concourse import mybir

FP, BF, U32 = mybir.dt.float32, mybir.dt.bfloat16, mybir.dt.uint32
ALU, ACT, AX = mybir.AluOpType, mybir.ActivationFunctionType, mybir.AxisListType

P = 128
STOP = None
B, T, D = 2, 1024, 256
S = 154
H, DH = 16, 16
KT = D // P
NCH, CH = 4, 512
TI = CH // P
SR = S - P
SP_ = 160
G4 = 4
EPS = 1e-5
HID0, RANK = 1024, 16
NKEY, TOPK, PH, NEXP1, INTER = 128, 8, 4, 4096, 512
E2, M2 = 8, 10
E3 = 8
U = SP_ // 16
EXT = T + SP_
TOPC = 6
RING, GRP = 20, 4
NG = PH * TOPK // GRP
Q_PARTS, K_PARTS = (0, 0, 0, 1, 1, 1, 2), (0, 1, 2, 0, 1, 2, 0)
NB = len(Q_PARTS)
MROW = NB * DH
SWAP = [lane ^ 1 for lane in range(32)]
MAX_UNITS = [(i, h, min(h + 6, H)) for i in range(TI) for h in range(0, H, 6)]
NU = len(MAX_UNITS)

STEPS = dict(kv=(2, 0, 4), attn1=(1, 3, 2, 0, 4, 0, 1), attn2=(0, 2, 3, 0, 2, 1, 1), ffn1=(2, 0, 0, 1, 0, 0, 2),
             ffn2=(2, (1, 1, 1, 0, 1, 1, 1, 1, 1, 0), 0, 4, 2))

TERN_ROWS = {1: range(0, 4), 2: range(4, 8), 3: range(8, 10)}

ATTN_PACK = dict(wq=KT * D, wk=KT * D, wv=KT * D, wo=KT * D, bq=2, bk=2, bv=D, bo=D)
CORR_PACK = ATTN_PACK
FFN0_PACK = dict(fc=8 * D, proj=2 * HID0, ut=HID0, v=D, fbt=RANK, gate=1)
FFN1_PACK = dict(wq=KT * D, keys=2 * 512, wg=KT * INTER, wu=KT * INTER, wd=4 * D)
FFN2_PACK = dict(gate=KT * E2, gu=KT * M2 * 2 * P, down=M2 * D)
FFN3_PACK = dict(gate=KT * E3, we=KT * E3 * D, be=D)
CONST_PACK = dict(ident=P, mask8=8, padrow=1, iota8=8, selh=2 * 32, valid=SP_)
LATE_PACK = dict(iota=T, ctxr=KT * B * SP_)
ROPE_PACK = dict(cos=T, sin=T)


def columns(pack):
    at, out = 0, {}
    for name, n in pack.items():
        out[name] = slice(at, at + n)
        at += n
    return out, at


def schedule():
    out = [("kv", 0, 0)] + [("attn", 0, c) for c in range(NCH)] + [("tern", 0, 0)]
    out += [("ffn0", 0, c) for c in range(NCH - 1)] + [("kv", 1, 0), ("ffn0", 0, NCH - 1)]
    for layer in (1, 2):
        for c in range(NCH):
            out.append(("attn", layer, c))
            if layer == 1 and c == NCH - 1:
                out.append(("kv", 2, 0))
            out.append((f"ffn{layer}", layer, c))
    out.append(("kv3", 3, 0))
    for b in range(B):
        out += [("q3", b, 2 * b), ("q3", b, 2 * b + 1), ("corr", b, 0)]
    out += [("out3", b, 0) for b in range(B)]
    out += [("ffn3", 3, c) for c in range(NCH)]
    return out


def build(nc, io, stop=None):
    phases = schedule()[:stop]
    fronts = [n for n, (kind, _, _) in enumerate(phases) if kind in ("attn", "ffn0", "ffn1", "ffn2", "q3", "ffn3")]
    front_of = {n: f for f, n in enumerate(fronts)}

    def instance(n):
        return sum(p[0] == phases[n][0] for p in phases[:n])

    def next_front(n):
        f = sum(m <= n for m in fronts)
        if f >= len(fronts):
            return None
        m = fronts[f]
        kind, b, _ = phases[n]
        if phases[m][0] == "ffn3" and phases[m - 1][0] == "out3":
            return f if kind == "out3" and b == 1 else None
        return f if n == (fronts[f - 1] if f else 0) else None

    def is_tail(n):
        f = next_front(n)
        return f is not None and phases[fronts[f]][2] == phases[n][2]

    def stack_of(n):
        return n + 1 if n + 1 < len(phases) and phases[n + 1][0] == "attn" else None

    def stacks_before(f):
        return sum(phases[m][0] == "attn" for m in fronts[:f])

    ctx = ExitStack()
    with ctx:
        def sb(name, shape, dt=FP):
            return ctx.enter_context(nc.sbuf_tensor(name, shape, dt))

        def sem(name):
            return ctx.enter_context(nc.semaphore(name))

        x_sb = sb("x_sb", [P, NCH * TI, D])
        xa = sb("xa", [P, TI, D])
        xg = [sb(f"xg{i}", [P, TI, D]) for i in range(3)]
        xt = sb("xt", [P, KT, CH])
        stats = sb("stats", [P, TI, 6])
        mv = sb("mv", [P, TI, 2])
        vare, stdev, newton, rstd = (sb(s, [P, TI]) for s in ("vare", "stdev", "newton", "rstd"))
        AC, AN = columns(ATTN_PACK)
        CC, CN = columns(CORR_PACK)
        F0, F0N = columns(FFN0_PACK)
        F1, F1N = columns(FFN1_PACK)
        F2, F2N = columns(FFN2_PACK)
        F3, F3N = columns(FFN3_PACK)
        KC, KN = columns(CONST_PACK)
        RN, (LC, LN) = columns(ROPE_PACK)[1], columns(LATE_PACK)
        const = sb("const", [P, KN])
        ctxt = sb("ctxt", [P, KT, B * S])
        wattn = sb("wattn", [P, max(AN, CN)])
        wf = sb("wf", [P, max(4096, F1N, F2N, F3N)])
        bufA = sb("bufA", [P, 8832])
        bufB = sb("bufB", [P, 10240])
        ringb = sb("ring", [P, RING * 2 * D])
        prob = [sb(f"prob{z}", [P, P]) for z in range(3)]
        rowid = [sb(f"rowid{z}", [P, P], U32) for z in range(3)]
        mt = sb("mt", [H, CH], BF)
        m4 = sb("m4", [P, TI, H])
        bqs = sb("bqs", [P, 2])
        psum = ctx.enter_context(nc.psum_tensor("psum", [P, 8, 512], FP))
        scrq = nc.dram_tensor("scr_queries", (3, D, CH), BF).ap()
        scrk = nc.dram_tensor("scr_keys", (3, D, B * SP_), BF).ap()
        scr1 = nc.dram_tensor("scr_corr", (4, P, T + 16), FP).ap()
        scr2 = nc.dram_tensor("scr_roll", (B, H, 2 * T), FP).ap()
        scrv = nc.dram_tensor("scr_v", (B, SP_, D), FP).ap()

        def bank(i):
            return psum[:, i, :]

        ident = const[:, KC["ident"]]
        mask8 = const[:, KC["mask8"]]
        padrow = const[:, KC["padrow"]]
        iota8 = const[:, KC["iota8"]]
        selh = const[:, KC["selh"]].rearrange("p (a m) -> p a m", a=2)
        valid = const[0:1, KC["valid"]]

        def w(name, kt=KT, where=wattn, cols=AC):
            return where[:, cols[name]].rearrange("p (k n) -> p k n", k=kt)

        def keys(b):
            at = b * H * SP_ // 2
            return bufB[:, at:at + H * SP_ // 2].bitcast(BF).rearrange("p (h k) -> p h k", h=H)

        VA_AT = H * SP_
        QS_AT = VA_AT + 4 * 512
        QP_AT = QS_AT + H * CH // 2
        queries = bufB[:, QS_AT:QP_AT].bitcast(BF).rearrange("p (h n) -> p h n", h=H)
        qparts = bufB[:, QP_AT:QP_AT + 3 * CH].bitcast(BF).rearrange("p (z g n) -> p z g n", z=3, g=2)

        def vmain(b):
            return bufB[:, VA_AT + b * 512:VA_AT + (b + 1) * 512]

        def vrest(b):
            at = VA_AT + 1024 + b * 512
            return bufB[:, at:at + 512].rearrange("p (g n) -> p g n", g=G4)

        ld_const, ld_x0, ld_x, ld_ctx, ld_rope = (sem(s) for s in ("ld_const", "ld_x0", "ld_x", "ld_ctx", "ld_rope"))
        ld_attn = sem("ld_attn")
        ld_f0, ld_f1, ld_f2, ld_f3 = sem("ld_f0"), sem("ld_f1"), sem("ld_f2"), sem("ld_f3")
        ends = {e: sem(f"end_{e}") for e in ("pe", "act", "dve")}
        ld_late = sem("ld_late")
        fr_var, fr_std, fr_xn, fr_tp, fr_ev = (sem(s) for s in ("fr_var", "fr_std", "fr_xn", "fr_tp", "fr_ev"))
        kv_k, kv_kt, kv_v, kv_z, kv_m, kv_p, kv_wr, kv_rd = (
            sem(s) for s in ("kv_k", "kv_kt", "kv_v", "kv_z", "kv_m", "kv_p", "kv_wr", "kv_rd"))
        sk_q, sk_f, sk_p, sk_wr, sk_rd = (sem(s) for s in ("sk_q", "sk_f", "sk_p", "sk_wr", "sk_rd"))
        at_p1, at_mx, at_mt, at_mts, at_mr, at_s2, at_ex, at_pv = (
            sem(s) for s in ("at_p1", "at_mx", "at_mt", "at_mts", "at_mr", "at_s2", "at_ex", "at_pv"))
        at_ou, at_tt, at_on, at_tb, at_ot, at_wo, at_bo = (
            sem(s) for s in ("at_ou", "at_tt", "at_on", "at_tb", "at_ot", "at_wo", "at_bo"))
        tn_w, tn_z, tn_zs, tn_u, tn_nat, tn_tp, tn_ev = (
            sem(s) for s in ("tn_w", "tn_z", "tn_zs", "tn_u", "tn_nat", "tn_tp", "tn_ev"))
        f0_h, f0_r, f0_sq, f0_y, f0_x = (sem(s) for s in ("f0_h", "f0_r", "f0_sq", "f0_y", "f0_x"))
        f1_q, f1_qt, f1_sim, f1_tk, f1_g, f1_sg, f1_hm, f1_y = (
            sem(s) for s in ("f1_q", "f1_qt", "f1_sim", "f1_tk", "f1_g", "f1_sg", "f1_hm", "f1_y"))
        f1_sc, f1_se, f1_idx, f1_dot, f1_th, f1_acc = (
            sem(s) for s in ("f1_sc", "f1_se", "f1_idx", "f1_dot", "f1_th", "f1_acc"))
        gathered = [sem(f"gathered{i}") for i in range(RING // GRP)]
        f2_lg, f2_sc, f2_g, f2_sg, f2_hm, f2_y, f2_x = (
            sem(s) for s in ("f2_lg", "f2_sc", "f2_g", "f2_sg", "f2_hm", "f2_y", "f2_x"))
        f3_lg, f3_ls, f3_ex, f3_gt, f3_gp, f3_gs, f3_b, f3_y, f3_x = (
            sem(s) for s in ("f3_lg", "f3_ls", "f3_ex", "f3_gt", "f3_gp", "f3_gs", "f3_b", "f3_y", "f3_x"))
        k3_k, k3_kt, k3_v, k3_vs, k3_wr, k3_rd = (
            sem(s) for s in ("k3_k", "k3_kt", "k3_v", "k3_vs", "k3_wr", "k3_rd"))
        q3_q = sem("q3_q")
        co_c, co_s, co_wr, co_rd, co_m = (sem(s) for s in ("co_c", "co_s", "co_wr", "co_rd", "co_m"))
        tp_n, tp_e, tp_r, tp_wr, tp_rd = (sem(s) for s in ("tp_n", "tp_e", "tp_r", "tp_wr", "tp_rd"))
        o3_o, o3_s, o3_y, o3_x, o3_bo = (sem(s) for s in ("o3_o", "o3_s", "o3_y", "o3_x", "o3_bo"))
        own_dve, own_act, own_pool = sem("own_dve"), sem("own_act"), sem("own_pool")
        stored, end_pool = sem("stored"), sem("end_pool")

        block = ctx.enter_context(nc.Block())

        def normed(f):
            kind, _, c = phases[fronts[f]]
            return xg[c % 3] if kind == "ffn1" else xa

        def enter(eng, me, n):
            if n:
                for e, s in ends.items():
                    if e != me:
                        eng.wait_ge(s, n)

        def leave(eng, me):
            eng.drain().then_inc(ends[me], 1)

        def after_phase(kind, layer):
            name = f"attn{layer or 1}" if kind == "attn" else kind
            return STEPS[name][-1] if name in STEPS else 0

        class Gather:

            def __init__(self):
                self.named = self.taken = 0

            def take(self, count):
                first = self.taken
                self.taken = min(self.named, first + count)
                return range(first, self.taken)

            def rest(self, c):
                return self.take(max(0, (c + 1) * TI * NG - self.taken))

        class Own:

            def __init__(self, eng, s):
                self.eng, self.s, self.n = eng, s, 0

            def mark(self, ins):
                self.n += 1
                ins.then_inc(self.s, 1)

            def wait(self):
                self.eng.wait_ge(self.s, self.n)

            def link(self, ins):
                self.mark(ins)
                self.wait()

        def A(at, n):
            return bufA[:, at:at + n]

        probs = [A(2560 * i, 2560).rearrange("p (h n) -> p h n", h=5) for i in range(2)]
        oun = A(5120, 2048).rearrange("p (g n) -> p g n", g=G4)
        oden = A(7168, TI * H).rearrange("p (g i j) -> p g i j", g=G4, i=TI)
        onorm = A(0, 1024).rearrange("p (i n) -> p i n", i=TI)
        ot = A(1024, 1024).rearrange("p (g n) -> p g n", g=2)
        qf = A(7296, 1024).rearrange("p (g n) -> p g n", g=2)
        qsw = A(8320, 512)
        kts = A(0, 2 * B * SP_).rearrange("p (g b s) -> p g b s", g=2, b=B)
        ksw = A(1024, 2 * B * SP_).rearrange("p (g b s) -> p g b s", g=2, b=B)
        kparts = A(7296, 3 * B * SP_).bitcast(BF).rearrange("p (z g b s) -> p z g b s", z=3, g=2, b=B)
        rope = sb("rope", [P, max(RN, LN)])
        late = rope
        iota = late[:, LC["iota"]]
        ctxr = late[:, LC["ctxr"]].rearrange("p (k n) -> p k n", k=KT)
        fc_t = wf[:, 0:2048].rearrange("p (k n) -> p k n", k=KT)
        proj_t = wf[:, 2048:4096].rearrange("p (m n) -> p m n", m=8)
        raw0 = ringb[:, 0:F0N]
        fcnat = raw0[:, F0["fc"]].rearrange("p (m n) -> p m n", m=8)
        projnat = raw0[:, F0["proj"]].rearrange("p (o n) -> p o n", o=2)
        utg = raw0[:, F0["ut"]]
        lowv = ringb[:, F0N:F0N + D]
        absum, hi_th, lo_th, sclip = (ringb[:, at:at + 10] for at in range(F0N + D, F0N + D + 40, 10))
        tplus, tminus = (ringb[:, at:at + HID0] for at in (F0N + D + 40, F0N + D + 40 + HID0))
        hid0 = A(0, 4096).rearrange("p (m n) -> p m n", m=8)

        def f0(name):
            return raw0[:, F0[name]]

        def w1(name, kt=KT):
            return w(name, kt, wf, F1)

        q1 = A(0, 1024).rearrange("p (g n) -> p g n", g=2)
        sg1 = A(1024, 1024).rearrange("p (g n) -> p g n", g=2)
        hm1 = A(2048, 2048).rearrange("p (m n) -> p m n", m=4)
        topv = A(4096, 256).rearrange("p (a r k) -> p a r k", a=2, k=TOPK)
        topi = A(4352, 256).bitcast(U32).rearrange("p (a r k) -> p a r k", a=2, k=TOPK)
        topf = A(4608, 256).rearrange("p (a r k) -> p a r k", a=2, k=TOPK)
        sums = A(4864, 1024).rearrange("p (r i j) -> p r i j", r=16, i=TOPK)
        best = A(6912, 128).rearrange("p (r k) -> p r k", r=16)
        pos = A(0, 128).bitcast(U32)
        pside = [A(128 + 128 * z, 128).bitcast(U32) for z in range(2)]
        psidef = [A(384 + 128 * z, 128) for z in range(2)]
        pick = [A(640 + 128 * z, 128) for z in range(2)]
        rowf = A(896, 128)
        eq = [A(4864 + 1024 * z, 1024).rearrange("p (r k j) -> p r k j", r=16, k=TOPK) for z in range(2)]
        ex1 = A(7040, 128)
        esum, erec = A(7168, 16), A(7184, 16)
        dots, thalf, ew = (sb(s, [P, 4, GRP]) for s in ("dots", "thalf", "ew"))
        ring = ringb[:, :].rearrange("p (s n) -> p s n", s=RING)

        def w2(name, kt=KT):
            return w(name, kt, wf, F2)

        sg2 = A(0, 1024).rearrange("p (g n) -> p g n", g=2)
        hm2 = A(1024, 5120).rearrange("p (m n) -> p m n", m=M2)
        sc2 = A(6144, 32)
        tv2 = A(6176, 32).rearrange("p (i k) -> p i k", i=TI)
        ti2 = A(6208, 32).bitcast(U32).rearrange("p (i k) -> p i k", i=TI)
        tf2 = A(6240, 32).rearrange("p (i k) -> p i k", i=TI)
        s2 = [A(6272 + 8 * z, 4) for z in range(4)]
        comb2 = [A(6304 + 32 * z, 32).rearrange("p (i e) -> p i e", i=TI) for z in range(3)]

        def w3(name, kt=KT):
            return w(name, kt, wf, F3)

        ex3 = A(0, 32)
        mx3 = A(64, 4)
        tv3 = A(96, 32).rearrange("p (i k) -> p i k", i=TI)
        ti3 = A(128, 32).bitcast(U32).rearrange("p (i k) -> p i k", i=TI)
        tf3 = A(160, 32).rearrange("p (i k) -> p i k", i=TI)
        pr3 = A(192, 32)
        s3 = [A(224 + 8 * z, 4) for z in range(4)]
        comb3 = [A(256 + 32 * z, 32).rearrange("p (i e) -> p i e", i=TI) for z in range(3)]
        gate3 = A(256, 32)
        gatet = A(512, 512)

        k3t = A(0, 2 * B * SP_).rearrange("p (g n) -> p g n", g=2)
        v3m, v3r = (ringb[:, at:at + 512].rearrange("p (b n) -> p b n", b=B) for at in (7168, 7680))
        v3s = ringb[:, 8192:8192 + 4 * U * 16].rearrange("p (a u d) -> p a u d", a=4, u=U)
        qx = A(0, 2 * EXT).rearrange("p (g n) -> p g n", g=2)
        c1 = [ringb[:, 1040 * g:1040 * (g + 1)] for g in range(2)]
        c2 = [ringb[:, 2080 + T * a:2080 + T * (a + 1)] for a in range(4)]
        cor = A(6816, T)
        ot3 = A(4768, 2048).rearrange("p (g n) -> p g n", g=2)
        topw, topj, topjf, rsum3 = A(7840, 8), A(7848, 8).bitcast(U32), A(7856, 8), A(7864, 8)
        topm = A(7872, 8)
        rollw, rollt = ringb[:, 6176:6176 + T], [ringb[:, 6176 + (1 + z) * T:6176 + (2 + z) * T] for z in range(2)]

        def kst(b, g):
            return bufB[:, (2 * b + g) * U * P:(2 * b + g + 1) * U * P].rearrange("p (u n) -> p u n", u=U)

        def vst(b, g):
            at = 4 * U * P + (2 * b + g) * U * P
            return bufB[:, at:at + U * P].rearrange("p (u n) -> p u n", u=U)

        def roll(a):
            at = 2400 + a * (T + SP_) if a < 2 else (a - 2) * (T + SP_)
            return A(at, T + SP_)


        @block.tensor
        def _(eng):
            mm = eng.matmul

            def front(f):
                if f is None:
                    return
                eng.wait_ge(fr_xn, TI * (f + 1))
                if f:
                    eng.wait_ge(fr_ev, KT * f)
                if stacks_before(f):
                    eng.wait_ge(sk_p, stacks_before(f))
                for kt in range(KT):
                    for i in range(TI):
                        ins = eng.transpose(psum[:, 6 + kt, i * P:(i + 1) * P], normed(f)[:, i, kt * P:(kt + 1) * P], ident)
                    ins.then_inc(fr_tp, 1)

            def stack(n):
                if n is None:
                    return
                f = front_of[n]
                eng.wait_ge(fr_ev, KT * (f + 1))
                for g in range(2):
                    for kt in range(KT):
                        ins = mm(bank(6 + g), w("wq")[:, kt, g * P:(g + 1) * P], xt[:, kt, :], start=kt == 0, stop=kt == KT - 1)
                ins.then_inc(sk_q, 1)

            def kv(n, layer):
                enter(eng, "pe", n)
                eng.wait_ge(ld_const, 16)
                eng.wait_ge(ld_ctx, 16)
                eng.wait_ge(ld_attn, 16 * (layer + 1))
                for g in range(2):
                    for kt in range(KT):
                        ins = mm(psum[:, g, 0:B * S], w("wk")[:, kt, g * P:(g + 1) * P], ctxt[:, kt, :],
                                 start=kt == 0, stop=kt == KT - 1)
                ins.then_inc(kv_k, 1)
                bias = wattn[0:1, AC["bv"]]
                for b in range(B):
                    o = psum[:, 4 + b, 0:D]
                    for kt in range(KT):
                        mm(o, ctxt[:, kt, b * S:b * S + P], w("wv")[:, kt, :], start=kt == 0, stop=False)
                    mm(o, valid[:, 0:P], bias, start=False, stop=True)
                    for j in range(4):
                        o = psum[32 * j:32 * j + SR, 4 + b, D:2 * D]
                        for kt in range(KT):
                            mm(o, ctxt[:, kt, b * S + P:(b + 1) * S], w("wv")[:, kt, :], start=kt == 0, stop=False)
                        ins = mm(o, valid[:, 0:SR], bias, start=False, stop=True)
                ins.then_inc(kv_v, 1)
                if n == 0:
                    front(0)
                stack(stack_of(n))

            def attn(n, layer, c):
                k, b = instance(n), c // 2
                enter(eng, "pe", n)
                eng.wait_ge(kv_rd, 16 * B * NB * (layer + 1))
                eng.wait_ge(sk_rd, 16 * NB * (k + 1))
                for u, (i, h0, h1) in enumerate(MAX_UNITS):
                    pair = 2 * (u % 3)
                    if u >= 3:
                        eng.wait_ge(at_mx, NU * k + u - 2)
                    for h in range(h0, h1):
                        z, at = (h - h0) // 3, (h - h0) % 3 * S
                        ins = mm(psum[:, pair + z, at:at + S], queries[0:MROW, h, i * P:(i + 1) * P], keys(b)[0:MROW, h, 0:S],
                                 start=True, stop=True)
                    ins.then_inc(at_p1, 1)
                eng.wait_ge(at_mx, NU * (k + 1))
                for i in range(TI):
                    ins = eng.transpose(psum[0:H, 0, i * P:(i + 1) * P], m4[:, i, :], ident)
                ins.then_inc(at_mt, 1)
                eng.wait_ge(at_mts, k + 1)
                eng.wait_ge(at_mr, 16 * (k + 1))

                def weigh(G):
                    eng.wait_ge(at_ex, 12 * k + 3 * G + 3)
                    if G:
                        eng.wait_ge(at_ou, 4 * k + G)
                    p = probs[G % 2]
                    mm(bank(5), vrest(b)[:, G, :], p[:, 4, :], start=True, stop=False, skip_group_check=True)
                    for j in range(4):
                        h = 4 * G + j
                        ins = mm(psum[32 * j:32 * j + 32, 5, :], vmain(b)[:, h * 32:h * 32 + 32], p[:, j, :],
                                 start=False, stop=True, skip_group_check=True)
                    ins.then_inc(at_pv, 1)

                for G in range(G4):
                    for a in range(2):
                        if G:
                            eng.wait_ge(at_ex, 12 * k + 3 * (G - 1) + a + 1)
                        for z in range(2):
                            ins = mm(bank(2 * a + z), keys(b)[0:MROW + 1, 4 * G + 2 * a + z, 0:P],
                                     queries[0:MROW + 1, 4 * G + 2 * a + z, :], start=True, stop=True)
                        ins.then_inc(at_s2, 1)
                    if G:
                        eng.wait_ge(at_ex, 12 * k + 3 * G)
                    for j in range(4):
                        ins = mm(psum[32 * j:32 * j + 32, 4, :], keys(b)[0:MROW + 1, 4 * G + j, P:SP_],
                                 queries[0:MROW + 1, 4 * G + j, :], start=True, stop=True, skip_group_check=True)
                    ins.then_inc(at_s2, 1)
                    if G:
                        weigh(G - 1)
                    if G == 0 and not is_tail(n):
                        front(next_front(n))
                    if G == 1:
                        stack(stack_of(n))
                weigh(G4 - 1)
                for G in range(G4):
                    eng.wait_ge(at_ou, 4 * k + G + 1)
                    for i in range(TI):
                        ins = eng.transpose(psum[:, G, i * P:(i + 1) * P], oun[:, G, i * P:(i + 1) * P], ident)
                    ins.then_inc(at_tt, 1)
                for g in range(2):
                    eng.wait_ge(at_on, 4 * k + 2 * g + 2)
                    for i in range(TI):
                        ins = eng.transpose(psum[:, 4 + g, i * P:(i + 1) * P], onorm[:, i, g * P:(g + 1) * P], ident)
                    ins.then_inc(at_tb, 1)
                eng.wait_ge(at_ot, 2 * (k + 1))
                for i in range(TI):
                    for g in range(2):
                        ins = mm(psum[:, i, 0:D], ot[:, g, i * P:(i + 1) * P], w("wo")[:, g, :],
                                 start=g == 0, stop=g == 1 and layer != 1)
                    if layer == 1:
                        ins = mm(psum[:, i, 0:D], valid[:, 0:P], wattn[0:1, AC["bo"]], start=False, stop=True)
                    ins.then_inc(at_wo, 1)
                if is_tail(n):
                    front(next_front(n))

            def tern(n):
                enter(eng, "pe", n)
                eng.wait_ge(ld_f0, 16)
                eng.wait_ge(tn_w, 1)
                mm(psum[0:RANK, 0, 0:D], f0("fbt")[0:RANK, :], f0("v")[0:RANK, :], start=True, stop=True).then_inc(tn_z, 1)
                eng.wait_ge(tn_zs, 1)
                for m in range(8):
                    if m >= 2:
                        eng.wait_ge(tn_nat, m - 1)
                    mm(psum[:, 1 + m % 2, 0:D], utg[0:RANK, m * P:(m + 1) * P], lowv[0:RANK, :],
                       start=True, stop=True).then_inc(tn_u, 1)
                eng.wait_ge(tn_nat, 8)
                for t in range(8):
                    if t >= 2:
                        eng.wait_ge(tn_ev, t - 1)
                    for z in range(4):
                        if t < 4:
                            kt, m = t // 2, 4 * (t % 2) + z
                            src = fcnat[:, m, kt * P:(kt + 1) * P]
                        else:
                            mo = 4 * (t - 4) + z
                            m, o = mo // 2, mo % 2
                            src = projnat[:, o, m * P:(m + 1) * P]
                        ins = eng.transpose(psum[:, 4 + t % 2, z * P:(z + 1) * P], src, ident)
                    ins.then_inc(tn_tp, 1)

            def ffn0(n, c):
                k, x = instance(n), xt
                enter(eng, "pe", n)
                eng.wait_ge(fr_ev, KT * (front_of[n] + 1))
                for m in range(8):
                    if m >= 4:
                        eng.wait_ge(f0_r, 8 * k + m - 3)
                    for kt in range(KT):
                        ins = mm(bank(m % 4), fc_t[:, kt, m * P:(m + 1) * P], x[:, kt, :], start=kt == 0, stop=kt == KT - 1)
                    ins.then_inc(f0_h, 1)
                front(next_front(n))
                stack(stack_of(n))
                eng.wait_ge(f0_sq, 8 * k + 8)
                for i in range(TI):
                    if i >= 2:
                        eng.wait_ge(f0_x, 4 * k + i - 1)
                    for m in range(8):
                        ins = mm(psum[:, 4 + i % 2, 0:D], hid0[:, m, i * P:(i + 1) * P], proj_t[:, m, :], start=m == 0, stop=m == 7)
                    ins.then_inc(f0_y, 1)

            def ffn1(n, c):
                k, x = instance(n), xt
                enter(eng, "pe", n)
                eng.wait_ge(ld_f1, 16)
                eng.wait_ge(fr_ev, KT * (front_of[n] + 1))
                for p in range(2):
                    for kt in range(KT):
                        ins = mm(bank(p), w1("wq")[:, kt, p * P:(p + 1) * P], x[:, kt, :], start=kt == 0, stop=kt == KT - 1)
                    ins.then_inc(f1_q, 1)
                eng.wait_ge(f1_qt, 2 * k + 2)

                def similarities(i):
                    if i >= 2:
                        eng.wait_ge(f1_tk, 4 * k + i - 1)
                    for p in range(2):
                        ins = mm(bank(2 * (i % 2) + p), q1[:, p, i * P:(i + 1) * P], w1("keys")[:, p, :], start=True, stop=True)
                    ins.then_inc(f1_sim, 1)

                similarities(0)
                similarities(1)
                for m in range(4):
                    if m:
                        eng.wait_ge(f1_hm, 4 * k + m)
                    for r, name in enumerate(("wg", "wu")):
                        for kt in range(KT):
                            ins = mm(bank(4 + r), w1(name)[:, kt, m * P:(m + 1) * P], x[:, kt, :], start=kt == 0, stop=kt == KT - 1)
                    ins.then_inc(f1_g, 1)
                    if m < 2:
                        similarities(m + 2)
                front(next_front(n))
                stack(stack_of(n))
                eng.wait_ge(f1_tk, 4 * k + 4)
                eng.wait_ge(f1_hm, 4 * k + 4)
                for i in range(TI):
                    for m in range(4):
                        ins = mm(psum[:, i, 0:D], hm1[:, m, i * P:(i + 1) * P], w1("wd", 4)[:, m, :], start=m == 0, stop=m == 3)
                    ins.then_inc(f1_y, 1)

            def ffn2(n, c):
                k, x = instance(n), xt
                enter(eng, "pe", n)
                eng.wait_ge(ld_f2, 16)
                eng.wait_ge(fr_ev, KT * (front_of[n] + 1))
                for i in range(TI):
                    for kt in range(KT):
                        ins = mm(psum[:, 5, i * E2:(i + 1) * E2], x[:, kt, i * P:(i + 1) * P], w2("gate")[:, kt, :],
                                 start=kt == 0, stop=kt == KT - 1)
                ins.then_inc(f2_lg, 1)
                gu = w2("gu").rearrange("p k (m r n) -> p k m r n", m=M2, r=2)
                for m in range(M2):
                    if m >= 2:
                        eng.wait_ge(f2_hm, M2 * k + m - 1)
                    for r in range(2):
                        for kt in range(KT):
                            ins = mm(bank(2 * (m % 2) + r), gu[:, kt, m, r, :], x[:, kt, :], start=kt == 0, stop=kt == KT - 1)
                    ins.then_inc(f2_g, 1)
                front(next_front(n))
                stack(stack_of(n))
                eng.wait_ge(f2_hm, M2 * (k + 1))
                down = w2("down", M2)
                for y in range(TI * 9):
                    i, e = y // 9, y % 9
                    if y >= 5:
                        eng.wait_ge(f2_x, TI * 9 * k + y - 4)
                    ms = (8, 9) if e == 8 else (e,)
                    for m in ms:
                        ins = mm(psum[:, y % 5, 0:D], hm2[:, m, i * P:(i + 1) * P], down[:, m, :], start=m == ms[0], stop=m == ms[-1])
                    ins.then_inc(f2_y, 1)

            def ffn3(n, c):
                k, x = instance(n), xt
                enter(eng, "pe", n)
                eng.wait_ge(ld_f3, 16)
                eng.wait_ge(fr_ev, KT * (front_of[n] + 1))
                for i in range(TI):
                    for kt in range(KT):
                        ins = mm(psum[:, 5, i * E3:(i + 1) * E3], x[:, kt, i * P:(i + 1) * P], w3("gate")[:, kt, :],
                                 start=kt == 0, stop=kt == KT - 1)
                ins.then_inc(f3_lg, 1)
                for y in range(TI * 4):
                    i, e = y // 4, y % 4
                    if y >= 4:
                        eng.wait_ge(f3_x, TI * 4 * k + y - 3)
                    for kt in range(KT):
                        ins = mm(bank(y % 4), x[:, kt, i * P:(i + 1) * P], w3("we")[:, kt, e * 512:(e + 1) * 512],
                                 start=kt == 0, stop=kt == KT - 1)
                    ins.then_inc(f3_y, 1)
                    if y == 3:
                        eng.wait_ge(f3_gt, k + 1)
                        for t in range(TI):
                            ins = eng.transpose(psum[0:E3, 4, t * P:(t + 1) * P], gate3[:, t * E3:(t + 1) * E3], ident)
                        ins.then_inc(f3_gp, 1)
                    if y == 4 * TI - 5:
                        eng.wait_ge(f3_gs, k + 1)
                        for t in range(TI):
                            ins = mm(psum[:, 4 + t // 2, (t % 2) * D:(t % 2 + 1) * D], gatet[0:E3, t * P:(t + 1) * P],
                                     wf[0:E3, F3["be"]], start=True, stop=True)
                        ins.then_inc(f3_b, 1)
                front(next_front(n))

            def kv3(n):
                enter(eng, "pe", n)
                eng.wait_ge(ld_attn, 16 * 4)
                eng.wait_ge(ld_late, 16)
                for g in range(2):
                    for kt in range(KT):
                        ins = mm(psum[:, g, 0:B * S], w("wk", KT, wattn, CC)[:, kt, g * P:(g + 1) * P], ctxt[:, kt, :],
                                 start=kt == 0, stop=kt == KT - 1)
                ins.then_inc(k3_k, 1)
                for b in range(B):
                    for r, (a, z) in enumerate(((0, P), (P, SP_))):
                        o = psum[0:z - a, 2 + b, r * D:(r + 1) * D]
                        for kt in range(KT):
                            mm(o, ctxr[:, kt, b * SP_ + a:b * SP_ + z], w("wv", KT, wattn, CC)[:, kt, :], start=kt == 0, stop=False)
                        ins = mm(o, valid[:, a:z], wattn[0:1, CC["bv"]], start=False, stop=True)
                ins.then_inc(k3_v, 1)

            def q3(n, c):
                k, x = instance(n), xt
                enter(eng, "pe", n)
                eng.wait_ge(fr_ev, KT * (front_of[n] + 1))
                for g in range(2):
                    for kt in range(KT):
                        ins = mm(bank(g), w("wq", KT, wattn, CC)[:, kt, g * P:(g + 1) * P], x[:, kt, :], start=kt == 0, stop=kt == KT - 1)
                ins.then_inc(q3_q, 1)
                front(next_front(n))

            def top(b):
                eng.wait_ge(co_rd, 32 * (b + 1))
                for g in range(2):
                    for N in range(2):
                        ins = mm(psum[0:32, 6 + N, :], selh[:, g, :], c2[2 * b + g][:, N * 512:(N + 1) * 512], start=g == 0, stop=g == 1,
                                 skip_group_check=True)
                ins.then_inc(co_m, 1)

            def corr(n, b):
                enter(eng, "pe", n)
                if b:
                    top(b - 1)
                for g in range(2):
                    for N in range(2):
                        for u in range(U):
                            ins = mm(bank(2 * g + N), kst(b, g)[:, u, :], qx[:, g, 16 * u + N * 512:16 * u + N * 512 + 512],
                                     start=u == 0, stop=u == U - 1)
                    ins.then_inc(co_c, 1)

            def out3(n, b):
                enter(eng, "pe", n)
                eng.wait_ge(tp_rd, 32 * (b + 1))
                for g in range(2):
                    for N in range(2):
                        for u in range(U):
                            at = SP_ - 16 * u + N * 512
                            ins = mm(bank(2 * g + N), vst(b, g)[:, u, :], roll(2 * b + g)[:, at:at + 512],
                                     start=u == 0, stop=u == U - 1)
                        ins.then_inc(o3_o, 1)
                    if g == 0 and b < B - 1:
                        top(b + 1)
                front(next_front(n))
                eng.wait_ge(o3_s, 4 * b + 4)
                for i in range(8):
                    if i >= 2:
                        eng.wait_ge(o3_x, 8 * b + i - 1)
                    for g in range(2):
                        ins = mm(psum[:, 4 + i % 2, 0:D], ot3[:, g, i * P:(i + 1) * P], w("wo", KT, wattn, CC)[:, g, :],
                                 start=g == 0, stop=g == 1)
                    ins.then_inc(o3_y, 1)

            for n, (kind, layer, c) in enumerate(phases):
                {"kv": lambda: kv(n, layer), "attn": lambda: attn(n, layer, c), "tern": lambda: tern(n),
                 "ffn0": lambda: ffn0(n, c), "ffn1": lambda: ffn1(n, c), "ffn2": lambda: ffn2(n, c), "ffn3": lambda: ffn3(n, c),
                 "kv3": lambda: kv3(n), "q3": lambda: q3(n, c), "corr": lambda: corr(n, layer), "out3": lambda: out3(n, layer)}[kind]()
                leave(eng, "pe")

        @block.scalar
        def _(eng):
            act = eng.activation
            own = Own(eng, own_act)

            def front(f):
                if f is None:
                    return
                for kt in range(KT):
                    eng.wait_ge(fr_tp, KT * f + kt + 1)
                    act(xt[:, kt, :], bank(6 + kt), ACT.Copy).then_inc(fr_ev, 1)

            def stack(n):
                if n is None or phases[n][1] == 2:
                    return
                eng.wait_ge(sk_q, instance(n) + 1)
                eng.wait_ge(kv_wr, 16 * (phases[n][1] + 1))
                for g in range(2):
                    act(qf[:, g, :], bank(6 + g), ACT.Identity, bias=bqs[:, g:g + 1], scale=0.25).then_inc(sk_f, 1)
                    act(qparts[:, 0, g, :], bank(6 + g), ACT.Identity, bias=bqs[:, g:g + 1], scale=0.25).then_inc(sk_f, 1)

            gather = Gather()

            def gather_steps(groups):
                for g in groups:
                    eng.wait_ge(f1_dot, g + 1)
                    if g >= 4:
                        eng.wait_ge(f1_acc, g - 3)
                    act(thalf[:, g % 4, :], dots[:, g % 4, :], ACT.Tanh, scale=0.5).then_inc(f1_th, 1)

            def deviation(f):
                if f is None:
                    return
                kind, layer, c = phases[fronts[f]]
                if (kind, layer) == ("attn", 2):
                    gather_steps(gather.rest(c))
                if kind == "ffn1" and c >= 3:
                    gather_steps(gather.rest(c - 3))
                eng.wait_ge(fr_var, f + 1)
                act(stdev[:, :], vare[:, :], ACT.Sqrt).then_inc(fr_std, 1)

            def kv(n, layer):
                enter(eng, "act", n)
                if n == 0:
                    deviation(0)
                eng.wait_ge(kv_k, layer + 1)
                for g in range(2):
                    act(kts[:, g, :, 0:S], psum[:, g, 0:B * S].rearrange("p (b s) -> p b s", b=B), ACT.Identity,
                        bias=wattn[:, AC["bk"].start + g:AC["bk"].start + g + 1]).then_inc(kv_kt, 1)
                if layer < 2:
                    own.link(act(bqs[:, :], wattn[:, AC["bq"]], ACT.Copy, scale=0.25))
                gather_steps(gather.take(STEPS["kv"][0]))
                if n == 0:
                    front(0)
                stack(stack_of(n))
                gather_steps(gather.take(STEPS["kv"][1]))

            def attn(n, layer, c):
                k = instance(n)
                enter(eng, "act", n)
                gather_steps(gather.take(STEPS[f"attn{layer or 1}"][0]))
                eng.wait_ge(at_mt, k + 1)
                act(mt[0:H, :], psum[0:H, 0, :], ACT.Copy).then_inc(at_mts, 1)
                if not is_tail(n):
                    deviation(next_front(n))
                before = gather.take(STEPS[f"attn{layer or 1}"][1])

                def unload(G):
                    eng.wait_ge(at_pv, 4 * k + G + 1)
                    act(oun[:, G, :], bank(5), ACT.Copy).then_inc(at_ou, 1)

                for G in range(G4):
                    p = probs[G % 2]
                    if G >= 2:
                        eng.wait_ge(at_pv, 4 * k + G - 1)
                    for a in range(2):
                        eng.wait_ge(at_s2, 12 * k + 3 * G + a + 1)
                        act(p[:, 2 * a:2 * a + 2, :], psum[:, 2 * a:2 * a + 2, :], ACT.Exp).then_inc(at_ex, 1)
                    eng.wait_ge(at_s2, 12 * k + 3 * G + 3)
                    act(p[:, 4, :], bank(4), ACT.Exp, bias=padrow).then_inc(at_ex, 1)
                    if G:
                        unload(G - 1)
                    if G == 0:
                        if not is_tail(n):
                            front(next_front(n))
                        gather_steps(before[0:1])
                    if G == 1:
                        gather_steps(before[1:])
                        stack(stack_of(n))
                        after_ = gather.take(STEPS[f"attn{layer or 1}"][2])
                    if G == 2:
                        gather_steps(after_[0:1])
                unload(G4 - 1)
                gather_steps(after_[1:])
                gather_steps(gather.take(STEPS[f"attn{layer or 1}"][3]))
                for g in range(2):
                    eng.wait_ge(at_tb, 2 * k + g + 1)
                    act(ot[:, g, :], bank(4 + g), ACT.Copy).then_inc(at_ot, 1)
                gather_steps(gather.take(STEPS[f"attn{layer or 1}"][4]))
                if is_tail(n):
                    deviation(next_front(n))
                    front(next_front(n))
                gather_steps(gather.take(STEPS[f"attn{layer or 1}"][5]))

            def tern(n):
                enter(eng, "act", n)
                eng.wait_ge(tn_z, 1)
                act(lowv[0:RANK, :], psum[0:RANK, 0, 0:D], ACT.Copy).then_inc(tn_zs, 1)
                for t in range(8):
                    eng.wait_ge(tn_tp, t + 1)
                    if t < 4:
                        kt, m = t // 2, 4 * (t % 2)
                        dst = fc_t[:, kt, m * P:(m + 4) * P]
                    else:
                        m = 2 * (t - 4)
                        dst = proj_t[:, m:m + 2, :].rearrange("p m n -> p (m n)")
                    act(dst, bank(4 + t % 2), ACT.Copy).then_inc(tn_ev, 1)

            def ffn0(n, c):
                k = instance(n)
                enter(eng, "act", n)
                deviation(next_front(n))
                for m in range(8):
                    eng.wait_ge(f0_h, 8 * k + m + 1)
                    act(hid0[:, m, :], bank(m % 4), ACT.Relu).then_inc(f0_r, 1)
                front(next_front(n))
                stack(stack_of(n))

            def ffn1(n, c):
                k = instance(n)
                enter(eng, "act", n)
                deviation(next_front(n))
                for p in range(2):
                    eng.wait_ge(f1_q, 2 * k + p + 1)
                    act(q1[:, p, :], bank(p), ACT.Copy).then_inc(f1_qt, 1)
                gather_steps(gather.take(STEPS["ffn1"][0]))
                for m in range(4):
                    eng.wait_ge(f1_g, 4 * k + m + 1)
                    act(sg1[:, m % 2, :], bank(4), ACT.Silu).then_inc(f1_sg, 1)
                    if m == 1:
                        gather_steps(gather.take(STEPS["ffn1"][1]))
                gather_steps(gather.take(STEPS["ffn1"][2]))
                front(next_front(n))
                eng.wait_ge(f1_sc, k + 1)
                act(ex1[:, :], ex1[:, :], ACT.Exp).then_inc(f1_se, 1)
                stack(stack_of(n))
                gather_steps(gather.take(STEPS["ffn1"][3]))
                gather_steps(gather.take(STEPS["ffn1"][4]))
                gather.named += TI * NG
                gather_steps(gather.take(STEPS["ffn1"][5]))

            def ffn2(n, c):
                k = instance(n)
                enter(eng, "act", n)
                eng.wait_ge(f2_lg, k + 1)
                act(sc2[:, :], psum[:, 5, 0:TI * E2], ACT.Sigmoid).then_inc(f2_sc, 1)
                gather_steps(gather.take(STEPS["ffn2"][0]))
                for m in range(M2):
                    eng.wait_ge(f2_g, M2 * k + m + 1)
                    if m >= 2:
                        eng.wait_ge(f2_hm, M2 * k + m - 1)
                    act(sg2[:, m % 2, :], bank(2 * (m % 2)), ACT.Silu).then_inc(f2_sg, 1)
                    if m:
                        gather_steps(gather.take(STEPS["ffn2"][1][m - 1]))
                gather_steps(gather.take(STEPS["ffn2"][1][M2 - 1]))
                deviation(next_front(n))
                front(next_front(n))
                gather_steps(gather.take(STEPS["ffn2"][3]))
                stack(stack_of(n))
                for _ in range(TI):
                    gather_steps(gather.take(STEPS["ffn2"][2]))

            def ffn3(n, c):
                k = instance(n)
                enter(eng, "act", n)
                deviation(next_front(n))
                eng.wait_ge(f3_ls, k + 1)
                act(ex3[:, :], ex3[:, :], ACT.Exp).then_inc(f3_ex, 1)
                eng.wait_ge(f3_gp, k + 1)
                act(gatet[0:E3, :], psum[0:E3, 4, :], ACT.Copy).then_inc(f3_gs, 1)
                front(next_front(n))

            def kv3(n):
                enter(eng, "act", n)
                eng.wait_ge(k3_k, 1)
                for g in range(2):
                    for b in range(B):
                        act(k3t[:, g, b * SP_:b * SP_ + S], psum[:, g, b * S:(b + 1) * S], ACT.Identity,
                            bias=wattn[:, CC["bk"].start + g:CC["bk"].start + g + 1]).then_inc(k3_kt, 1)
                eng.wait_ge(k3_v, 1)
                for b in range(B):
                    act(v3m[:, b, :], psum[:, 2 + b, 0:D], ACT.Copy).then_inc(k3_vs, 1)
                    act(v3r[0:32, b, :], psum[0:32, 2 + b, D:2 * D], ACT.Copy).then_inc(k3_vs, 1)

            def q3(n, c):
                k = instance(n)
                enter(eng, "act", n)
                deviation(next_front(n))
                eng.wait_ge(q3_q, k + 1)
                at = (c % 2) * CH
                for g in range(2):
                    bias = wattn[:, CC["bq"].start + g:CC["bq"].start + g + 1]
                    act(qx[:, g, at:at + CH], bank(g), ACT.Identity, bias=bias)
                    if c % 2 == 0:
                        act(qx[:, g, T:EXT], psum[:, g, 0:SP_], ACT.Identity, bias=bias)
                front(next_front(n))

            def top(b):
                eng.wait_ge(tp_n, b + 1)
                act(topw[0:H, 0:8], topw[0:H, 0:8], ACT.Exp).then_inc(tp_e, 1)

            def corr(n, b):
                enter(eng, "act", n)
                if b:
                    eng.wait_ge(co_wr, 32 * b)
                    top(b - 1)
                for g in range(2):
                    eng.wait_ge(co_c, 2 * b + g + 1)
                    act(c1[g][:, 0:T], psum[:, 2 * g:2 * g + 2, :].rearrange("p a n -> p (a n)"), ACT.Copy).then_inc(co_s, 1)
                    act(c1[g][:, T:T + 16], psum[:, 2 * g, 0:16], ACT.Copy).then_inc(co_s, 1)

            def out3(n, b):
                enter(eng, "act", n)
                deviation(next_front(n))
                for g in range(2):
                    for N in range(2):
                        eng.wait_ge(o3_o, 4 * b + 2 * g + N + 1)
                        act(ot3[:, g, N * 512:(N + 1) * 512], bank(2 * g + N), ACT.Copy).then_inc(o3_s, 1)
                    if g == 0 and b < B - 1:
                        top(b + 1)
                front(next_front(n))

            for n, (kind, layer, c) in enumerate(phases):
                {"kv": lambda: kv(n, layer), "attn": lambda: attn(n, layer, c), "tern": lambda: tern(n),
                 "ffn0": lambda: ffn0(n, c), "ffn1": lambda: ffn1(n, c), "ffn2": lambda: ffn2(n, c), "ffn3": lambda: ffn3(n, c),
                 "kv3": lambda: kv3(n), "q3": lambda: q3(n, c), "corr": lambda: corr(n, layer), "out3": lambda: out3(n, layer)}[kind]()
                leave(eng, "act")
                gather_steps(gather.take(after_phase(kind, layer)))

        @block.vector
        def _(eng):
            own = Own(eng, own_dve)
            tt, ts, stt = eng.tensor_tensor, eng.tensor_scalar, eng.scalar_tensor_tensor

            def cast(ap, shape):
                return ap.broadcast_to(shape)

            gather, added = Gather(), []

            def dot(g, j):
                c, i = g // (TI * NG), g // NG % TI
                row = ring[:, GRP * (g % (RING // GRP)) + j, 0:D]
                return eng.tensor_tensor_reduce(row, xg[c % 3][:, i, :], row, 1.0, 0.0, ALU.mult, ALU.add, dots[:, g % 4, j:j + 1])

            def add_row(g, j):
                x = x_sb[:, g // NG, :]
                return stt(x, ring[:, GRP * (g % (RING // GRP)) + j, D:2 * D], ew[:, g % 4, j:j + 1], x, ALU.mult, ALU.add)

            def step(g, more):
                c, s, at = g // (TI * NG), g % 4, g % (TI * NG) * GRP
                eng.wait_ge(f1_th, g + 1)
                own.mark(stt(ew[:, s, :], dots[:, s, :], 0.5, prob[c % 3][:, at:at + GRP], ALU.mult, ALU.mult))
                if more:
                    dot(g + 1, 0)
                own.wait()
                own.mark(stt(ew[:, s, :], thalf[:, s, :], 1.0, ew[:, s, :], ALU.add, ALU.mult))
                if more:
                    dot(g + 1, 1)
                if g:
                    eng.wait_ge(f1_acc, g)
                own.wait()
                own.mark(add_row(g, 0))
                if more:
                    dot(g + 1, 2)
                own.wait()
                own.mark(add_row(g, 1))
                if more:
                    dot(g + 1, 3).then_inc(f1_dot, 1)
                own.wait()
                own.link(add_row(g, 2))
                add_row(g, 3).then_inc(f1_acc, 1)
                added.append(g)

            def gather_steps(groups):
                for g in groups:
                    eng.wait_ge(gathered[g % (RING // GRP)], 16 * GRP * (g // (RING // GRP) + 1))
                    if g > len(added):
                        step(g - 1, True)
                    else:
                        for j in range(GRP):
                            ins = dot(g, j)
                        ins.then_inc(f1_dot, 1)

            def gather_all(c):
                if c < 0:
                    return
                gather_steps(gather.rest(c))
                if len(added) < (c + 1) * TI * NG:
                    step(len(added), False)
                eng.wait_ge(f1_acc, (c + 1) * TI * NG)

            def front(f):
                if f is None:
                    return
                kind, layer, c = phases[fronts[f]]
                if (kind, layer) == ("attn", 2):
                    gather_all(c)
                if kind == "ffn1":
                    gather_all(c - 3)
                if f == 1:
                    eng.wait_ge(ld_x, 16)
                for i in range(TI):
                    own.mark(eng.bn_stats(stats[:, i, :], x_sb[:, c * TI + i, :]))
                own.wait()
                for i in range(TI):
                    own.mark(eng.bn_aggr(mv[:, i, :], stats[:, i, :]))
                own.wait()
                ts(vare[:, :], mv[:, :, 1], EPS, None, ALU.add).then_inc(fr_var, 1)
                eng.wait_ge(fr_std, f + 1)
                own.link(eng.reciprocal(rstd[:, :], stdev[:, :]))
                own.link(tt(newton[:, :], rstd[:, :], rstd[:, :], ALU.mult))
                own.link(stt(newton[:, :], newton[:, :], -0.5, vare[:, :], ALU.mult, ALU.mult))
                own.link(stt(rstd[:, :], newton[:, :], 1.5, rstd[:, :], ALU.add, ALU.mult))
                if f:
                    eng.wait_ge(fr_tp, KT * f)
                for i in range(TI):
                    ts(normed(f)[:, i, :], x_sb[:, c * TI + i, :], mv[:, i, 0:1], rstd[:, i:i + 1], ALU.subtract, ALU.mult)\
                        .then_inc(fr_xn, 1)

            def add_x(c, i, src):
                return tt(x_sb[:, c * TI + i, :], x_sb[:, c * TI + i, :], src, ALU.add)

            def split(src, parts):
                own.link(tt(src, src, parts[0], ALU.subtract))
                own.link(eng.tensor_copy(parts[1], src))
                return tt(parts[2], src, parts[1], ALU.subtract)

            def stack(n):
                if n is None:
                    return
                k, (_, layer, c) = instance(n), phases[n]
                if layer == 2:
                    eng.wait_ge(sk_q, k + 1)
                    eng.wait_ge(kv_wr, 16 * (layer + 1))
                    at = (c % 2) * CH
                    cos, sin = rope[:, at:at + CH], rope[:, T + at:T + at + CH]
                    for g in range(2):
                        own.mark(stt(qf[:, g, :], bank(6 + g), 0.25, cos, ALU.mult, ALU.mult))
                        own.link(eng.stream_shuffle(qsw, bank(6 + g), SWAP))
                        own.link(stt(qsw, qsw, 0.25, sin, ALU.mult, ALU.mult))
                        own.link(tt(qf[:, g, :], qf[:, g, :], qsw, ALU.add))
                    own.link(eng.tensor_copy(qparts[:, 0], qf))
                else:
                    eng.wait_ge(sk_f, 4 * (k + 1))
                split(qf, [qparts[:, z] for z in range(3)]).then_inc(sk_p, 1)

            def kv(n, layer):
                enter(eng, "dve", n)
                if n == 0:
                    eng.wait_ge(ld_x0, 16)
                    front(0)
                for b in range(B):
                    ins = eng.memset(keys(b)[96:P], -1.0)
                    own.mark(ins)
                own.mark(eng.memset(kts[:, :, :, S:SP_], 0.0))
                own.wait()
                eng.sem_inc(kv_m, 1)
                gather_steps(gather.take(STEPS["kv"][0]))
                eng.wait_ge(kv_kt, 2 * (layer + 1))
                if layer == 2:
                    eng.wait_ge(ld_rope, 16)
                    cos, sin = (cast(rope[:, a:a + S].unsqueeze(1), [P, B, S]) for a in (0, T))
                    own.link(eng.stream_shuffle(ksw.rearrange("p g b s -> p (g b s)"), kts.rearrange("p g b s -> p (g b s)"), SWAP))
                    for g in range(2):
                        own.mark(tt(kts[:, g, :, 0:S], kts[:, g, :, 0:S], cos, ALU.mult))
                        own.mark(tt(ksw[:, g, :, 0:S], ksw[:, g, :, 0:S], sin, ALU.mult))
                    own.wait()
                    own.link(tt(kts, kts, ksw, ALU.add))
                own.link(eng.tensor_copy(kparts[:, 0], kts))
                split(kts, [kparts[:, z] for z in range(3)]).then_inc(kv_p, 1)
                stack(stack_of(n))
                eng.wait_ge(kv_v, layer + 1)
                eng.wait_ge(kv_z, 1)
                for b in range(B):
                    eng.tensor_copy(vmain(b).rearrange("p (h n) -> p h n", h=H)[:, :, 0:DH],
                                    psum[:, 4 + b, 0:D].rearrange("p (h d) -> p h d", h=H))
                    for j in range(4):
                        r = slice(32 * j, 32 * j + SR)
                        eng.tensor_copy(vrest(b)[r, :, j * 32:j * 32 + DH],
                                        psum[r, 4 + b, D:2 * D].rearrange("p (g j d) -> p g j d", g=G4, j=4)[:, :, j, :])
                gather_steps(gather.take(STEPS["kv"][1]))

            def attn(n, layer, c):
                k = instance(n)
                enter(eng, "dve", n)
                for u, (i, h0, h1) in enumerate(MAX_UNITS):
                    pair, nh = 2 * (u % 3), h1 - h0
                    eng.wait_ge(at_p1, NU * k + u + 1)
                    if nh == 6:
                        eng.reduce_max(m4[:, i, h0:h1].rearrange("p (a b) -> p a b", a=2),
                                       psum[:, pair:pair + 2, 0:3 * S].rearrange("p a (b s) -> p a b s", b=3), AX.X).then_inc(at_mx, 1)
                    else:
                        own.mark(eng.reduce_max(m4[:, i, h0:h0 + 3], psum[:, pair, 0:3 * S].rearrange("p (b s) -> p b s", b=3), AX.X))
                        own.mark(eng.reduce_max(m4[:, i, h0 + 3:h1], psum[:, pair + 1, 0:(nh - 3) * S].rearrange("p (b s) -> p b s", b=nh - 3), AX.X))
                        own.wait()
                        eng.sem_inc(at_mx, 1)
                    if u == 5:
                        gather_steps(gather.take(STEPS[f"attn{layer or 1}"][0]))
                if not is_tail(n):
                    front(next_front(n))

                gather_steps(gather.take(STEPS[f"attn{layer or 1}"][1]))
                stack(stack_of(n))
                if layer == 0 and c == 0:
                    scales()
                if layer == 0 and c:
                    ternary(TERN_ROWS[c])
                gather_steps(gather.take(STEPS[f"attn{layer or 1}"][2]))
                for G in range(G4):
                    eng.wait_ge(at_tt, 4 * k + G + 1)
                    sums_and_values = psum[:, G, :].rearrange("p (i j n) -> p i j n", i=TI, j=4)
                    own.link(eng.reciprocal(oden[:, G], sums_and_values[:, :, :, DH]))
                    tt(onorm[:, :, G * 4 * DH:(G + 1) * 4 * DH].rearrange("p i (j d) -> p i j d", j=4), sums_and_values[:, :, :, 0:DH],
                       cast(oden[:, G].unsqueeze(3), [P, TI, 4, DH]), ALU.mult).then_inc(at_on, 1)
                    if G == 1:
                        gather_steps(gather.take(STEPS[f"attn{layer or 1}"][3]))
                gather_steps(gather.take(STEPS[f"attn{layer or 1}"][4]))
                if layer == 0:
                    eng.wait_ge(at_bo, k + 1)
                for i in range(TI):
                    eng.wait_ge(at_wo, 4 * k + i + 1)
                    own.mark(add_x(c, i, psum[:, i, 0:D]))
                if is_tail(n):
                    own.wait()
                    front(next_front(n))
                gather_steps(gather.take(STEPS[f"attn{layer or 1}"][5]))

            def scales():
                eng.wait_ge(ld_f0, 16)
                own.mark(eng.tensor_reduce(absum[:, 0:8], fcnat, AX.X, ALU.add, apply_absolute_value=True))
                own.link(eng.tensor_reduce(absum[:, 8:10], projnat, AX.X, ALU.add, apply_absolute_value=True))
                own.mark(ts(sclip[:, 0:8], absum[:, 0:8], 1.0 / D, 1e-5, ALU.mult, ALU.max))
                own.link(ts(sclip[:, 8:10], absum[:, 8:10], 1.0 / HID0, 1e-5, ALU.mult, ALU.max))
                own.mark(ts(hi_th, sclip, 0.5, None, ALU.mult))
                own.link(ts(lo_th, sclip, -0.5, None, ALU.mult))

            def ternary(rows):
                for r in rows:
                    nat, n_ = (fcnat[:, r, :], D) if r < 8 else (projnat[:, r - 8, :], HID0)
                    own.mark(ts(tplus[:, 0:n_], nat, hi_th[:, r:r + 1], sclip[:, r:r + 1], ALU.is_gt, ALU.mult))
                    own.link(ts(tminus[:, 0:n_], nat, lo_th[:, r:r + 1], sclip[:, r:r + 1], ALU.is_lt, ALU.mult))
                    own.link(tt(nat, tplus[:, 0:n_], tminus[:, 0:n_], ALU.subtract))

            def tern(n):
                enter(eng, "dve", n)
                ts(utg[0:RANK, :], utg[0:RANK, :], f0("gate")[0:RANK, :], None, ALU.mult).then_inc(tn_w, 1)
                for r in range(8):
                    eng.wait_ge(tn_u, r + 1)
                    tt(fcnat[:, r, :], fcnat[:, r, :], psum[:, 1 + r % 2, 0:D], ALU.add).then_inc(tn_nat, 1)

            def ffn0(n, c):
                k = instance(n)
                enter(eng, "dve", n)
                front(next_front(n))
                for m in range(8):
                    eng.wait_ge(f0_r, 8 * k + m + 1)
                    tt(hid0[:, m, :], hid0[:, m, :], hid0[:, m, :], ALU.mult).then_inc(f0_sq, 1)
                stack(stack_of(n))
                for i in range(TI):
                    eng.wait_ge(f0_y, 4 * k + i + 1)
                    add_x(c, i, psum[:, 4 + i % 2, 0:D]).then_inc(f0_x, 1)

            def ffn1(n, c):
                k = instance(n)
                enter(eng, "dve", n)
                front(next_front(n))
                gather_steps(gather.take(STEPS["ffn1"][0]))
                for i in range(TI):
                    eng.wait_ge(f1_sim, 4 * k + i + 1)
                    for p in range(2):
                        for h in range(PH):
                            own.mark(eng.max(topv[:, p, i * PH + h, :], psum[:, 2 * (i % 2) + p, h * NKEY:(h + 1) * NKEY]))
                    own.wait()
                    for p in range(2):
                        for h in range(PH):
                            ins = eng.max_index(topi[:, p, i * PH + h, :], topv[:, p, i * PH + h, :],
                                                psum[:, 2 * (i % 2) + p, h * NKEY:(h + 1) * NKEY])
                    ins.then_inc(f1_tk, 1)
                    eng.wait_ge(f1_sg, 4 * k + i + 1)
                    tt(hm1[:, i, :], sg1[:, i % 2, :], bank(5), ALU.mult).then_inc(f1_hm, 1)
                    if i % 2:
                        gather_steps(gather.take(STEPS["ffn1"][1 + i // 2]))
                eng.wait_ge(f1_tk, 4 * k + 4)
                own.mark(eng.tensor_copy(topf, topi))
                R = 16
                own.link(tt(sums, cast(topv[:, 0].unsqueeze(3), [P, R, 8, 8]), cast(topv[:, 1].unsqueeze(2), [P, R, 8, 8]), ALU.add))
                for r in range(R):
                    own.mark(eng.max(best[:, r, :], sums[:, r].rearrange("p i j -> p (i j)")))
                own.wait()
                ex = ex1.rearrange("p (r k) -> p r k", r=R)
                tt(ex, best, cast(best[:, :, 0:1], [P, R, 8]), ALU.subtract).then_inc(f1_sc, 1)
                for r in range(R):
                    own.mark(eng.max_index(pos[:, r * 8:r * 8 + 8], best[:, r, :], sums[:, r].rearrange("p i j -> p (i j)")))
                own.wait()
                stack(stack_of(n))
                gather_steps(gather.take(STEPS["ffn1"][3]))
                own.mark(ts(pside[0], pos, 3, None, ALU.logical_shift_right))
                own.link(ts(pside[1], pos, 7, None, ALU.bitwise_and))
                for z in range(2):
                    own.mark(eng.tensor_copy(psidef[z], pside[z]))
                own.wait()
                for z in range(2):
                    own.mark(tt(eq[z].rearrange("p r k j -> p (r k) j"), cast(psidef[z].unsqueeze(2), [P, P, 8]),
                                cast(iota8.unsqueeze(1), [P, P, 8]), ALU.is_equal))
                own.wait()
                for z in range(2):
                    own.mark(tt(eq[z], eq[z], cast(topf[:, z].unsqueeze(2), [P, R, 8, 8]), ALU.mult))
                own.wait()
                for z in range(2):
                    own.mark(eng.reduce_sum(pick[z], eq[z].rearrange("p r k j -> p (r k) j"), AX.X))
                own.wait()
                own.link(stt(rowf, pick[0], float(NKEY), pick[1], ALU.mult, ALU.add))
                gather_steps(gather.take(STEPS["ffn1"][4]))
                ts(rowid[c % 3][:, :], rowf, float(NEXP1 - 1), None, ALU.min).then_inc(f1_idx, 1)
                eng.wait_ge(f1_se, k + 1)
                own.link(eng.reduce_sum(esum, ex, AX.X))
                own.link(eng.reciprocal(erec, esum))
                tt(prob[c % 3][:, :].rearrange("p (r k) -> p r k", r=R), ex, cast(erec.unsqueeze(2), [P, R, 8]), ALU.mult).then_inc(f1_idx, 1)
                for i in range(TI):
                    eng.wait_ge(f1_y, 4 * k + i + 1)
                    own.mark(add_x(c, i, psum[:, i, 0:D]))
                own.wait()
                gather.named += TI * NG
                gather_steps(gather.take(STEPS["ffn1"][5]))

            def ffn2(n, c):
                k = instance(n)
                enter(eng, "dve", n)
                gather_steps(gather.take(STEPS["ffn2"][0]))
                eng.wait_ge(f2_sc, k + 1)
                best_two(sc2, tv2, ti2, tf2)
                own.link(tt(s2[0], tv2[:, :, 0], tv2[:, :, 1], ALU.add))
                own.link(ts(s2[1], s2[0], 1e-20, None, ALU.add))
                own.link(eng.reciprocal(s2[2], s2[1]))
                own.link(ts(s2[3], s2[2], 2.5, None, ALU.mult))
                spread(comb2, tv2, tf2, s2[3])
                for m in range(M2):
                    eng.wait_ge(f2_sg, M2 * k + m + 1)
                    tt(hm2[:, m, :], sg2[:, m % 2, :], bank(2 * (m % 2) + 1), ALU.mult).then_inc(f2_hm, 1)
                    gather_steps(gather.take(STEPS["ffn2"][1][m]))
                front(next_front(n))
                gather_steps(gather.take(STEPS["ffn2"][3]))
                stack(stack_of(n))
                for y in range(TI * 9):
                    i, e, K = y // 9, y % 9, TI * 9 * k + y
                    eng.wait_ge(f2_y, K + 1)
                    if e:
                        eng.wait_ge(f2_x, K)
                    src = psum[:, y % 5, 0:D]
                    ins = add_x(c, i, src) if e == 8 else stt(
                        x_sb[:, c * TI + i, :], src, comb2[0][:, i, e:e + 1], x_sb[:, c * TI + i, :], ALU.mult, ALU.add)
                    ins.then_inc(f2_x, 1)
                    if e == 8:
                        gather_steps(gather.take(STEPS["ffn2"][2]))

            def best_two(src, tv, ti, tf):
                for i in range(TI):
                    own.mark(eng.max(tv[:, i, :], src[:, i * 8:(i + 1) * 8]))
                own.wait()
                for i in range(TI):
                    own.mark(eng.max_index(ti[:, i, :], tv[:, i, :], src[:, i * 8:(i + 1) * 8]))
                own.wait()
                own.link(eng.tensor_copy(tf, ti))

            def spread(comb, tv, tf, scale):
                shape = [P, TI, 8]
                for r in range(2):
                    own.mark(tt(comb[r], cast(tf[:, :, r:r + 1], shape), cast(iota8.unsqueeze(1), shape), ALU.is_equal))
                own.wait()
                for r in range(2):
                    own.mark(tt(comb[r], comb[r], cast(tv[:, :, r:r + 1], shape), ALU.mult))
                own.wait()
                own.link(tt(comb[2], comb[0], comb[1], ALU.add))
                own.link(tt(comb[0], comb[2], cast(scale.unsqueeze(2), shape), ALU.mult))

            def ffn3(n, c):
                k = instance(n)
                enter(eng, "dve", n)
                front(next_front(n))
                eng.wait_ge(f3_lg, k + 1)
                lg = psum[:, 5, 0:TI * E3].rearrange("p (i e) -> p i e", i=TI)
                shape = [P, TI, E3]
                ex = ex3.rearrange("p (i e) -> p i e", i=TI)
                own.link(eng.reduce_max(mx3, lg, AX.X))
                tt(ex, lg, cast(mx3.unsqueeze(2), shape), ALU.subtract).then_inc(f3_ls, 1)
                eng.wait_ge(f3_ex, k + 1)
                own.link(eng.reduce_sum(s3[0], ex, AX.X))
                own.link(eng.reciprocal(s3[1], s3[0]))
                own.link(tt(pr3.rearrange("p (i e) -> p i e", i=TI), ex, cast(s3[1].unsqueeze(2), shape), ALU.mult))
                best_two(pr3, tv3, ti3, tf3)
                own.link(tt(s3[2], tv3[:, :, 0], tv3[:, :, 1], ALU.add))
                own.link(eng.reciprocal(s3[3], s3[2]))
                spread(comb3, tv3, tf3, s3[3])
                eng.sem_inc(f3_gt, 1)
                for y in range(TI * 4):
                    i, K = y // 4, TI * 4 * k + y
                    if y == 4 * TI - 4:
                        eng.wait_ge(f3_b, k + 1)
                        eng.wait_ge(f3_x, K)
                        for t in range(TI):
                            own.mark(add_x(c, t, psum[:, 4 + t // 2, (t % 2) * D:(t % 2 + 1) * D]))
                        own.wait()
                    eng.wait_ge(f3_y, K + 1)
                    if y % 4:
                        eng.wait_ge(f3_x, K)
                    for r in range(2):
                        e = 2 * (y % 4) + r
                        ins = stt(x_sb[:, c * TI + i, :], psum[:, y % 4, r * D:(r + 1) * D], comb3[0][:, i, e:e + 1],
                                  x_sb[:, c * TI + i, :], ALU.mult, ALU.add)
                        if r == 0:
                            own.link(ins)
                    ins.then_inc(f3_x, 1)

            def kv3(n):
                enter(eng, "dve", n)
                for g in range(2):
                    for b in range(B):
                        own.mark(eng.memset(k3t[:, g, b * SP_ + S:(b + 1) * SP_], 0.0))
                own.wait()
                eng.wait_ge(k3_kt, 4)
                shape = [P, U, 8, 16]
                mask = cast(mask8.unsqueeze(1).unsqueeze(3), shape)
                for b in range(B):
                    for g in range(2):
                        src = k3t[:, g, b * SP_:(b + 1) * SP_].rearrange("p (u s) -> p u s", u=U)
                        tt(kst(b, g).rearrange("p u (h s) -> p u h s", h=8), cast(src.unsqueeze(2), shape), mask, ALU.mult)

            def top(b):
                r = slice(0, H)
                eng.wait_ge(co_m, b + 1)
                if b:
                    eng.wait_ge(tp_wr, 32 * b)
                own.link(eng.tensor_copy(cor[r, :], psum[r, 6:8, :].rearrange("p a n -> p (a n)")))
                own.link(eng.max(topm[r, :], cor[r, :]))
                own.mark(eng.max_index(topj[r, :], topm[r, :], cor[r, :]))
                tt(topw[r, :], topm[r, :], cast(topm[r, 0:1], [H, 8]), ALU.subtract).then_inc(tp_n, 1)
                own.wait()
                own.link(eng.tensor_copy(topjf[r, :], topj[r, :]))
                own.link(ts(topjf[r, :], topjf[r, :], -1.0, float(T), ALU.mult, ALU.add))
                own.link(ts(topm[r, :], topjf[r, :], float(T), float(T), ALU.is_ge, ALU.mult))
                own.link(tt(topjf[r, :], topjf[r, :], topm[r, :], ALU.subtract))
                eng.wait_ge(tp_e, b + 1)
                own.link(eng.reduce_sum(rsum3[r, 0:1], topw[r, 0:TOPC], AX.X))
                own.link(eng.reciprocal(rsum3[r, 1:2], rsum3[r, 0:1]))
                own.link(ts(topw[r, :], topw[r, :], rsum3[r, 1:2], None, ALU.mult))
                for k in range(TOPC):
                    out = rollw if k == 0 else rollt[k % 2]
                    own.link(ts(out[r, :], iota[r, :], topjf[r, k:k + 1], topw[r, k:k + 1], ALU.is_equal, ALU.mult))
                    if k:
                        own.link(tt(rollw[r, :], rollw[r, :], out[r, :], ALU.add))
                eng.sem_inc(tp_r, 1)

            def out3(n, b):
                enter(eng, "dve", n)
                front(next_front(n))
                if b < B - 1:
                    top(b + 1)
                eng.wait_ge(o3_bo, b + 1)
                for i in range(8):
                    eng.wait_ge(o3_y, 8 * b + i + 1)
                    add_x(2 * b, i, psum[:, 4 + i % 2, 0:D]).then_inc(o3_x, 1)

            def q3(n):
                enter(eng, "dve", n)
                front(next_front(n))

            def corr(n, b):
                enter(eng, "dve", n)
                if b:
                    top(b - 1)
                else:
                    shape = [P, U, 8, 16]
                    mask = cast(mask8.unsqueeze(1).unsqueeze(3), shape)
                    eng.wait_ge(k3_rd, 16 * 32)
                    for b in range(B):
                        for g in range(2):
                            tt(vst(b, g).rearrange("p u (h d) -> p u h d", h=8), cast(v3s[:, 2 * b + g].unsqueeze(2), shape), mask, ALU.mult)

            for n, (kind, layer, c) in enumerate(phases):
                {"kv": lambda: kv(n, layer), "attn": lambda: attn(n, layer, c), "tern": lambda: tern(n),
                 "ffn0": lambda: ffn0(n, c), "ffn1": lambda: ffn1(n, c), "ffn2": lambda: ffn2(n, c), "ffn3": lambda: ffn3(n, c),
                 "kv3": lambda: kv3(n), "q3": lambda: q3(n), "corr": lambda: corr(n, layer), "out3": lambda: out3(n, layer)}[kind]()
                leave(eng, "dve")
                gather_steps(gather.take(after_phase(kind, layer)))

        @block.gpsimd
        def _(eng):
            own = Own(eng, own_pool)
            for b in range(B):
                own.mark(eng.memset(vmain(b).rearrange("p (h n) -> p h n", h=H)[:, :, DH:32], 1.0))
                own.mark(eng.memset(vrest(b), 0.0))
            own.wait()
            for b in range(B):
                for j in range(4):
                    ins = eng.memset(vrest(b)[32 * j:32 * j + SR, :, j * 32 + DH:j * 32 + 32], 1.0)
            ins.then_inc(kv_z, 1)

            def add_bias(kind, layer, signal):
                for n, (kind_, layer_, c) in enumerate(phases):
                    if kind_ == kind and layer_ in layer:
                        enter(eng, "pool", n)
                        tiles = range(c * TI, (c + 1) * TI) if kind == "attn" else range(8 * layer_, 8 * layer_ + 8)
                        for t in tiles:
                            ins = eng.tensor_tensor(x_sb[:, t, :], x_sb[:, t, :], wattn[:, AC["bo"]], ALU.add)
                        ins.then_inc(signal, 1)

            add_bias("attn", (0,), at_bo)

            def fetch(g):
                c, s, at = g // (TI * NG), g % (RING // GRP), g % (TI * NG) * GRP
                if at == 0:
                    eng.wait_ge(f1_idx, 2 * (c + 1))
                if g >= RING // GRP:
                    eng.wait_ge(f1_acc, g - RING // GRP + 1)
                for j in range(GRP):
                    eng.indirect_dma_start(ring[:, s * GRP + j, :], None, io["table"],
                                           bass.IndirectOffsetOnAxis(ap=rowid[c % 3][:, at + j:at + j + 1], axis=0))\
                        .then_inc(gathered[s], 16)

            for g in range(sum(p[0] == "ffn1" for p in phases) * TI * NG):
                fetch(g)
            add_bias("out3", (0, 1), o3_bo)
            eng.drain().then_inc(end_pool, 1)

        @block.sync
        def _(eng):
            loads = {}

            def load(dst, src, s):
                loads[s.name] = (s, loads.get(s.name, (s, 0))[1] + 16)
                eng.dma_start(dst, src).then_inc(s, 16)

            def last(kind, layer):
                ns = [n for n, p in enumerate(phases) if p[0] == kind and p[1] == layer]
                return max(ns) if ns else None

            def after(n):
                for s in ends.values():
                    eng.wait_ge(s, n + 1)

            def stack(n):
                if n is None:
                    return
                k = instance(n)
                eng.wait_ge(sk_p, k + 1)
                eng.dma_start(scrq.rearrange("z (g p) n -> p (z g) n", p=P),
                              qparts.rearrange("p z g n -> p (z g) n")).then_inc(sk_wr, 16)
                eng.wait_ge(sk_wr, 16 * (k + 1))
                if k:
                    eng.wait_ge(at_s2, 12 * k)
                for z in range(NB):
                    eng.dma_start(queries[z * DH:(z + 1) * DH], scrq[Q_PARTS[z]].rearrange("(h d) n -> d h n", d=DH))\
                        .then_inc(sk_rd, 16)

            def top(b):
                eng.wait_ge(tp_r, b + 1)
                for z in range(2):
                    eng.dma_start(scr2[b, :, z * T:(z + 1) * T], rollw[0:H, :]).then_inc(tp_wr, 16)
                eng.wait_ge(tp_wr, 32 * (b + 1))
                for g in range(2):
                    src = bass.AP(scr2.tensor, (H * b + 8 * g) * 2 * T + T - SP_ - 15, [[2 * T, 8], [1, 16], [1, T + SP_]])
                    eng.dma_start(roll(2 * b + g), src).then_inc(tp_rd, 16)

            x_in = io["x"].rearrange("(i p) d -> p i d", p=P)
            load(x_sb[:, 0:TI, :], x_in[:, 0:TI, :], ld_x0)
            load(const[:, :], io["const"], ld_const)
            load(ctxt[:, :, :].rearrange("p k n -> p (k n)"), io["ctxt"], ld_ctx)
            load(wattn[:, 0:AN], io["attn0"], ld_attn)
            load(x_sb[:, TI:, :], x_in[:, TI:, :], ld_x)
            for n, (kind, layer, c) in enumerate(phases):
                if kind == "kv":
                    enter(eng, "sp", n)
                    eng.wait_ge(kv_p, layer + 1)
                    eng.dma_start(scrk.rearrange("z (g p) n -> p (z g) n", p=P),
                                  kparts.rearrange("p z g b s -> p (z g) (b s)")).then_inc(kv_wr, 16)
                    eng.wait_ge(kv_wr, 16 * (layer + 1))
                    eng.wait_ge(kv_m, layer + 1)
                    for z in range(NB):
                        for b in range(B):
                            src = scrk[K_PARTS[z]].rearrange("(h d) (b s) -> b d h s", d=DH, b=B)[b]
                            eng.dma_start(keys(b)[z * DH:(z + 1) * DH], src).then_inc(kv_rd, 16)
                if kind == "attn":
                    k = instance(n)
                    eng.wait_ge(at_mts, k + 1)
                    eng.dma_start(queries[MROW:MROW + 1], mt[:, :]).then_inc(at_mr, 16)
                stack(stack_of(n))
                if kind == "kv3":
                    enter(eng, "sp", n)
                    eng.wait_ge(k3_vs, 4)
                    for b in range(B):
                        eng.dma_start(scrv[b, 0:P, :], v3m[:, b, :]).then_inc(k3_wr, 16)
                        eng.dma_start(scrv[b, P:SP_, :], v3r[0:32, b, :]).then_inc(k3_wr, 16)
                    eng.wait_ge(k3_wr, 16 * 4)
                    for b in range(B):
                        for g in range(2):
                            src = scrv[b].rearrange("(u s) (a h d) -> a h s u d", s=16, a=2, d=DH)[g]
                            for h in range(8):
                                eng.dma_start(v3s[h * 16:(h + 1) * 16, 2 * b + g], src[h]).then_inc(k3_rd, 16)
                if kind == "corr":
                    if layer:
                        top(layer - 1)
                    for g in range(2):
                        a = 2 * layer + g
                        eng.wait_ge(co_s, 4 * layer + 2 * g + 2)
                        eng.dma_start(scr1[a], c1[g]).then_inc(co_wr, 16)
                    for g in range(2):
                        a = 2 * layer + g
                        eng.wait_ge(co_wr, 16 * 2 * (layer + 1))
                        src = bass.AP(scr1.tensor, a * P * (T + 16), [[16 * (T + 16), 8], [T + 17, 16], [1, T]])
                        eng.dma_start(c2[a], src).then_inc(co_rd, 16)
                if kind == "out3" and layer < B - 1:
                    top(layer + 1)
                if kind == "ffn3" or (stop is not None and n == len(phases) - 1):
                    eng.wait_ge(ends["dve"], n + 1)
                    for q in ([c] if kind == "ffn3" else range(NCH)):
                        eng.dma_start(io["out"].rearrange("(i p) d -> p i d", p=P)[:, q * TI:(q + 1) * TI, :],
                                      x_sb[:, q * TI:(q + 1) * TI, :]).then_inc(stored, 16)
                if n == 0:
                    load(raw0, io["ffn0"], ld_f0)
                    load(rope[:, 0:RN], io["rope"], ld_rope)
                if kind == "attn" and n == last("attn", layer):
                    after(n)
                    if layer < 2:
                        load(wattn[:, 0:AN], io[f"attn{layer + 1}"], ld_attn)
                    else:
                        load(wattn[:, 0:CN], io["corr"], ld_attn)
                if n == last("attn", 2):
                    load(late[:, 0:LN], io["late"], ld_late)
                if n == last("ffn0", 0):
                    after(n)
                    load(wf[:, 0:F1N], io["ffn1"], ld_f1)
                if n == last("ffn1", 1):
                    after(n)
                    load(wf[:, 0:F2N], io["ffn2"], ld_f2)
                if n == last("ffn2", 2):
                    after(n)
                    load(wf[:, 0:F3N], io["ffn3"], ld_f3)
            eng.wait_ge(end_pool, 1)
            eng.wait_ge(stored, 16 * NCH)
            for s, count in loads.values():
                eng.wait_ge(s, count)


def packed(widths, **arrays):
    cols, n = columns(widths)
    out = np.zeros((P, n), np.float32)
    for name, a in arrays.items():
        a = np.asarray(a, np.float32).reshape(a.shape[0], -1)
        out[:a.shape[0], cols[name]] = a
    return out


def by_rows(w):
    w = np.asarray(w)
    return w.reshape(-1, P, w.shape[1]).transpose(1, 0, 2)


def per_feature(b):
    return np.asarray(b).reshape(2, P).T


def on_all(row):
    return np.broadcast_to(np.asarray(row).reshape(1, -1), (P, np.size(row)))


def constants():
    p = np.arange(P)
    selh = np.zeros((P, 2, 32), np.float32)
    for a in range(2):
        selh[p, a, 8 * a + p // 16] = 1.0 / DH
    mask8 = (p[:, None] // 16 == np.arange(8)[None]).astype(np.float32)
    padrow = np.where(p % 32 < SR, 0.0, -3e38).astype(np.float32)[:, None]
    token = np.arange(SP_) // 16 * 16 + 15 - np.arange(SP_) % 16
    valid = on_all((token < S).astype(np.float32))
    const = packed(CONST_PACK, ident=np.eye(P, dtype=np.float32), mask8=mask8, padrow=padrow,
                   iota8=on_all(np.arange(8, dtype=np.float32)), selh=selh,
                   valid=valid)
    inv = (np.float32(10000.0) ** (-np.arange(0, DH, 2, dtype=np.float32) / np.float32(DH))).astype(np.float32)
    ang = (np.arange(T, dtype=np.float32)[None, :] * inv[:, None]).astype(np.float32)
    d = p % DH
    sign = np.where(d % 2 == 0, -1.0, 1.0).astype(np.float32)
    rope = packed(ROPE_PACK, cos=np.cos(ang)[d // 2], sin=np.sin(ang)[d // 2] * sign[:, None])
    return const, rope


def kernel(**inputs):
    import concourse.bacc as _bacc
    from concourse.bass_utils import run_bass_kernel_spmd as _run

    a = {k: np.asarray(v) for k, v in inputs.items()}
    zero = np.zeros(D, np.float32)

    def attention(wq, wk, wv, wo, bq, bk, bv, bo):
        return packed(ATTN_PACK, wq=by_rows(wq), wk=by_rows(wk), wv=by_rows(wv), wo=by_rows(wo), bq=per_feature(bq),
                      bk=per_feature(bk), bv=on_all(bv), bo=on_all(bo))

    l0, l1, l2, l3 = ({k[9:]: v for k, v in a.items() if k.startswith(f"L{i}_xattn")} for i in range(4))
    f0, f1, f2, f3 = ({k[7:]: v for k, v in a.items() if k.startswith(f"L{i}_ffn")} for i in range(4))
    arrays = {"x": a["x"].reshape(B * T, D)}
    ctx = a["ctx_1024"]
    arrays["ctxt"] = by_rows(ctx.reshape(B * S, D).T).reshape(P, -1)
    rev = np.zeros((B, SP_, D), np.float32)
    rev[:, :S] = ctx
    rev = rev.reshape(B, U, 16, D)[:, :, ::-1].reshape(B * SP_, D)
    arrays["late"] = packed(LATE_PACK, iota=on_all(np.arange(T, dtype=np.float32)), ctxr=by_rows(rev.T))
    arrays["attn0"] = attention(l0["Wq"], l0["Wk"], l0["Wv"], l0["Wo"], l0["b_q"], l0["b_k"], l0["b_v"], l0["b_o"])
    arrays["attn1"] = attention(l1["wq_w"].T, l1["wk_w"].T, l1["wv_w"].T, l1["dense_w"].T,
                                l1["wq_b"], l1["wk_b"], l1["wv_b"], l1["dense_b"])
    arrays["attn2"] = attention(l2["Wq"], l2["Wk"], l2["Wv"], l2["Wo"], zero, zero, zero, zero)
    arrays["corr"] = packed(CORR_PACK, wq=by_rows(l3["Wq"]), wk=by_rows(l3["Wk"]), wv=by_rows(l3["Wv"]), wo=by_rows(l3["Wo"]),
                            bq=per_feature(l3["bq"]), bk=per_feature(l3["bk"]), bv=on_all(l3["bv"]), bo=on_all(l3["bo"]))
    arrays["ffn0"] = packed(FFN0_PACK, fc=by_rows(f0["w_fc"]), proj=by_rows(f0["w_proj"]), ut=f0["u"].T, v=f0["v"],
                            fbt=f0["fast_b"].T, gate=on_all(f0["gate"]))
    keys = np.zeros((2, PH, 32, PH, NKEY), np.float32)
    for h in range(PH):
        keys[:, h, :, h, :] = f1["keys"][h].transpose(1, 2, 0)
    arrays["ffn1"] = packed(FFN1_PACK, wq=by_rows(f1["w_queries"].T), keys=keys.reshape(2, P, 512).transpose(1, 0, 2),
                            wg=by_rows(f1["w_gate"].T), wu=by_rows(f1["w_up"].T), wd=by_rows(f1["w_down"].T))
    arrays["table"] = np.concatenate([f1["down_embed"], f1["up_embed"]], axis=1)
    gu = np.stack([np.concatenate([f2["w_gate"], f2["ws_gate"].reshape(2, P, D)]),
                   np.concatenate([f2["w_up"], f2["ws_up"].reshape(2, P, D)])], axis=1)
    down = np.concatenate([f2["w_down"].transpose(2, 0, 1), f2["ws_down"].T.reshape(2, P, D).transpose(1, 0, 2)], axis=1)
    arrays["ffn2"] = packed(FFN2_PACK, gate=by_rows(f2["gate_weight"].T), gu=by_rows(gu.reshape(-1, D).T), down=down)
    arrays["ffn3"] = packed(FFN3_PACK, gate=by_rows(f3["Wg"]), we=by_rows(f3["We"].transpose(1, 0, 2).reshape(D, -1)), be=f3["be"])
    arrays["const"], arrays["rope"] = constants()

    nc = _bacc.Bacc("TRN2", target_bir_lowering=False, num_devices=1)
    ins, io = {}, {}
    for name, v in arrays.items():
        ins[f"in_{name}"] = np.ascontiguousarray(v)
        io[name] = nc.dram_tensor(f"in_{name}", v.shape, FP, kind="ExternalInput").ap()
    io["out"] = nc.dram_tensor("out", (B * T, D), FP, kind="ExternalOutput").ap()
    build(nc, io, STOP)
    r = _run(nc, [ins], core_ids=[0])
    return r.results[0]["out"].reshape(B, T, D)
```
